# Optimizing a Trainium2 kernel written in Bass

```python
import numpy as np
import jax
import jax.numpy as jnp

def _softmax(x, axis=-1):
    return jax.nn.softmax(x, axis=axis)

def _gelu(x):
    return jax.nn.gelu(x, approximate=True)

def _silu(x):
    return jax.nn.silu(x)

def _sigmoid(x):
    return jax.nn.sigmoid(x)

def _layernorm(x, axis=-1, eps=1e-05):
    m = jnp.mean(x, axis=axis, keepdims=True)
    v = jnp.var(x, axis=axis, keepdims=True)
    return (x - m) / jnp.sqrt(v + eps)

def _scatter_add(tgt, idx, src, axis=0):
    return tgt.at[idx].add(src)

def _segment_sum(src, seg, n):
    return jax.ops.segment_sum(src, seg, n)
kernel_name = 'mk_xattn_seq_d2_seqx_r4_47969e'

def setup_inputs(seed: int=0):
    np.random.seed(seed)
    _w = jnp.asarray

    def _rec_inputs():
        import jax
        import jax.numpy as jnp
        _rk = jax.random.key(seed)
        x = -0.0001548 + 1 * jax.random.normal(jax.random.fold_in(_rk, 1), (8, 256, 320), jnp.float32)
        _lenS = 256 - jax.random.randint(jax.random.fold_in(_rk, 7), (8,), 0, max(1, 256 // 4) + 1, jnp.int32)
        _lenS2 = 77 - jax.random.randint(jax.random.fold_in(_rk, 8), (8,), 0, max(1, 77 // 4) + 1, jnp.int32)
        _ctx_768P = jax.random.normal(jax.random.fold_in(_rk, 11), (8, 16, 192), jnp.float32)
        _ctx_768c = jax.random.dirichlet(jax.random.fold_in(_rk, 511), 0.3 * jnp.ones((16,), jnp.float32), (8, 77))
        _ctx_768t = jnp.einsum('bsk,bkd->bsd', _ctx_768c, _ctx_768P)
        _ctx_768t = _ctx_768t * jax.lax.rsqrt(jnp.mean(jnp.square(_ctx_768t)) + 1e-12) * 0.953939
        ctx_768 = 0.00141353 + 0.998943 * (_ctx_768t + 0.3 * jax.random.normal(jax.random.fold_in(_rk, 611), (8, 77, 192), jnp.float32))
        return (x, ctx_768)
    x, ctx_768 = _rec_inputs()

    def _L0_xattn_setup():
        import jax, jax.numpy as jnp
        import numpy as np
        HEADS = 8
        NUM_TOKENS = 4
        CROSS_ATTENTION_DIM = 192

        def _mha(q, k, v, heads=HEADS):
            B, Sq, H = q.shape
            Sk = k.shape[1]
            d = H // heads
            qh = q.reshape(B, Sq, heads, d).transpose(0, 2, 1, 3)
            kh = k.reshape(B, Sk, heads, d).transpose(0, 2, 1, 3)
            vh = v.reshape(B, Sk, heads, d).transpose(0, 2, 1, 3)
            scores = jnp.einsum('bhqd,bhkd->bhqk', qh, kh) * jnp.asarray(d, q.dtype) ** (-0.5)
            probs = jax.nn.softmax(scores, axis=-1)
            out = jnp.einsum('bhqk,bhkd->bhqd', probs, vh)
            return out.transpose(0, 2, 1, 3).reshape(B, Sq, H)
        key = jax.random.key(seed)
        ks = jax.random.split(key, 10)
        B, S, H, CAD, T = (4, 256, 320, CROSS_ATTENTION_DIM, NUM_TOKENS)
        sc = 0.02
        return {'hidden_states': jax.random.normal(ks[0], (B, S, H), jnp.float32), 'encoder_hidden_states': jax.random.normal(ks[1], (B, 77 + T, CAD), jnp.float32), 'Wq': jax.random.normal(ks[2], (H, H), jnp.float32) * sc, 'Wk': jax.random.normal(ks[3], (CAD, H), jnp.float32) * sc, 'Wv': jax.random.normal(ks[4], (CAD, H), jnp.float32) * sc, 'Wq_ca': jax.random.normal(ks[5], (T, H), jnp.float32) * sc, 'Wk_ca': jax.random.normal(ks[6], (CAD, H), jnp.float32) * sc, 'Wv_ca': jax.random.normal(ks[7], (CAD, H), jnp.float32) * sc, 'Wout': jax.random.normal(ks[8], (H, H), jnp.float32) * sc, 'b_out': jnp.zeros((H,), jnp.float32)}
    _L0_xattn_all = _L0_xattn_setup()
    _L0_xattn_in = {k: v for k, v in _L0_xattn_all.items() if k in ('Wq', 'Wk', 'Wv', 'Wq_ca', 'Wk_ca', 'Wv_ca', 'Wout', 'b_out')}
    del _L0_xattn_all

    def _L1_xattn_setup():
        import jax, jax.numpy as jnp
        import numpy as np
        HEADS = 20
        NUM_AOE = 16
        NUM_IP = 16
        key = jax.random.key(seed)
        ks = jax.random.split(key, 7)
        B, Sq, H = (8, 1024, 320)
        Skv, C = (109, 192)
        scale = 0.02
        return {'hidden_states': jax.random.normal(ks[0], (B, Sq, H), jnp.float32), 'encoder_hidden_states': jax.random.normal(ks[1], (B, Skv, C), jnp.float32), 'Wq': jax.random.normal(ks[2], (H, H), jnp.float32) * scale, 'Wk': jax.random.normal(ks[3], (C, H), jnp.float32) * scale, 'Wv': jax.random.normal(ks[4], (C, H), jnp.float32) * scale, 'Wo': jax.random.normal(ks[5], (H, H), jnp.float32) * scale, 'bo': jnp.zeros((H,), jnp.float32)}
    _L1_xattn_all = _L1_xattn_setup()
    _L1_xattn_in = {k: v for k, v in _L1_xattn_all.items() if k in ('Wq', 'Wk', 'Wv', 'Wo', 'bo')}
    del _L1_xattn_all
    return {'x': x, 'ctx_768': ctx_768, 'L0_xattn_Wq': _L0_xattn_in['Wq'], 'L0_xattn_Wk': _L0_xattn_in['Wk'], 'L0_xattn_Wv': _L0_xattn_in['Wv'], 'L0_xattn_Wq_ca': _L0_xattn_in['Wq_ca'], 'L0_xattn_Wk_ca': _L0_xattn_in['Wk_ca'], 'L0_xattn_Wv_ca': _L0_xattn_in['Wv_ca'], 'L0_xattn_Wout': _L0_xattn_in['Wout'], 'L0_xattn_b_out': _L0_xattn_in['b_out'], 'L1_xattn_Wq': _L1_xattn_in['Wq'], 'L1_xattn_Wk': _L1_xattn_in['Wk'], 'L1_xattn_Wv': _L1_xattn_in['Wv'], 'L1_xattn_Wo': _L1_xattn_in['Wo'], 'L1_xattn_bo': _L1_xattn_in['bo']}

def reference(x, ctx_768, L0_xattn_Wq, L0_xattn_Wk, L0_xattn_Wv, L0_xattn_Wq_ca, L0_xattn_Wk_ca, L0_xattn_Wv_ca, L0_xattn_Wout, L0_xattn_b_out, L1_xattn_Wq, L1_xattn_Wk, L1_xattn_Wv, L1_xattn_Wo, L1_xattn_bo):
    import jax
    import jax.numpy as jnp

    def _L0_xattn_ref(hidden_states, encoder_hidden_states, Wq, Wk, Wv, Wq_ca, Wk_ca, Wv_ca, Wout, b_out):
        import jax, jax.numpy as jnp
        import numpy as np
        HEADS = 8
        NUM_TOKENS = 4
        CROSS_ATTENTION_DIM = 192

        def _mha(q, k, v, heads=HEADS):
            B, Sq, H = q.shape
            Sk = k.shape[1]
            d = H // heads
            qh = q.reshape(B, Sq, heads, d).transpose(0, 2, 1, 3)
            kh = k.reshape(B, Sk, heads, d).transpose(0, 2, 1, 3)
            vh = v.reshape(B, Sk, heads, d).transpose(0, 2, 1, 3)
            scores = jnp.einsum('bhqd,bhkd->bhqk', qh, kh) * jnp.asarray(d, q.dtype) ** (-0.5)
            probs = jax.nn.softmax(scores, axis=-1)
            out = jnp.einsum('bhqk,bhkd->bhqd', probs, vh)
            return out.transpose(0, 2, 1, 3).reshape(B, Sq, H)
        residual = hidden_states
        unet_size = residual.shape[1]
        end_pos = encoder_hidden_states.shape[1] - NUM_TOKENS
        enc = encoder_hidden_states[:, :end_pos, :]
        ca = encoder_hidden_states[:, end_pos:, :]
        query = hidden_states @ Wq
        keyt = enc @ Wk
        valt = enc @ Wv
        hs = _mha(query, keyt, valt)
        ca_q1 = jnp.einsum('btc,th->bch', ca, Wq_ca)
        indices = np.linspace(0, CROSS_ATTENTION_DIM - 1, unet_size).astype(np.int64)
        ca_q1 = ca_q1[:, indices, :]
        ca_hs1 = _mha(ca_q1, residual, residual)
        ca_q2 = ca_hs1 @ Wq
        ca_k2 = ca @ Wk_ca
        ca_v2 = ca @ Wv_ca
        ca_hs2 = _mha(ca_q2, ca_k2, ca_v2)
        out = hs + ca_hs2
        out = out @ Wout + b_out
        out = out + residual
        return out

    def _L1_xattn_ref(hidden_states, encoder_hidden_states, Wq, Wk, Wv, Wo, bo):
        import jax, jax.numpy as jnp
        import numpy as np
        HEADS = 20
        NUM_AOE = 16
        NUM_IP = 16
        B, Sq, H = hidden_states.shape
        Skv = encoder_hidden_states.shape[1]
        head_dim = H // HEADS
        residual = hidden_states
        q = (hidden_states @ Wq).reshape(B, Sq, HEADS, head_dim).transpose(0, 2, 1, 3)
        k = (encoder_hidden_states @ Wk).reshape(B, Skv, HEADS, head_dim).transpose(0, 2, 1, 3)
        v = (encoder_hidden_states @ Wv).reshape(B, Skv, HEADS, head_dim).transpose(0, 2, 1, 3)
        scores = jnp.einsum('bhqd,bhkd->bhqk', q, k) / jnp.sqrt(jnp.asarray(head_dim, q.dtype))
        probs = jax.nn.softmax(scores, axis=-1)
        scale_aoe = jnp.asarray(1.0, probs.dtype)
        scale_ip = jnp.asarray(1.0, probs.dtype)
        idx = jnp.arange(Skv)
        scale_vector = jnp.where(idx < NUM_AOE, scale_aoe, 1.0)
        scale_vector = jnp.where(idx >= Skv - NUM_IP, scale_vector * scale_ip, scale_vector)
        probs = probs * scale_vector
        probs = probs / probs.sum(axis=-1, keepdims=True)
        out = jnp.einsum('bhqk,bhkd->bhqd', probs, v)
        out = out.transpose(0, 2, 1, 3).reshape(B, Sq, H)
        out = out @ Wo + bo
        return out + residual
    x = _L0_xattn_ref(x, ctx_768, L0_xattn_Wq, L0_xattn_Wk, L0_xattn_Wv, L0_xattn_Wq_ca, L0_xattn_Wk_ca, L0_xattn_Wv_ca, L0_xattn_Wout, L0_xattn_b_out)
    x = _L1_xattn_ref(x, ctx_768, L1_xattn_Wq, L1_xattn_Wk, L1_xattn_Wv, L1_xattn_Wo, L1_xattn_bo)
    return x

_drawn_inputs = setup_inputs


def setup_inputs(seed=0):
    import zlib

    import numpy as np

    out = dict(_drawn_inputs(seed))
    spreads = {'L0_xattn_b_out': (0.0, 0.1), 'L1_xattn_bo': (0.0, 0.1)}
    factors = {'L0_xattn_Wq': 8.0,
     'L0_xattn_Wk': 8.0,
     'L0_xattn_Wq_ca': 41.462,
     'L0_xattn_Wk_ca': 25.905,
     'L1_xattn_Wq': 8.0,
     'L1_xattn_Wk': 8.0}
    for name, (base, spread) in spreads.items():
        noise = np.random.default_rng([zlib.crc32(name.encode()), seed]).standard_normal(out[name].shape)
        drawn = base * np.exp(spread * noise) if base else spread * noise
        out[name] = jnp.asarray(drawn.astype(out[name].dtype))
    for name, factor in factors.items():
        out[name] = (out[name] * factor).astype(out[name].dtype)
    return out
```

```python
import concourse.bass as bass
from concourse import mybir
from contextlib import ExitStack
import numpy as np

B, SQ, H = 8, 256, 320
CTX, CAD, T = 77, 192, 4
QT = SQ // 128
CK = CAD // 2
XG = [112, 112, 96]
HEADS0, D0, KEYS0 = 8, 40, CTX - T
HG0 = [3, 3, 2]
G0 = [h * D0 for h in HG0]
HEADS1, D1, KEYS1 = 20, 16, CTX
HG1 = [7, 7, 6]
TILES0 = [2, 2, 2]
TILES1 = [5, 5, 4]
T0, T1 = sum(TILES0), sum(TILES1)
V0C, V1C = 3 * D0 + 3, 7 * D1 + 7
CCOL = HEADS0 * CAD
NC = CCOL // 128
PAIRS = HEADS0 // 2
HT = HEADS0 * T
SCALE0, SCALE1 = float(D0) ** -0.5, float(D1) ** -0.5
JOBS_A, JOBS_B = 32, 24
USES_A, USES_B = JOBS_A // 4, JOBS_B // 4
A_Q01, A_Q2G, A_V0, A_V1, A_CS, A_SM, A_M, A_CT, A_CU, A_ST, A_U, A_S2, A_TR, A_EX, A_O = (
    0, 1, 2, 3, 4, 10, 13, 14, 20, 22, 25, 27, 28, 29, 30)
B_Q, B_SM, B_M, B_ST, B_U, B_O = 0, 2, 10, 12, 19, 22


def pieces(heads, keys):
    out = []
    for h in range(heads):
        k = 0
        while k < keys:
            tile, row = divmod(h * keys + k, 128)
            n = min(keys - k, 128 - row)
            out.append((h, k, n, tile, row))
            k += n
    return out


def offsets(sizes):
    return [sum(sizes[:i]) for i in range(len(sizes))]


TO0, TO1, HO0, HO1, GO0, XO = (offsets(s) for s in (TILES0, TILES1, HG0, HG1, G0, XG))
N_V0 = sum(len(pieces(n, KEYS0)) for n in HG0)
N_V1 = sum(len(pieces(n, KEYS1)) for n in HG1)


def constants():
    c = {}
    c["ident"] = np.eye(128)
    head0 = np.zeros((128, 3))
    head1 = np.zeros((128, 7))
    head8 = np.zeros((128, 3, HEADS0))
    for r in range(120):
        head0[r, r // D0] = 1
    for r in range(112):
        head1[r, r // D1] = 1
    for g in range(3):
        for r in range(G0[g]):
            head8[r, g, HO0[g] + r // D0] = 1
    c["head0"], c["head1"], c["head8"] = head0, head1, head8.reshape(128, -1)
    for name, hg, to, ho, keys, tiles, cols, d in (("0", HG0, TO0, HO0, KEYS0, T0, V0C, D0), ("1", HG1, TO1, HO1, KEYS1, T1, V1C, D1)):
        sel = np.zeros((128, tiles, 128))
        v = np.zeros((128, tiles, cols))
        for g in range(3):
            for h, _, n, tile, row in pieces(hg[g], keys):
                sel[ho[g] + h, to[g] + tile, row:row + n] = 1
                v[row:row + n, to[g] + tile, hg[g] * d + h] = 1
        c["sel" + name], c["vone" + name] = sel.reshape(128, -1), v.reshape(128, -1)
    expand = np.zeros((96, 2, SQ))
    for q, ch in enumerate(np.linspace(0, CAD - 1, SQ).astype(np.int64)):
        expand[ch % 96, ch // 96, q] = 1
    c["expand"] = expand.reshape(96, -1)
    return {k: np.ascontiguousarray(v, dtype=np.float32) for k, v in c.items()}


def xattn_kernel(nc, t):
    f32, f32r = mybir.dt.float32, mybir.dt.float32r
    ALU, ACT, AX = mybir.AluOpType, mybir.ActivationFunctionType, mybir.AxisListType.X
    es = ExitStack()
    with es:
        def sb(name, shape, dt=f32):
            return es.enter_context(nc.sbuf_tensor(name, shape, dt))

        def sem(name):
            return es.enter_context(nc.semaphore(name))

        ident = sb("ident", [128, 128])
        head0 = sb("head0", [128, 3])
        head1 = sb("head1", [128, 7])
        head8 = sb("head8", [128, 3, HEADS0])
        sel0 = sb("sel0", [128, T0, 128], f32r)
        sel1 = sb("sel1", [128, T1, 128], f32r)
        expand = sb("expand", [96, 2, SQ])
        wq0 = sb("wq0", [112, 3, H])
        wca = sb("wca", [112, 3, 3 * HT])
        wo0 = sb("wo0", [128, 3, H])
        wq1 = sb("wq1", [112, 3, H])
        wo1 = sb("wo1", [112, 3, H])
        wk0, wv0, wk1, wv1 = (sb(n, [CK, 2, H]) for n in ("wk0", "wv0", "wk1", "wv1"))
        bias0 = sb("bias0", [112, 3])
        bias1 = sb("bias1", [112, 3])
        enc = sb("enc", [CK, 2, B, CTX])
        encb = sb("encb", [CK, 2, CTX])
        kt0 = sb("kt0", [120, 3, B, KEYS0])
        kt1 = sb("kt1", [112, 3, B, KEYS1])
        k2t = sb("k2t", [120, 3, B * T])
        v2t = sb("v2t", [120, 3, B * T])
        wk2 = sb("wk2", [128, PAIRS, B * HT])
        v2w = sb("v2w", [128, 2, H])
        xt = sb("xt", [112, 3, SQ])
        xres = sb("xres", [112, 3, SQ])
        xkeys = sb("xkeys", [128, QT, HEADS0, 64])
        cast = sb("cast", [97, CCOL], f32r)
        gst = sb("gst", [97, SQ], f32r)
        q0 = sb("q0", [120, 3, SQ])
        q0hi = sb("q0hi", [120, 3, SQ], f32r)
        q1 = sb("q1", [112, 3, SQ])
        q1hi = sb("q1hi", [112, 3, SQ], f32r)
        k0 = sb("k0", [120, T0 * 128])
        k0hi = sb("k0hi", [120, T0 * 128], f32r)
        k1 = sb("k1", [112, T1 * 128])
        k1hi = sb("k1hi", [112, T1 * 128], f32r)
        v0s = sb("v0s", [KEYS0, H])
        v1s = sb("v1s", [KEYS1, H])
        v0 = sb("v0", [128, T0, V0C])
        v1 = sb("v1", [128, T1, V1C])
        negm0 = sb("negm0", [128, QT, HEADS0])
        negm1 = sb("negm1", [128, QT, HEADS1])
        negmc = sb("negmc", [128, NC])
        mt0 = sb("mt0", [128, SQ], f32r)
        mt1 = sb("mt1", [128, SQ], f32r)
        mtc = sb("mtc", [NC, 128], f32r)
        p0 = sb("p0", [128, T0, SQ])
        p1 = sb("p1", [128, T1, SQ])
        pc = sb("pc", [128, QT, CCOL])
        u0 = sb("u0", [V0C, 3, SQ])
        u1 = sb("u1", [120, 3, SQ])
        uc = sb("uc", [128, PAIRS, CAD])
        den0 = sb("den0", [HEADS0, SQ])
        den1 = sb("den1", [HEADS1, SQ])
        denc = sb("denc", [2 * PAIRS, CAD])
        rec0 = sb("rec0", [HEADS0, SQ])
        rec1 = sb("rec1", [HEADS1, SQ])
        recc = sb("recc", [2 * PAIRS, CAD])
        rb0 = sb("rb0", [120, 3, SQ])
        rb1 = sb("rb1", [112, 3, SQ])
        rbc = sb("rbc", [128, PAIRS, CAD])
        at0 = sb("at0", [128, 3, SQ])
        at1 = sb("at1", [112, 3, SQ])
        hsc = sb("hsc", [128, PAIRS, CAD])
        wk2b = sb("wk2b", [128, PAIRS, HT])
        s2t = sb("s2t", [HT, CAD])
        mx2 = sb("mx2", [96, 2 * HEADS0])
        sh2 = sb("sh2", [96, 2 * HEADS0, T])
        e2 = sb("e2", [96, 2 * HEADS0, T])
        sum2 = sb("sum2", [96, 2 * HEADS0])
        rc2 = sb("rc2", [96, 2 * HEADS0])
        p2 = sb("p2", [96, 2 * HEADS0, T])
        x1 = sb("x1", [112, 3, SQ])
        x1res = sb("x1res", [112, 3, SQ])
        outs = sb("outs", [112, 3, SQ])
        cabd = pc
        cahi = p1[:, 0:2 * CCOL // SQ, :].rearrange("p a q -> p (a q)").bitcast(f32r)
        calo = pc[:, :, :].rearrange("p j n -> p (j n)").bitcast(f32r)
        wq0t = p0[0:120, :, :].rearrange("p (g e) q -> p g (e q)", g=3)
        k2bd, v2bd = u0, u1
        wkca, wvca = (x[0:CK, :, :].rearrange("p g q -> p (g q)")[:, 0:2 * H].rearrange("p (j n) -> p j n", j=2) for x in (x1, x1res))
        bank = [es.enter_context(nc.psum_tensor(f"bank{i}", [128, 512], f32)) for i in range(8)]
        def dram(name, shape, dt=f32):
            return nc.dram_tensor(name, shape, dt, kind="Internal").ap()

        sel_d = [dram("sel0_scratch", (128, T0 * 128)), dram("sel1_scratch", (128, T1 * 128))]
        ca_d = dram("ca_hilo_scratch", (2, B, HT, CCOL))
        mtc_d = dram("mtc_scratch", (NC, 128))
        wk2_d = dram("wk2_scratch", (B, 128, PAIRS, HT))
        v2w_d = dram("v2w_scratch", (B, HT, H))
        denc_d = dram("denc_scratch", (2, PAIRS, CAD))
        r0_d = dram("rec0_scratch", (HEADS0, SQ))
        r1_d = dram("rec1_scratch", (HEADS1, SQ))
        rc_d = dram("recc_scratch", (2, PAIRS, CAD))

        full_a = [sem(f"bank_a{i}_full") for i in range(4)]
        free_a = [sem(f"bank_a{i}_drained") for i in range(4)]
        full_b = [sem(f"bank_b{i}_full") for i in range(4)]
        free_b = [sem(f"bank_b{i}_drained") for i in range(4)]
        const_in = sem("constants_loaded")
        wo0_in = sem("wo0_loaded")
        sel_copied = sem("sel_copied")
        sel_ready = sem("sel_loaded")
        setup_full = sem("setup_bank_full")
        setup_free = sem("setup_bank_free")
        init_dve = sem("dve_buffers_initialised")
        init_pool = sem("pool_buffers_initialised")
        ca_split = sem("ca_split")
        ca_stored = sem("ca_stored")
        kv2_masked = sem("k2_v2_masked")
        dve_init_step = sem("dve_init_step")
        v2w_stored, wk2_stored = sem("v2w_stored"), sem("wk2_stored")
        xt_in, enc_in, xres_in, xkeys_in, ca_in, v2w_in = (
            sem(n) for n in ("xt_loaded", "enc_loaded", "xres_loaded", "xkeys_loaded", "ca_loaded", "v2w_loaded"))
        q0hi_ready, q1hi_ready = sem("q0hi_ready"), sem("q1hi_ready")
        g_hi = sem("g_hi_written")
        k0_ready, k1_ready = (sem(n) for n in ("k0_ready", "k1_ready"))
        v0_placed, v1_placed = sem("v0_placed"), sem("v1_placed")
        mtc_ready, mtc_st, mtc_placed = sem("mtc_ready"), sem("mtc_stored"), sem("mtc_placed")
        denc_st = sem("denc_stored")
        den0_in, den1_in, denc_in = (sem(n) for n in ("den0_gathered", "den1_gathered", "denc_gathered"))
        rec0_ready, rec1_ready, recc_ready = (sem(n) for n in ("rec0_ready", "rec1_ready", "recc_ready"))
        rec0_st, rec1_st, recc_st = (sem(n) for n in ("rec0_stored", "rec1_stored", "recc_stored"))
        rb0_in, rb1_in, rbc_in = (sem(n) for n in ("rb0_spread", "rb1_spread", "rbc_spread"))
        at0_ready, at1_ready, hsc_ready = (sem(n) for n in ("at0_ready", "at1_ready", "hsc_ready"))
        wk2b_in, p2_ready = sem("wk2b_loaded"), sem("p2_ready")
        e2_ready, soft2 = sem("e2_ready"), sem("soft2_step")
        x1res_ready, out_stored = sem("x1res_ready"), sem("out_stored")

        def at(b, n, k):
            return b * n + k

        def wait(eng, s, b, n, k):
            v = at(b, n, k)
            if not isinstance(v, int) or v > 0:
                eng.wait_ge(s, v)

        def a_free(pe, b, j):
            wait(pe, free_a[j % 4], b, USES_A, j // 4)

        def a_full(eng, b, j):
            wait(eng, full_a[j % 4], b, USES_A, j // 4 + 1)

        def a_full_before(eng, b, j):
            wait(eng, full_a[j % 4], b, USES_A, j // 4 + 1 - USES_A)

        def a_drained(eng, b, *jobs):
            for j in jobs:
                wait(eng, free_a[j % 4], b, USES_A, j // 4 + 1)

        def b_drained(eng, b, *jobs):
            for j in jobs:
                wait(eng, free_b[j % 4], b, USES_B, j // 4 + 1)

        def b_free(pe, b, j):
            wait(pe, free_b[j % 4], b, USES_B, j // 4)

        def b_full(eng, b, j):
            wait(eng, full_b[j % 4], b, USES_B, j // 4 + 1)

        def bank_a(j):
            return bank[j % 4]

        def bank_b(j):
            return bank[4 + j % 4]

        consts = [(ident[:, :], t["ident"]), (head0[:, :], t["head0"]), (head1[:, :], t["head1"]),
                  (head8[:, :, :].rearrange("p g h -> p (g h)"), t["head8"]), 
                  (expand[:, :, :].rearrange("p a q -> p (a q)"), t["expand"]),
                  (v0[:, :, :].rearrange("p a c -> p (a c)"), t["vone0"]), (v1[:, :, :].rearrange("p a c -> p (a c)"), t["vone1"])]
        for g in range(3):
            n, o = XG[g], XO[g]
            consts += [(wq0[0:n, g, :], t["wq0"][o:o + n, :]), (wca[0:n, g, :], t["wca"][o:o + n, :]),
                       (wq1[0:n, g, :], t["wq1"][o:o + n, :]), (wo1[0:n, g, :], t["wo1"][o:o + n, :]),
                       (bias0[0:n, g:g + 1], t["b0"][o:o + n, :]), (bias1[0:n, g:g + 1], t["b1"][o:o + n, :])]
            n, o = G0[g], GO0[g]
            consts.append((wq0t[0:n, g, :], t["wq0t"][o:o + n, :]))
        for w, name in ((wk0, "wk0"), (wv0, "wv0"), (wk1, "wk1"), (wv1, "wv1"), (wkca, "wkca"), (wvca, "wvca")):
            consts.append((w[:, :, :], t[name].rearrange("(j p) n -> p j n", p=CK)))
        consts.append((enc[:, :, :, :].rearrange("p j b k -> p j (b k)"), t["enc"].rearrange("(j p) n -> p j n", p=CK)))
        consts.append((cabd[:, :, :], t["cabd"].rearrange("(j p) n -> p j n", p=128)))
        consts_late = [(wo0[0:G0[g], g, :], t["wo0"][GO0[g]:GO0[g] + G0[g], :]) for g in range(3)]
        N_CONST = 16 * len(consts)
        N_LATE = 16 * len(consts_late)

        KT_JOBS = [(g, half) for g in range(3) for half in range(2)]
        SETUP = 2 * len(KT_JOBS) + 2 + PAIRS // 2 + 2

        TILE_GROUP0 = [(g, tile) for g in range(3) for tile in range(TILES0[g])]
        TILE_GROUP1 = [(g, tile) for g in range(3) for tile in range(TILES1[g])]

        def schedule(eng, body):
            body(0, True, False, False, True)
            body(1, True, True, False, True)
            with eng.Fori(2, B - 1) as b:
                body(b, True, True, True, True)
            body(B - 1, True, True, True, False)
            body(B, False, True, True, False)
            body(B + 1, False, False, True, False)

        block = es.enter_context(nc.Block())

        @block.sync
        def _(sp):
            for dst, src in consts:
                sp.dma_start(dst, src).then_inc(const_in, 16)
            for part, name in zip(sel_d, ("sel0", "sel1")):
                sp.dma_start(part, t[name]).then_inc(sel_copied, 16)

            def load_xt(b):
                for g in range(3):
                    sp.dma_start(xt[0:XG[g], g, :], t["xt"][b, XO[g]:XO[g] + XG[g], :]).then_inc(xt_in, 16)

            def load_enc(b):
                sp.dma_start(encb[:, :, :], t["encb"][b].rearrange("(j p) k -> p j k", p=CK)).then_inc(enc_in, 16)

            def load_xres(b):
                for g in range(3):
                    sp.dma_start(xres[0:XG[g], g, :], t["xt"][b, XO[g]:XO[g] + XG[g], :]).then_inc(xres_in, 16)

            def load_xkeys(b):
                for k in range(QT):
                    sp.dma_start(xkeys[:, k, :, 0:D0], t["x"][b, k * 128:(k + 1) * 128, :].rearrange("p (h d) -> p h d", d=D0))\
                        .then_inc(xkeys_in, 16)

            def load_ca(b):
                for r, part in enumerate((0, 0, 1)):
                    sp.dma_start(cast[HT * r:HT * (r + 1), :].bitcast(f32), ca_d[part, b, :, :]).then_inc(ca_in, 16)

            def load_v2w(b):
                sp.dma_start(wo0[96:128, 2, :], v2w_d[b, :, :]).then_inc(v2w_in, 16)

            def load_wk2(b):
                sp.dma_start(wk2b[:, :, :], wk2_d[b, :, :, :]).then_inc(wk2b_in, 16)

            def place_v(layer):
                src, dst, hg, ho, to, keys, d, done = (
                    (v0s, v0, HG0, HO0, TO0, KEYS0, D0, v0_placed), (v1s, v1, HG1, HO1, TO1, KEYS1, D1, v1_placed))[layer]
                for g in range(3):
                    for h, k, n, tile, row in pieces(hg[g], keys):
                        c = (ho[g] + h) * d
                        sp.dma_start(dst[row:row + n, to[g] + tile, h * d:(h + 1) * d], src[k:k + n, c:c + d]).then_inc(done, 16)

            sp.wait_ge(init_dve, 1)
            for dst, src in consts_late:
                sp.dma_start(dst, src).then_inc(wo0_in, 16)
            sp.wait_ge(sel_copied, 32)
            for dst, src in zip((sel0, sel1), sel_d):
                sp.dma_start(dst[:, :, :].rearrange("p a r -> p (a r)").bitcast(f32), src).then_inc(sel_ready, 16)
            load_xt(0)
            load_enc(0)
            load_xres(0)
            load_xkeys(0)
            sp.wait_ge(ca_split, 2)
            sp.dma_start(ca_d[0].rearrange("(j b) r n -> (b r) j n", j=2), cahi.bitcast(f32).rearrange("p (j n) -> p j n", j=2)).then_inc(ca_stored, 16)
            sp.dma_start(ca_d[1].rearrange("(j b) r n -> (b r) j n", j=2), calo.bitcast(f32).rearrange("p (j n) -> p j n", j=2)).then_inc(ca_stored, 16)
            sp.wait_ge(ca_stored, 32)
            load_ca(0)
            sp.wait_ge(setup_free, SETUP)
            for p in range(PAIRS):
                sp.dma_start(wk2_d[:, :, p, :].rearrange("b r n -> r b n"), wk2[:, p, :].rearrange("r (b n) -> r b n", b=B)).then_inc(wk2_stored, 16)
            sp.wait_ge(wk2_stored, 16 * PAIRS)
            load_wk2(0)
            sp.dma_start(v2w_d.rearrange("(j b) r n -> (b r) j n", j=2), v2w[:, :, :]).then_inc(v2w_stored, 16)
            sp.wait_ge(v2w_stored, 16)
            load_v2w(0)

            def body(b, do_a, do_b, do_c, more_a):
                if do_a:
                    a_full(sp, b, A_Q2G)
                    if more_a:
                        load_xt(b + 1)
                    a_full_before(sp, b, A_U + 1)
                    a_drained(sp, b, A_V0)
                    place_v(0)
                if do_c:
                    b_drained(sp, b - 2, B_O, B_O + 1)
                    for g in range(3):
                        sp.dma_start(t["out"][b - 2, XO[g]:XO[g] + XG[g], :], outs[0:XG[g], g, :]).then_inc(out_stored, 16)
                if do_a:
                    wait(sp, mtc_ready, b, 1, 1)
                    sp.dma_start(mtc_d, mtc[:, :].bitcast(f32)).then_inc(mtc_st, 16)
                    wait(sp, mtc_st, b, 16, 16)
                    sp.dma_start(cast[96:97, :].bitcast(f32), mtc_d.rearrange("j c -> (j c)").unsqueeze(0)).then_inc(mtc_placed, 16)
                    if more_a:
                        a_full(sp, b, A_V1)
                        load_enc(b + 1)
                    a_drained(sp, b, A_CU, A_CU + 1)
                    for odd in range(2):
                        sp.dma_start(denc_d[odd], uc[64 * odd + D0:64 * odd + D0 + 1, :, :]).then_inc(denc_st, 16)
                    wait(sp, denc_st, b, 32, 32)
                    sp.dma_start(denc[:, :], denc_d.rearrange("o p c -> (o p) c")).then_inc(denc_in, 16)
                    if more_a:
                        load_xkeys(b + 1)
                        load_ca(b + 1)
                    wait(sp, recc_ready, b, 1, 1)
                    sp.dma_start(rc_d.rearrange("o p c -> (o p) c"), recc[:, :]).then_inc(recc_st, 16)
                    wait(sp, recc_st, b, 16, 16)
                    for odd in range(2):
                        sp.dma_start(rbc[64 * odd:64 * odd + D0, :, :],
                                     rc_d[odd].unsqueeze(0).to_broadcast([D0, PAIRS, CAD])).then_inc(rbc_in, 16)
                    a_drained(sp, b, A_U, A_U + 1)
                    for g in range(3):
                        sp.dma_start(den0[HO0[g]:HO0[g] + HG0[g], :], u0[G0[g]:G0[g] + HG0[g], g, :]).then_inc(den0_in, 16)
                    wait(sp, rec0_ready, b, 1, 1)
                    sp.dma_start(r0_d[:, :], rec0[:, :]).then_inc(rec0_st, 16)
                    wait(sp, rec0_st, b, 16, 16)
                    for g in range(3):
                        sp.dma_start(rb0[0:G0[g], g, :], r0_d[HO0[g]:HO0[g] + HG0[g], :].unsqueeze(1)
                                     .to_broadcast([HG0[g], D0, SQ])).then_inc(rb0_in, 16)
                if do_b:
                    b_drained(sp, b - 1, B_U + 2)
                    for g in range(3):
                        n = HG1[g] * D1
                        sp.dma_start(den1[HO1[g]:HO1[g] + HG1[g], :], u1[n:n + HG1[g], g, :]).then_inc(den1_in, 16)
                if do_a:
                    a_drained(sp, b, A_V1)
                    place_v(1)
                if do_b:
                    wait(sp, rec1_ready, b - 1, 1, 1)
                    sp.dma_start(r1_d[:, :], rec1[:, :]).then_inc(rec1_st, 16)
                    wait(sp, rec1_st, b - 1, 16, 16)
                    for g in range(3):
                        sp.dma_start(rb1[0:XG[g], g, :], r1_d[HO1[g]:HO1[g] + HG1[g], :].unsqueeze(1)
                                     .to_broadcast([HG1[g], D1, SQ])).then_inc(rb1_in, 16)
                if do_a and more_a:
                    a_drained(sp, b, A_O, A_O + 1)
                    load_xres(b + 1)
                    load_v2w(b + 1)
                    load_wk2(b + 1)

            schedule(sp, body)
            sp.wait_ge(out_stored, 16 * 3 * B)

        @block.tensor
        def _(pe):
            mm, tr = nc.tensor.matmul, nc.tensor.transpose
            pe.wait_ge(const_in, N_CONST)

            def setup_bank(n):
                if n >= 8:
                    pe.wait_ge(setup_free, n - 7)
                return bank[n % 8]

            n = 0
            for w, keys, rows, offs in ((wk0, KEYS0, G0, GO0), (wk1, KEYS1, XG, XO)):
                for g, half in KT_JOBS:
                    ps = setup_bank(n)
                    for j in range(2):
                        last = mm(ps[0:rows[g], 0:4 * keys], w[:, j, offs[g]:offs[g] + rows[g]],
                                  enc[:, j, 4 * half:4 * half + 4, 0:keys], start=j == 0, stop=j == 1)
                    last.then_inc(setup_full, 1)
                    n += 1
            for w in (wkca, wvca):
                ps = setup_bank(n)
                for g in range(3):
                    for j in range(2):
                        last = mm(ps[0:G0[g], g * B * T:(g + 1) * B * T], w[:, j, GO0[g]:GO0[g] + G0[g]],
                                  enc[:, j, :, KEYS0:CTX], start=j == 0, stop=j == 1)
                last.then_inc(setup_full, 1)
                n += 1
            pe.wait_ge(kv2_masked, 6)
            for half in range(PAIRS // 2):
                ps = setup_bank(n)
                for e in range(2):
                    p = 2 * half + e
                    for g in range(3):
                        last = mm(ps[:, e * B * HT:(e + 1) * B * HT], wq0t[0:G0[g], g, p * 128:(p + 1) * 128],
                                  k2bd[0:G0[g], g, :], start=g == 0, stop=g == 2)
                last.then_inc(setup_full, 1)
                n += 1
            pe.wait_ge(wo0_in, N_LATE)
            for half in range(2):
                ps = setup_bank(n)
                for g in range(3):
                    last = mm(ps[:, 0:H], v2bd[0:G0[g], g, 128 * half:128 * (half + 1)], wo0[0:G0[g], g, :],
                              start=g == 0, stop=g == 2)
                last.then_inc(setup_full, 1)
                n += 1
            pe.wait_ge(setup_free, SETUP)
            pe.wait_ge(init_dve, 1)
            pe.wait_ge(init_pool, 1)
            pe.wait_ge(sel_ready, 32)

            def body(b, do_a, do_b, do_c, more_a):
                if do_a:
                    wait(pe, xt_in, b, 48, 48)
                    a_free(pe, b, A_Q01)
                    for g in range(2):
                        for k in range(3):
                            last = mm(bank_a(A_Q01)[0:G0[g], g * SQ:(g + 1) * SQ], wq0[0:XG[k], k, GO0[g]:GO0[g] + G0[g]],
                                      xt[0:XG[k], k, :], start=k == 0, stop=k == 2)
                    last.then_inc(full_a[A_Q01 % 4], 1)
                    a_free(pe, b, A_Q2G)
                    for k in range(3):
                        mm(bank_a(A_Q2G)[0:G0[2], 0:SQ], wq0[0:XG[k], k, GO0[2]:H], xt[0:XG[k], k, :], start=k == 0, stop=k == 2)
                    for k in range(3):
                        last = mm(bank_a(A_Q2G)[0:3 * HT, SQ:2 * SQ], wca[0:XG[k], k, :], xt[0:XG[k], k, :], start=k == 0, stop=k == 2)
                    last.then_inc(full_a[A_Q2G % 4], 1)
                    wait(pe, enc_in, b, 16, 16)
                    for job, keys, w in ((A_V0, KEYS0, wv0), (A_V1, KEYS1, wv1)):
                        a_free(pe, b, job)
                        for j in range(2):
                            last = mm(bank_a(job)[0:keys, 0:H], encb[:, j, 0:keys], w[:, j, :], start=j == 0, stop=j == 1)
                        last.then_inc(full_a[job % 4], 1)
                if do_c:
                    wait(pe, at1_ready, b - 2, 2, 2)
                    for i, ms in enumerate(((0, 1), (2,))):
                        b_free(pe, b - 2, B_O + i)
                        for e, m in enumerate(ms):
                            for g in range(3):
                                last = mm(bank_b(B_O + i)[0:XG[m], e * SQ:(e + 1) * SQ], wo1[0:XG[g], g, XO[m]:XO[m] + XG[m]],
                                          at1[0:XG[g], g, :], start=g == 0, stop=g == 2)
                        last.then_inc(full_b[(B_O + i) % 4], 1)
                if do_b:
                    a_drained(pe, b - 1, A_O, A_O + 1)
                    for i, ms in enumerate(((0, 1), (2,))):
                        b_free(pe, b - 1, B_Q + i)
                        for e, m in enumerate(ms):
                            for g in range(3):
                                last = mm(bank_b(B_Q + i)[0:XG[m], e * SQ:(e + 1) * SQ], wq1[0:XG[g], g, XO[m]:XO[m] + XG[m]],
                                          x1[0:XG[g], g, :], start=g == 0, stop=g == 2)
                        last.then_inc(full_b[(B_Q + i) % 4], 1)
                if do_a:
                    wait(pe, ca_in, b, 48, 48)
                    a_drained(pe, b, A_Q2G)
                    for i in range(NC // 2):
                        a_free(pe, b, A_CS + i)
                        for e in range(2):
                            c = (2 * i + e) * 128
                            last = mm(bank_a(A_CS + i)[:, e * SQ:(e + 1) * SQ], cast[0:96, c:c + 128], gst[0:96, :], start=True, stop=True)
                        last.then_inc(full_a[(A_CS + i) % 4], 1)
                    wait(pe, q0hi_ready, b, 1, 1)
                    wait(pe, k0_ready, b, 1, 1)
                    for i in range(3):
                        a_free(pe, b, A_SM + i)
                        for q, g in (((i, 0), (i, 1)) if i < 2 else ((0, 2), (1, 2))):
                            cols = (HG0[g] * KEYS0 + 1) // 2 * 2
                            c = (220 * g) if i < 2 else 146 * q
                            last = mm(bank_a(A_SM + i)[:, c:c + cols], q0hi[:, g, q * 128:(q + 1) * 128],
                                      k0hi[:, 256 * g:256 * g + cols], start=True, stop=True)
                        last.then_inc(full_a[(A_SM + i) % 4], 1)
                    a_drained(pe, b, A_SM, A_SM + 1, A_SM + 2)
                    a_drained(pe, b, A_CS + 2, A_CS + 3, A_CS + 4, A_CS + 5)
                    a_free(pe, b, A_M)
                    for q in range(QT):
                        tr(bank_a(A_M)[0:HEADS0, q * 128:(q + 1) * 128], negm0[:, q, :], ident[:, :])
                    tr(bank_a(A_M)[0:NC, SQ:SQ + 128], negmc[:, :], ident[:, :]).then_inc(full_a[A_M % 4], 1)
                if do_b:
                    wait(pe, q1hi_ready, b - 1, 2, 2)
                    wait(pe, k1_ready, b - 1, 1, 1)
                    for q in range(QT):
                        for i, parts in enumerate((((0, 0, 308, 0),), ((0, 308, 232, 0), (1, 308, 232, 232)), ((1, 0, 308, 0),), ((2, 0, 462, 0),))):
                            job = B_SM + 4 * q + i
                            b_free(pe, b - 1, job)
                            for g, k, cols, c in parts:
                                last = mm(bank_b(job)[:, c:c + cols], q1hi[0:XG[g], g, q * 128:(q + 1) * 128],
                                          k1hi[0:XG[g], 128 * TO1[g] + k:128 * TO1[g] + k + cols], start=True, stop=True)
                            last.then_inc(full_b[job % 4], 1)
                if do_a:
                    wait(pe, mtc_placed, b, 16, 16)
                    for c in range(3):
                        for k in range(QT):
                            job = A_CT + 2 * c + k
                            a_free(pe, b, job)
                            mm(bank_a(job)[:, :], gst[:, k * 128:(k + 1) * 128], cast[:, c * 512:(c + 1) * 512], start=True, stop=True)\
                                .then_inc(full_a[job % 4], 1)
                    wait(pe, xkeys_in, b, 32, 32)
                    for i in range(2):
                        a_drained(pe, b, *(range(A_CT, A_CT + 4), range(A_CT + 4, A_CT + 6))[i])
                        a_free(pe, b, A_CU + i)
                        for e in range(2):
                            for k in range(QT):
                                for odd in range(2):
                                    h = 4 * i + 2 * e + odd
                                    last = mm(bank_a(A_CU + i)[64 * odd:64 * odd + 64, e * CAD:(e + 1) * CAD], xkeys[:, k, h, :],
                                              pc[:, k, h * CAD:(h + 1) * CAD], start=k == 0, stop=k == QT - 1)
                        last.then_inc(full_a[(A_CU + i) % 4], 1)
                    a_drained(pe, b, A_Q01, A_Q2G)
                    a_drained(pe, b, A_M)
                    for i in range(3):
                        a_free(pe, b, A_ST + i)
                        for e in range(2):
                            tile = 2 * i + e
                            g = TILE_GROUP0[tile][0]
                            ps = bank_a(A_ST + i)[:, e * SQ:(e + 1) * SQ]
                            mm(ps, k0[:, tile * 128:(tile + 1) * 128], q0[:, g, :], start=True, stop=False)
                            last = mm(ps, sel0[:, tile, :], mt0[:, :], start=False, stop=True)
                        last.then_inc(full_a[(A_ST + i) % 4], 1)
                    wait(pe, v0_placed, b, 16 * N_V0, 16 * N_V0)
                    for i, gs in enumerate(((0, 1), (2,))):
                        a_drained(pe, b, *((A_ST, A_ST + 1), (A_ST + 2,))[i])
                        a_free(pe, b, A_U + i)
                        for e, g in enumerate(gs):
                            rows = G0[g] + HG0[g]
                            for tile in range(2):
                                last = mm(bank_a(A_U + i)[0:rows, e * SQ:(e + 1) * SQ], v0[:, 2 * g + tile, 0:rows],
                                          p0[:, 2 * g + tile, :], start=tile == 0, stop=tile == 1)
                        last.then_inc(full_a[(A_U + i) % 4], 1)
                if do_b:
                    b_drained(pe, b - 1, *range(B_SM + 4, B_SM + 8))
                    for q in range(QT):
                        b_free(pe, b - 1, B_M + q)
                        tr(bank_b(B_M + q)[0:HEADS1, 0:128], negm1[:, q, :], ident[:, :]).then_inc(full_b[(B_M + q) % 4], 1)
                    b_drained(pe, b - 1, B_Q, B_Q + 1)
                    b_drained(pe, b - 1, B_M, B_M + 1)
                    for i in range(T1 // 2):
                        b_free(pe, b - 1, B_ST + i)
                        for e in range(2):
                            tile = 2 * i + e
                            g = TILE_GROUP1[tile][0]
                            ps = bank_b(B_ST + i)[:, e * SQ:(e + 1) * SQ]
                            mm(ps, k1[0:XG[g], tile * 128:(tile + 1) * 128], q1[0:XG[g], g, :], start=True, stop=False)
                            last = mm(ps, sel1[:, tile, :], mt1[:, :], start=False, stop=True)
                        last.then_inc(full_b[(B_ST + i) % 4], 1)
                if do_a:
                    wait(pe, hsc_ready, b, 1, 1)
                    wait(pe, wk2b_in, b, 16, 16)
                    a_free(pe, b, A_S2)
                    for p in range(PAIRS):
                        last = mm(bank_a(A_S2)[0:HT, 0:CAD], wk2b[:, p, :], hsc[:, p, :], start=p == 0, stop=p == PAIRS - 1)
                    last.then_inc(full_a[A_S2 % 4], 1)
                    a_drained(pe, b, A_S2)
                    a_free(pe, b, A_TR)
                    for c in range(2):
                        last = mm(bank_a(A_TR)[0:96, c * HT:(c + 1) * HT], s2t[:, c * 96:(c + 1) * 96], ident[0:HT, 0:HT], start=True, stop=True)
                    last.then_inc(full_a[A_TR % 4], 1)
                if do_b:
                    wait(pe, v1_placed, b - 1, 16 * N_V1, 16 * N_V1)
                    for g in range(3):
                        b_drained(pe, b - 1, *range(B_ST + TO1[g] // 2, B_ST + (TO1[g] + TILES1[g] + 1) // 2))
                        b_free(pe, b - 1, B_U + g)
                        rows = HG1[g] * (D1 + 1)
                        for tile in range(TILES1[g]):
                            last = mm(bank_b(B_U + g)[0:rows, 0:SQ], v1[:, TO1[g] + tile, 0:rows], p1[:, TO1[g] + tile, :],
                                      start=tile == 0, stop=tile == TILES1[g] - 1)
                        last.then_inc(full_b[(B_U + g) % 4], 1)
                if do_a:
                    wait(pe, p2_ready, b, 1, 1)
                    a_free(pe, b, A_EX)
                    for c in range(2):
                        last = mm(bank_a(A_EX)[96:128, 0:SQ], p2[:, c * HEADS0:(c + 1) * HEADS0, :].rearrange("p h t -> p (h t)"),
                                  expand[:, c, :], start=c == 0, stop=c == 1)
                    last.then_inc(full_a[A_EX % 4], 1)
                    wait(pe, at0_ready, b, 2, 2)
                    a_drained(pe, b, A_EX)
                    wait(pe, v2w_in, b, 16, 16)
                    for i, ms in enumerate(((0, 1), (2,))):
                        a_free(pe, b, A_O + i)
                        for e, m in enumerate(ms):
                            for g in range(3):
                                rows = (120, 120, 128)[g]
                                last = mm(bank_a(A_O + i)[0:XG[m], e * SQ:(e + 1) * SQ], wo0[0:rows, g, XO[m]:XO[m] + XG[m]],
                                          at0[0:rows, g, :], start=g == 0, stop=g == 2)
                        last.then_inc(full_a[(A_O + i) % 4], 1)

            schedule(pe, body)

        @block.scalar
        def _(act):
            def copy(out, in_):
                return nc.scalar.activation(out, in_, ACT.Copy)

            n = 0
            for kt, keys, rows in ((kt0, KEYS0, G0), (kt1, KEYS1, XG)):
                for g, half in KT_JOBS:
                    act.wait_ge(setup_full, n + 1)
                    copy(kt[0:rows[g], g, 4 * half:4 * half + 4, :].rearrange("p b k -> p (b k)"), bank[n % 8][0:rows[g], 0:4 * keys])\
                        .then_inc(setup_free, 1)
                    n += 1
            for kt in (k2t, v2t):
                act.wait_ge(setup_full, n + 1)
                for g in range(3):
                    last = copy(kt[0:G0[g], g, :], bank[n % 8][0:G0[g], g * B * T:(g + 1) * B * T])
                last.then_inc(setup_free, 1)
                n += 1
            for half in range(2):
                act.wait_ge(setup_full, n + 1)
                copy(wk2[:, 2 * half:2 * half + 2, :].rearrange("p a n -> p (a n)"), bank[n % 8][:, :]).then_inc(setup_free, 1)
                n += 1
            for half in range(2):
                act.wait_ge(setup_full, n + 1)
                copy(v2w[:, half, :], bank[n % 8][:, 0:H]).then_inc(setup_free, 1)
                n += 1

            act.wait_ge(ca_stored, 32)

            def body(b, do_a, do_b, do_c, more_a):
                if do_a:
                    a_full(act, b, A_Q01)
                    copy(q0[:, 0:2, :], bank_a(A_Q01)[0:120, :].rearrange("p (g q) -> p g q", q=SQ))\
                        .then_inc(free_a[A_Q01 % 4], 1)
                    for job, vs, placed, pieces_ in ((A_V0, v0s, v0_placed, N_V0), (A_V1, v1s, v1_placed, N_V1)):
                        a_full(act, b, job)
                        wait(act, placed, b, 16 * pieces_, 0)
                        copy(vs[:, :], bank_a(job)[0:(KEYS0 if vs is v0s else KEYS1), 0:H]).then_inc(free_a[job % 4], 1)
                if do_b:
                    for i in range(2):
                        b_full(act, b - 1, B_Q + i)
                        dst, src = ((q1[:, 0:2, :], bank_b(B_Q)[0:112, :].rearrange("p (g q) -> p g q", q=SQ)),
                                    (q1[0:96, 2, :], bank_b(B_Q + 1)[0:96, 0:SQ]))[i]
                        copy(dst, src).then_inc(free_b[(B_Q + i) % 4], 1)
                if do_a:
                    for c in range(3):
                        for k in range(QT):
                            job = A_CT + 2 * c + k
                            a_full(act, b, job)
                            nc.scalar.activation(pc[:, k, c * 512:(c + 1) * 512], bank_a(job)[:, :], ACT.Exp, scale=SCALE0)\
                                .then_inc(free_a[job % 4], 1)
                    wait(act, hsc_ready, b, 1, 0)
                    for i in range(2):
                        a_full(act, b, A_CU + i)
                        copy(uc[:, 2 * i:2 * i + 2, :].rearrange("p e c -> p (e c)"), bank_a(A_CU + i)[:, 0:2 * CAD])\
                            .then_inc(free_a[(A_CU + i) % 4], 1)
                    for i in range(3):
                        a_full(act, b, A_ST + i)
                        nc.scalar.activation(p0[:, 2 * i:2 * i + 2, :].rearrange("p a q -> p (a q)"), bank_a(A_ST + i)[:, :], ACT.Exp, scale=SCALE0)\
                            .then_inc(free_a[(A_ST + i) % 4], 1)
                    wait(act, at0_ready, b, 2, 0)
                    for i in range(2):
                        a_full(act, b, A_U + i)
                        dst, src = ((u0[:, 0:2, :], bank_a(A_U)[0:V0C, :].rearrange("p (g q) -> p g q", q=SQ)),
                                    (u0[0:G0[2] + HG0[2], 2, :], bank_a(A_U + 1)[0:G0[2] + HG0[2], 0:SQ]))[i]
                        copy(dst, src).then_inc(free_a[(A_U + i) % 4], 1)
                if do_b:
                    for i in range(T1 // 2):
                        b_full(act, b - 1, B_ST + i)
                        nc.scalar.activation(p1[:, 2 * i:2 * i + 2, :].rearrange("p a q -> p (a q)"), bank_b(B_ST + i)[:, :], ACT.Exp, scale=SCALE1)\
                            .then_inc(free_b[(B_ST + i) % 4], 1)
                if do_a:
                    a_full(act, b, A_S2)
                    copy(s2t[:, :], bank_a(A_S2)[0:HT, 0:CAD]).then_inc(free_a[A_S2 % 4], 1)
                    a_drained(act, b, A_TR)
                    nc.scalar.activation(e2[:, :, :], sh2[:, :, :], ACT.Exp, scale=SCALE0).then_inc(e2_ready, 1)
                if do_b:
                    wait(act, at1_ready, b - 1, 2, 0)
                    for g in range(3):
                        b_full(act, b - 1, B_U + g)
                        rows = HG1[g] * (D1 + 1)
                        copy(u1[0:rows, g, :], bank_b(B_U + g)[0:rows, 0:SQ]).then_inc(free_b[(B_U + g) % 4], 1)

            schedule(act, body)

        @block.vector
        def _(dve):
            tt, cp = nc.vector.tensor_tensor, nc.vector.tensor_copy
            nc.vector.memset(xkeys[:, :, :, :].rearrange("p k h d -> p (k h d)"), 0.0).then_inc(dve_init_step, 1)
            nc.vector.memset(q0[:, 2, :], 0.0)
            nc.vector.memset(q0hi[:, 2, :].bitcast(f32), 0.0)
            nc.vector.memset(mt0[:, :].bitcast(f32), 0.0)
            nc.vector.memset(mt1[:, :].bitcast(f32), 0.0)
            nc.vector.memset(at0[:, 2, :], 0.0)
            nc.vector.memset(rbc[:, :, :].rearrange("p a c -> p (a c)"), 1.0)
            nc.vector.memset(wo0[64:96, 2, :], 0.0)
            nc.vector.memset(gst[96:97, :].bitcast(f32), 1.0)
            dve.wait_ge(dve_init_step, 1)
            nc.vector.memset(xkeys[:, :, :, D0:D0 + 1].rearrange("p k h d -> p (k h) d"), 1.0).then_inc(init_dve, 1)
            dve.wait_ge(const_in, N_CONST)
            whole = cabd[:, :, :].rearrange("p j n -> p (j n)")
            cp(cahi, whole).then_inc(ca_split, 1)
            dve.wait_ge(ca_split, 1)
            tt(calo, whole, cahi.bitcast(f32), ALU.subtract).then_inc(ca_split, 1)
            dve.wait_ge(setup_free, 2 * len(KT_JOBS) + 2)
            for src, dst in ((k2t, k2bd), (v2t, v2bd)):
                for g in range(3):
                    r = G0[g]
                    tt(dst[0:r, g, :].rearrange("p (b h t) -> p b h t", b=B, h=HEADS0),
                       src[0:r, g, :].rearrange("p (b t) -> p b t", t=T).unsqueeze(2).to_broadcast([r, B, HEADS0, T]),
                       head8[0:r, g, :].unsqueeze(1).unsqueeze(3).to_broadcast([r, B, HEADS0, T]), ALU.mult).then_inc(kv2_masked, 1)

            def body(b, do_a, do_b, do_c, more_a):
                if do_a:
                    a_full(dve, b, A_Q2G)
                    ps = bank_a(A_Q2G)
                    cp(q0[0:G0[2], 2, :], ps[0:G0[2], 0:SQ])
                    cp(gst[0:96, :], ps[0:96, SQ:2 * SQ]).then_inc(g_hi, 1)
                    wait(dve, g_hi, b, 1, 1)
                    tt(gst[32:64, :], ps[32:64, SQ:2 * SQ], gst[32:64, :].bitcast(f32), ALU.subtract)\
                        .then_inc(free_a[A_Q2G % 4], 1)
                    a_drained(dve, b, A_Q01)
                    cp(q0hi[:, :, :].rearrange("p g q -> p (g q)"), q0[:, :, :].rearrange("p g q -> p (g q)")).then_inc(q0hi_ready, 1)
                if do_c:
                    wait(dve, out_stored, b - 2, 48, 0)
                    wait(dve, x1res_ready, b - 2, 1, 1)
                    for i, ms in enumerate(((0, 1), (2,))):
                        b_full(dve, b - 2, B_O + i)
                        for e, m in enumerate(ms):
                            r = XG[m]
                            last = tt(outs[0:r, m, :], bank_b(B_O + i)[0:r, e * SQ:(e + 1) * SQ], x1res[0:r, m, :], ALU.add)
                        last.then_inc(free_b[(B_O + i) % 4], 1)
                if do_b:
                    b_drained(dve, b - 1, B_Q, B_Q + 1)
                    cp(q1hi[:, 0:2, :], q1[:, 0:2, :]).then_inc(q1hi_ready, 1)
                    cp(q1hi[0:96, 2, :], q1[0:96, 2, :]).then_inc(q1hi_ready, 1)
                if do_a:
                    for i in range(NC // 2):
                        a_full(dve, b, A_CS + i)
                        nc.vector.tensor_reduce(out=negmc[:, 2 * i:2 * i + 2], in_=bank_a(A_CS + i)[:, :].rearrange("p (e k) -> p e k", e=2),
                                                axis=AX, op=ALU.max, negate=True).then_inc(free_a[(A_CS + i) % 4], 1)
                    for i in range(3):
                        a_full(dve, b, A_SM + i)
                        if i < 2:
                            dst = negm0[:, i, 0:6].rearrange("p (g h) -> p g h", g=2)
                            src = bank_a(A_SM + i)[:, 0:440].rearrange("p (g k) -> p g k", g=2)[:, :, 0:219]\
                                .rearrange("p g (h k) -> p g h k", k=KEYS0)
                        else:
                            dst = negm0[:, :, 6:8]
                            src = bank_a(A_SM + i)[:, 0:292].rearrange("p (q h k) -> p q h k", q=2, k=KEYS0)
                        nc.vector.tensor_reduce(out=dst, in_=src, axis=AX, op=ALU.max, negate=True)\
                            .then_inc(free_a[(A_SM + i) % 4], 1)
                    a_full(dve, b, A_M)
                    cp(mtc[:, :], bank_a(A_M)[0:NC, SQ:SQ + 128]).then_inc(mtc_ready, 1)
                    cp(mt0[0:HEADS0, :], bank_a(A_M)[0:HEADS0, 0:SQ]).then_inc(free_a[A_M % 4], 1)
                if do_b:
                    for q in range(QT):
                        for i in range(4):
                            job = B_SM + 4 * q + i
                            b_full(dve, b - 1, job)
                            ps = bank_b(job)
                            if i == 1:
                                dst = negm1[:, q, 0:14].rearrange("p (g h) -> p g h", g=2)[:, :, 4:7]
                                src = ps[:, 0:464].rearrange("p (g k) -> p g k", g=2)[:, :, 0:231].rearrange("p g (h k) -> p g h k", k=KEYS1)
                            else:
                                h, n = ((0, 4), None, (7, 4), (14, 6))[i]
                                dst = negm1[:, q, h:h + n]
                                src = ps[:, 0:n * KEYS1].rearrange("p (h k) -> p h k", k=KEYS1)
                            nc.vector.tensor_reduce(out=dst, in_=src, axis=AX, op=ALU.max, negate=True)\
                                .then_inc(free_b[job % 4], 1)
                if do_a:
                    wait(dve, denc_in, b, 16, 16)
                    nc.vector.reciprocal(recc[:, :], denc[:, :]).then_inc(recc_ready, 1)
                if do_b:
                    for q in range(QT):
                        b_full(dve, b - 1, B_M + q)
                        cp(mt1[0:HEADS1, q * 128:(q + 1) * 128], bank_b(B_M + q)[0:HEADS1, 0:128])\
                            .then_inc(free_b[(B_M + q) % 4], 1)
                if do_a:
                    wait(dve, rbc_in, b, 32, 32)
                    tt(hsc[:, :, :], uc[:, :, :], rbc[:, :, :], ALU.mult).then_inc(hsc_ready, 1)
                    wait(dve, den0_in, b, 48, 48)
                    nc.vector.reciprocal(rec0[:, :], den0[:, :]).then_inc(rec0_ready, 1)
                    a_full(dve, b, A_TR)
                    s2 = bank_a(A_TR)[0:96, 0:2 * HT].rearrange("p (h t) -> p h t", t=T)
                    nc.vector.reduce_max(mx2[:, :], s2, AX).then_inc(soft2, 1)
                    wait(dve, soft2, b, 3, 1)
                    tt(sh2[:, :, :], s2, mx2[:, :].unsqueeze(2).to_broadcast([96, 2 * HEADS0, T]), ALU.subtract)\
                        .then_inc(free_a[A_TR % 4], 1)
                    wait(dve, e2_ready, b, 1, 1)
                    nc.vector.reduce_sum(sum2[:, :], e2[:, :, :], AX).then_inc(soft2, 1)
                    wait(dve, soft2, b, 3, 2)
                    nc.vector.reciprocal(rc2[:, :], sum2[:, :]).then_inc(soft2, 1)
                    wait(dve, soft2, b, 3, 3)
                    tt(p2[:, :, :], e2[:, :, :], rc2[:, :].unsqueeze(2).to_broadcast([96, 2 * HEADS0, T]), ALU.mult).then_inc(p2_ready, 1)
                    wait(dve, rb0_in, b, 48, 48)
                    tt(at0[0:120, 0:2, :], u0[0:120, 0:2, :], rb0[:, 0:2, :], ALU.mult).then_inc(at0_ready, 1)
                    tt(at0[0:80, 2, :], u0[0:80, 2, :], rb0[0:80, 2, :], ALU.mult).then_inc(at0_ready, 1)
                    a_full(dve, b, A_EX)
                    cp(at0[96:128, 2, :], bank_a(A_EX)[96:128, 0:SQ]).then_inc(free_a[A_EX % 4], 1)
                    wait(dve, xres_in, b, 48, 48)
                    wait(dve, x1res_ready, b, 1, 0)
                    for i, ms in enumerate(((0, 1), (2,))):
                        a_full(dve, b, A_O + i)
                        for e, m in enumerate(ms):
                            r = XG[m]
                            last = nc.vector.scalar_tensor_tensor(
                                out=x1[0:r, m, :], in0=bank_a(A_O + i)[0:r, e * SQ:(e + 1) * SQ], scalar=bias0[0:r, m:m + 1],
                                in1=xres[0:r, m, :], op0=ALU.add, op1=ALU.add)
                        last.then_inc(free_a[(A_O + i) % 4], 1)
                if do_b:
                    wait(dve, den1_in, b - 1, 48, 48)
                    nc.vector.reciprocal(rec1[:, :], den1[:, :]).then_inc(rec1_ready, 1)
                    wait(dve, rb1_in, b - 1, 48, 48)
                    tt(at1[:, 0:2, :], u1[0:112, 0:2, :], rb1[:, 0:2, :], ALU.mult).then_inc(at1_ready, 1)
                    tt(at1[0:96, 2, :], u1[0:96, 2, :], rb1[0:96, 2, :], ALU.mult).then_inc(at1_ready, 1)

            schedule(dve, body)

        @block.gpsimd
        def _(pool):
            for buf in (k0[:, :], k0hi[:, :].bitcast(f32), k1[:, :], k1hi[:, :].bitcast(f32)):
                last = nc.gpsimd.memset(buf, 0.0)
            last.then_inc(init_pool, 1)
            pool.wait_ge(init_pool, 1)
            pool.wait_ge(const_in, N_CONST)
            pool.wait_ge(setup_free, 2 * len(KT_JOBS) + 4)

            def build_k(layer, b):
                kt, mask, k, khi, hg, rows, to, keys, ready = (
                    (kt0, head0, k0, k0hi, HG0, G0, TO0, KEYS0, k0_ready), (kt1, head1, k1, k1hi, HG1, XG, TO1, KEYS1, k1_ready))[layer]
                for dst in (khi, k):
                    for g in range(3):
                        r, h, o = rows[g], hg[g], 128 * to[g]
                        last = nc.gpsimd.tensor_tensor(
                            dst[0:r, o:o + h * keys].rearrange("p (h k) -> p h k", k=keys),
                            kt[0:r, g, b, :].unsqueeze(1).to_broadcast([r, h, keys]),
                            mask[0:r, 0:h].unsqueeze(2).to_broadcast([r, h, keys]), ALU.mult)
                last.then_inc(ready, 1)

            build_k(0, 0)

            def body(b, do_a, do_b, do_c, more_a):
                if do_b:
                    a_drained(pool, b - 1, A_O, A_O + 1)
                    if do_c:
                        b_drained(pool, b - 2, B_O, B_O + 1)
                    for g in range(3):
                        r = XG[g]
                        last = nc.gpsimd.tensor_tensor(x1res[0:r, g, :], x1[0:r, g, :],
                                                       bias1[0:r, g:g + 1].to_broadcast([r, SQ]), ALU.add)
                    last.then_inc(x1res_ready, 1)
                if do_a and more_a:
                    a_full(pool, b, A_ST + 2)
                    build_k(0, b + 1)
                if do_b:
                    b_full(pool, b - 1, B_ST + T1 // 2 - 1)
                if do_a:
                    build_k(1, b)

            schedule(pool, body)


_OUT = (B, H, SQ)


def kernel(**inputs):
    import concourse.bacc as bacc
    from concourse.bass_utils import run_bass_kernel_spmd

    a = {k: np.asarray(v) for k, v in inputs.items()}
    x, ctx = a["x"], a["ctx_768"]
    wca = np.zeros((H, HEADS0, T), np.float32)
    cabd = np.zeros((B, HEADS0, T, HEADS0, CAD), np.float32)
    wq0t = np.zeros((H, PAIRS, 2, 64), np.float32)
    for h in range(HEADS0):
        wca[h * D0:(h + 1) * D0, h, :] = a["L0_xattn_Wq_ca"].T[h * D0:(h + 1) * D0]
        cabd[:, h, :, h, :] = ctx[:, KEYS0:, :]
    wq0t[:, :, :, 0:D0] = a["L0_xattn_Wq"].T.reshape(H, PAIRS, 2, D0)
    wca = wca.reshape(H, HT)
    arrays = {
        "xt": x.transpose(0, 2, 1), "x": x, "enc": ctx.transpose(2, 0, 1).reshape(CAD, B * CTX), "encb": ctx.transpose(0, 2, 1),
        "wq0": a["L0_xattn_Wq"], "wk0": a["L0_xattn_Wk"], "wv0": a["L0_xattn_Wv"], "wca": np.concatenate([wca, wca, wca], axis=1),
        "wkca": a["L0_xattn_Wk_ca"], "wvca": a["L0_xattn_Wv_ca"], "wo0": a["L0_xattn_Wout"], "b0": a["L0_xattn_b_out"].reshape(H, 1),
        "wq1": a["L1_xattn_Wq"], "wk1": a["L1_xattn_Wk"], "wv1": a["L1_xattn_Wv"], "wo1": a["L1_xattn_Wo"], "b1": a["L1_xattn_bo"].reshape(H, 1),
        "wq0t": wq0t.reshape(H, PAIRS * 128), "cabd": cabd.reshape(B * HT, CCOL), **constants(),
    }
    nc = bacc.Bacc("TRN2", target_bir_lowering=False, num_devices=1)
    f32 = mybir.dt.float32
    feed, t = {}, {}
    for name, v in arrays.items():
        feed["in_" + name] = np.ascontiguousarray(v)
        t[name] = nc.dram_tensor("in_" + name, v.shape, f32, kind="ExternalInput").ap()
    t["out"] = nc.dram_tensor("out_t", _OUT, f32, kind="ExternalOutput").ap()
    xattn_kernel(nc, t)
    r = run_bass_kernel_spmd(nc, [feed], core_ids=[0])
    return np.ascontiguousarray(np.asarray(r.results[0]["out_t"]).transpose(0, 2, 1))
```

```python
import concourse.bass as bass
from concourse import mybir
from contextlib import ExitStack
import numpy as np

B, SQ, H = 8, 256, 320
CTX, CAD, T = 77, 192, 4
QT = SQ // 128
CK = CAD // 2
XG = [112, 112, 96]
HEADS0, D0, KEYS0 = 8, 40, CTX - T
HG0 = [3, 3, 2]
G0 = [h * D0 for h in HG0]
HEADS1, D1, KEYS1 = 20, 16, CTX
HG1 = [7, 7, 6]
TILES0 = [2, 2, 2]
TILES1 = [5, 5, 4]
T0, T1 = sum(TILES0), sum(TILES1)
V0C, V1C = 3 * D0 + 3, 7 * D1 + 7
CCOL = HEADS0 * CAD
NC = CCOL // 128
PAIRS = HEADS0 // 2
HT = HEADS0 * T
SCALE0, SCALE1 = float(D0) ** -0.5, float(D1) ** -0.5
JOBS_A, JOBS_B = 32, 24
USES_A, USES_B = JOBS_A // 4, JOBS_B // 4
A_Q01, A_Q2G, A_CS, A_SM, A_M, A_CT, A_CU, A_ST, A_U, A_S2, A_TR, A_EX, A_O = (
    0, 1, 2, 8, 11, 12, 18, 20, 23, 26, 27, 28, 29)
B_Q, B_SM, B_M, B_ST, B_U, B_O = 0, 2, 10, 12, 19, 22


def pieces(heads, keys):
    out = []
    for h in range(heads):
        k = 0
        while k < keys:
            tile, row = divmod(h * keys + k, 128)
            n = min(keys - k, 128 - row)
            out.append((h, k, n, tile, row))
            k += n
    return out


def offsets(sizes):
    return [sum(sizes[:i]) for i in range(len(sizes))]


TO0, TO1, HO0, HO1, GO0, XO = (offsets(s) for s in (TILES0, TILES1, HG0, HG1, G0, XG))
VT = [(o, min(128, B * CTX - o)) for o in range(0, B * CTX, 128)]


def v_pieces(keys):
    out = []
    for tile, (o, n) in enumerate(VT):
        for b in range(B):
            lo, hi = max(o, b * CTX), min(o + n, b * CTX + keys)
            if lo < hi:
                out.append((tile, lo - o, hi - lo, b, lo - b * CTX))
    return out


def v_loads(hg, keys, tiles):
    full = [n * keys // 128 for n in hg]
    rest = [n * keys % 128 for n in hg]
    out = [(128, g, 1, 0, full[g]) for g in range(3) if full[g] > 1] or [(128, 0, 3, 0, 1)]
    return out + [(rest[0], 0, 2, full[0], 1), (rest[2], 2, 1, full[2], 1)]


LOADS0, LOADS1 = v_loads(HG0, KEYS0, TILES0), v_loads(HG1, KEYS1, TILES1)
N_V0, N_V1 = 16 * len(LOADS0), 16 * len(LOADS1)


SMALL = {"ident": 128, "head0": 3, "head1": 7, "head8": 3 * HEADS0, "head96": HEADS0, "vhead0": T0 * 3, "vhead1": T1 * 7}
WIDE = {"wq0": H, "wca": 3 * HT, "wq1": H, "wo1": H, "b0": 1, "b1": 1}


def constants():
    c = {}
    c["ident"] = np.eye(128)
    head0 = np.zeros((128, 3))
    head1 = np.zeros((128, 7))
    head8 = np.zeros((128, 3, HEADS0))
    for r in range(120):
        head0[r, r // D0] = 1
    for r in range(112):
        head1[r, r // D1] = 1
    for g in range(3):
        for r in range(G0[g]):
            head8[r, g, HO0[g] + r // D0] = 1
    head96 = np.zeros((128, HEADS0))
    for i in range(3 * HT):
        head96[i, i % HT // T] = 1
    c["head0"], c["head1"], c["head8"], c["head96"] = head0, head1, head8.reshape(128, -1), head96
    for name, hg, to, ho, keys, tiles, cols, d in (("0", HG0, TO0, HO0, KEYS0, T0, V0C, D0), ("1", HG1, TO1, HO1, KEYS1, T1, V1C, D1)):
        sel = np.zeros((128, tiles, 128))
        v = np.zeros((128, tiles, cols))
        for g in range(3):
            for h, _, n, tile, row in pieces(hg[g], keys):
                sel[ho[g] + h, to[g] + tile, row:row + n] = 1
                v[row:row + n, to[g] + tile, hg[g] * d + h] = 1
        c["sel" + name], c["vone" + name] = sel.reshape(128, -1), v.reshape(128, -1)
        mask = np.zeros((128, tiles, hg[0]))
        for g in range(3):
            for h, _, n, tile, row in pieces(hg[g], keys):
                mask[row:row + n, to[g] + tile, h] = 1
        c["vhead" + name] = mask.reshape(128, -1)
    expand = np.zeros((96, 2, SQ))
    for q, ch in enumerate(np.linspace(0, CAD - 1, SQ).astype(np.int64)):
        expand[ch % 96, ch // 96, q] = 1
    c["expand"] = expand.reshape(96, -1)
    c["small"] = np.concatenate([c.pop(n) for n in SMALL], axis=1)
    return {k: np.ascontiguousarray(v, dtype=np.float32) for k, v in c.items()}


def xattn_kernel(nc, t):
    f32, f32r = mybir.dt.float32, mybir.dt.float32r
    ALU, ACT, AX = mybir.AluOpType, mybir.ActivationFunctionType, mybir.AxisListType.X
    es = ExitStack()
    with es:
        def sb(name, shape, dt=f32):
            return es.enter_context(nc.sbuf_tensor(name, shape, dt))

        def sem(name):
            return es.enter_context(nc.semaphore(name))

        small = sb("small", [128, sum(SMALL.values())])
        o = offsets(list(SMALL.values()))
        ident, head0, head1, head8, head96, vhead0, vhead1 = (small[:, a:a + n] for a, n in zip(o, SMALL.values()))
        head8 = head8.rearrange("p (g h) -> p g h", g=3)
        vhead0, vhead1 = vhead0.rearrange("p (a h) -> p a h", h=3), vhead1.rearrange("p (a h) -> p a h", h=7)
        sel0 = sb("sel0", [128, T0, 128], f32r)
        sel1 = sb("sel1", [128, T1, 128], f32r)
        expand = sb("expand", [96, 2, SQ])
        wide = sb("wide", [112, 3, sum(WIDE.values())])
        o = offsets(list(WIDE.values()))
        wq0, wca, wq1, wo1, bias0, bias1 = (wide[:, :, a:a + n] for a, n in zip(o, WIDE.values()))
        bias0, bias1 = (w.rearrange("p g o -> p (g o)") for w in (bias0, bias1))
        wo0 = sb("wo0", [128, 3, H])
        enc = sb("enc", [CK, 2, B, CTX])
        kt0 = sb("kt0", [120, 3, B, KEYS0])
        kt1 = sb("kt1", [112, 3, B, KEYS1])
        k2t = sb("k2t", [120, 3, B * T])
        v2t = sb("v2t", [120, 3, B * T])
        ca = sb("ca", [3 * HT, B, CAD], f32r)
        xt = sb("xt", [112, 3, SQ])
        xres = sb("xres", [112, 3, SQ])
        xkeys = sb("xkeys", [128, QT, HEADS0, 64])
        cast = sb("cast", [97, CCOL], f32r)
        gst = sb("gst", [97, SQ], f32r)
        q0 = sb("q0", [120, 3, SQ])
        q0hi = sb("q0hi", [120, 3, SQ], f32r)
        q1 = sb("q1", [112, 3, SQ])
        q1hi = sb("q1hi", [112, 3, SQ], f32r)
        k0 = sb("k0", [120, T0 * 128])
        k0hi = sb("k0hi", [120, T0 * 128], f32r)
        k1 = sb("k1", [112, T1 * 128])
        k1hi = sb("k1hi", [112, T1 * 128], f32r)
        v0c = sb("v0c", [128, T0, D0])
        v1c = sb("v1c", [128, T1, D1])
        v0 = sb("v0", [128, T0, V0C])
        v1 = sb("v1", [128, T1, V1C])
        negm0 = sb("negm0", [128, QT, HEADS0])
        negm1 = sb("negm1", [128, QT, HEADS1])
        negmc = sb("negmc", [128, NC])
        mt0 = sb("mt0", [128, SQ], f32r)
        mt1 = sb("mt1", [128, SQ], f32r)
        mtc = sb("mtc", [NC, 128], f32r)
        p0 = sb("p0", [128, T0, SQ])
        p1 = sb("p1", [128, T1, SQ])
        pc = sb("pc", [128, QT, CCOL])
        u0 = sb("u0", [V0C, 3, SQ])
        u1 = sb("u1", [120, 3, SQ])
        uc = sb("uc", [128, PAIRS, CAD])
        den0, rec0 = sb("den0", [128, HEADS0 * SQ // 128]), sb("rec0", [128, HEADS0 * SQ // 128])
        den1, rec1 = sb("den1", [128, HEADS1 * SQ // 128]), sb("rec1", [128, HEADS1 * SQ // 128])
        denc, recc = sb("denc", [128, CCOL // 128]), sb("recc", [128, CCOL // 128])
        rb0 = sb("rb0", [120, 3, SQ])
        rb1 = sb("rb1", [112, 3, SQ])
        rbc = sb("rbc", [128, PAIRS, CAD])
        at0 = sb("at0", [128, 3, SQ])
        at1 = sb("at1", [112, 3, SQ])
        hsc = sb("hsc", [128, PAIRS, CAD])
        wk2b = sb("wk2b", [128, PAIRS, HT])
        s2t = sb("s2t", [HT, CAD])
        mx2 = sb("mx2", [96, 2 * HEADS0])
        sh2 = sb("sh2", [96, 2 * HEADS0, T])
        e2 = sb("e2", [96, 2 * HEADS0, T])
        sum2 = sb("sum2", [96, 2 * HEADS0])
        rc2 = sb("rc2", [96, 2 * HEADS0])
        p2 = sb("p2", [96, 2 * HEADS0, T])
        x1 = sb("x1", [112, 3, SQ])
        x1res = sb("x1res", [112, 3, SQ])
        outs = sb("outs", [112, 3, SQ])
        def inside(buf):
            return buf[0:CK, :, :].rearrange("p g q -> p (g q)")[:, 0:2 * H].rearrange("p (j n) -> p j n", j=2)

        wk0, wv0, wk1, wv1, wkca, wvca = (inside(x) for x in (q1, outs, at1, rb1, x1, x1res))
        wq0t = p0[0:120, :, :].rearrange("p (g e) q -> p g (e q)", g=3)
        k2bd, v2bd = u0, u1
        ca_whole = p1[0:3 * HT, 7:13, :].rearrange("p a q -> p (a q)")
        v0stage = pc[:, :, :].rearrange("p a n -> p (a n)")[:, 0:5 * H].rearrange("p (a n) -> p a n", a=5)
        wk2 = p1[:, 0:4, :]
        v2w = p1[:, 4:7, :].rearrange("p a q -> p (a q)")[:, 0:2 * H].rearrange("p (a n) -> p a n", a=2)
        v1stage = p1[:, 7:14, :].rearrange("p a q -> p (a q)")[:, 0:5 * H].rearrange("p (a n) -> p a n", a=5)
        bank = [es.enter_context(nc.psum_tensor(f"bank{i}", [128, 512], f32)) for i in range(8)]
        def dram(name, shape, dt=f32):
            return nc.dram_tensor(name, shape, dt, kind="Internal").ap()

        sel_d = [dram("sel0_scratch", (128, T0 * 128)), dram("sel1_scratch", (128, T1 * 128))]
        v0_d = dram("v0_scratch", (B, HEADS0, KEYS0, D0))
        v1_d = dram("v1_scratch", (B, HEADS1, KEYS1, D1))
        wk2_d = dram("wk2_scratch", (B, 128, PAIRS, HT))
        v2w_d = dram("v2w_scratch", (B, HT, H))
        mtc_d = dram("mtc_scratch", (NC, 128))
        den0_d, r0_d = dram("den0_scratch", (HEADS0, SQ)), dram("rec0_scratch", (HEADS0, SQ))
        den1_d, r1_d = dram("den1_scratch", (HEADS1, SQ)), dram("rec1_scratch", (HEADS1, SQ))
        denc_d, rc_d = dram("denc_scratch", (2, PAIRS, CAD)), dram("recc_scratch", (2, PAIRS, CAD))

        full_a = [sem(f"bank_a{i}_full") for i in range(4)]
        free_a = [sem(f"bank_a{i}_drained") for i in range(4)]
        full_b = [sem(f"bank_b{i}_full") for i in range(4)]
        free_b = [sem(f"bank_b{i}_drained") for i in range(4)]
        kv0_in, kv1_in, kvca_in, wq0t_in = (sem(n) for n in ("kv0_weights_loaded", "kv1_weights_loaded", "kvca_weights_loaded", "wq0t_loaded"))
        ca_in, small_in, wide_in, wo0_in, expand_in, vones_in = (
            sem(n) for n in ("ca_loaded", "small_loaded", "wide_loaded", "wo0_loaded", "expand_loaded", "value_ones_loaded"))
        sel_copied = sem("sel_copied")
        sel_ready = sem("sel_loaded")
        setup_full = sem("setup_bank_full")
        setup_free = sem("setup_bank_free")
        init_dve = sem("dve_buffers_initialised")
        init_pool = sem("pool_buffers_initialised")
        ca_split = sem("ca_split")
        v0_stored, v1_stored = sem("v0_stored"), sem("v1_stored")
        kv2_masked = sem("k2_v2_masked")
        dve_init_step = sem("dve_init_step")
        v2w_stored, wk2_stored = sem("v2w_stored"), sem("wk2_stored")
        xt_in, xres_in, xkeys_in, v2w_in, v0c_in, v1c_in = (
            sem(n) for n in ("xt_loaded", "xres_loaded", "xkeys_loaded", "v2w_loaded", "v0c_loaded", "v1c_loaded"))
        q0hi_ready, q1hi_ready = sem("q0hi_ready"), sem("q1hi_ready")
        g_hi = sem("g_hi_written")
        k0_ready, k1_ready = (sem(n) for n in ("k0_ready", "k1_ready"))
        v0_ready, v1_ready, cast_ready = sem("v0_ready"), sem("v1_ready"), sem("cast_ready")
        mtc_ready, mtc_st, mtc_placed = sem("mtc_ready"), sem("mtc_stored"), sem("mtc_placed")
        den0_st, den1_st, denc_st = sem("den0_stored"), sem("den1_stored"), sem("denc_stored")
        den0_in, den1_in, denc_in = (sem(n) for n in ("den0_gathered", "den1_gathered", "denc_gathered"))
        rec0_ready, rec1_ready, recc_ready = (sem(n) for n in ("rec0_ready", "rec1_ready", "recc_ready"))
        rec0_st, rec1_st, recc_st = (sem(n) for n in ("rec0_stored", "rec1_stored", "recc_stored"))
        rb0_in, rb1_in, rbc_in = (sem(n) for n in ("rb0_spread", "rb1_spread", "rbc_spread"))
        at0_ready, at1_ready, hsc_ready = (sem(n) for n in ("at0_ready", "at1_ready", "hsc_ready"))
        wk2b_in, p2_ready = sem("wk2b_loaded"), sem("p2_ready")
        e2_ready, soft2 = sem("e2_ready"), sem("soft2_step")
        x1res_ready, out_stored = sem("x1res_ready"), sem("out_stored")

        def at(b, n, k):
            return b * n + k

        def wait(eng, s, b, n, k):
            v = at(b, n, k)
            if not isinstance(v, int) or v > 0:
                eng.wait_ge(s, v)

        def a_free(pe, b, j):
            wait(pe, free_a[j % 4], b, USES_A, j // 4)

        def a_full(eng, b, j):
            wait(eng, full_a[j % 4], b, USES_A, j // 4 + 1)

        def a_full_before(eng, b, j):
            wait(eng, full_a[j % 4], b, USES_A, j // 4 + 1 - USES_A)

        def a_drained(eng, b, *jobs):
            for j in jobs:
                wait(eng, free_a[j % 4], b, USES_A, j // 4 + 1)

        def b_drained(eng, b, *jobs):
            for j in jobs:
                wait(eng, free_b[j % 4], b, USES_B, j // 4 + 1)

        def b_free(pe, b, j):
            wait(pe, free_b[j % 4], b, USES_B, j // 4)

        def b_full(eng, b, j):
            wait(eng, full_b[j % 4], b, USES_B, j // 4 + 1)

        def bank_a(j):
            return bank[j % 4]

        def bank_b(j):
            return bank[4 + j % 4]

        S_K0, S_V0, S_CA, S_WK2, S_V2W, S_K1, S_V1 = offsets([6, 5, 2, 2, 2, 6, 5])
        SETUP = S_V1 + 5
        HALVES = [(g, half) for g in range(3) for half in range(2)]

        def setup_bank(job):
            return bank[4 + job % 4]

        TILE_GROUP0 = [(g, tile) for g in range(3) for tile in range(TILES0[g])]
        TILE_GROUP1 = [(g, tile) for g in range(3) for tile in range(TILES1[g])]

        def schedule(eng, body):
            body(0, True, False, False, True)
            body(1, True, True, False, True)
            with eng.Fori(2, B - 1) as b:
                body(b, True, True, True, True)
            body(B - 1, True, True, True, False)
            body(B, False, True, True, False)
            body(B + 1, False, False, True, False)

        block = es.enter_context(nc.Block())

        @block.sync
        def _(sp):
            def load_xt(b):
                sp.dma_start(xt[:, :, :], t["xt"][b]).then_inc(xt_in, 16)

            def load_xres(b):
                sp.dma_start(xres[:, :, :], t["xt"][b]).then_inc(xres_in, 16)

            def load_xkeys(b):
                sp.dma_start(xkeys[:, :, :, 0:D0].rearrange("p k h d -> p (k h) d"), t["x"][b].rearrange("p (a d) -> p a d", d=D0))\
                    .then_inc(xkeys_in, 16)

            def load_v2w(b):
                sp.dma_start(wo0[96:128, 2, :], v2w_d[b, :, :]).then_inc(v2w_in, 16)

            def load_wk2(b):
                sp.dma_start(wk2b[:, :, :], wk2_d[b, :, :, :]).then_inc(wk2b_in, 16)

            def load_v(layer, b):
                src, dst, loads, ho, to, keys, done = (
                    (v0_d, v0c, LOADS0, HO0, TO0, KEYS0, v0c_in), (v1_d, v1c, LOADS1, HO1, TO1, KEYS1, v1c_in))[layer]
                rows_of = src[b].rearrange("h k d -> (h k) d")
                for rows, g, groups, tile, tiles in loads:
                    o = ho[g] * keys + tile * 128
                    if groups > 1:
                        step = (ho[g + 1] - ho[g]) * keys
                        part = bass.AP(rows_of.tensor, rows_of.offset + o * rows_of.ap[0][0],
                                       [[rows_of.ap[0][0], rows], [step * rows_of.ap[0][0], groups], rows_of.ap[1]])
                        to_step = to[g + 1] - to[g]
                        a = to[g] + tile
                        sp.dma_start(dst[0:rows, a:a + to_step * (groups - 1) + 1:to_step, :], part).then_inc(done, 16)
                    else:
                        part = rows_of[o:o + rows * tiles, :].rearrange("(a p) d -> p a d", p=rows)
                        sp.dma_start(dst[0:rows, to[g] + tile:to[g] + tile + tiles, :], part).then_inc(done, 16)

            sp.dma_start(enc[:, :, :, :].rearrange("p j b k -> p j (b k)"), t["enc"].rearrange("(j p) n -> p j n", p=CK)).then_inc(kv0_in, 16)
            for w, name, done in ((wk0, "wk0", kv0_in), (wv0, "wv0", kv0_in)):
                sp.dma_start(w, t[name].rearrange("(j p) n -> p j n", p=CK)).then_inc(done, 16)
            sp.dma_start(wide[:, :, :], t["wide"]).then_inc(wide_in, 16)
            load_xt(0)
            sp.dma_start(ca_whole, t["ca"]).then_inc(ca_in, 16)
            sp.dma_start(small[:, :], t["small"]).then_inc(small_in, 16)
            for part, name in zip(sel_d, ("sel0", "sel1")):
                sp.dma_start(part, t[name]).then_inc(sel_copied, 16)
            for w, name, done in ((wkca, "wkca", kvca_in), (wvca, "wvca", kvca_in), (wk1, "wk1", kv1_in), (wv1, "wv1", kv1_in)):
                sp.dma_start(w, t[name].rearrange("(j p) n -> p j n", p=CK)).then_inc(done, 16)
            sp.wait_ge(sel_copied, 32)
            for dst, src in zip((sel0, sel1), sel_d):
                sp.dma_start(dst[:, :, :].rearrange("p a r -> p (a r)").bitcast(f32), src).then_inc(sel_ready, 16)
            sp.dma_start(wq0t, t["wq0t"]).then_inc(wq0t_in, 16)
            sp.dma_start(wo0[:, :, :], t["wo0"]).then_inc(wo0_in, 16)
            sp.dma_start(v0[:, :, :].rearrange("p a c -> p (a c)"), t["vone0"]).then_inc(vones_in, 16)
            sp.dma_start(v1[:, :, :].rearrange("p a c -> p (a c)"), t["vone1"]).then_inc(vones_in, 16)
            sp.wait_ge(init_dve, 1)
            load_xkeys(0)
            sp.dma_start(expand[:, :, :].rearrange("p a q -> p (a q)"), t["expand"]).then_inc(expand_in, 16)
            load_xres(0)

            def store_v(stage, dst, keys, first_job, done):
                for tile, row, n, b, k in v_pieces(keys):
                    sp.wait_ge(setup_free, first_job + tile + 1)
                    sp.dma_start(dst[b, :, k:k + n, :].rearrange("h k d -> k h d"),
                                 stage[row:row + n, tile, :].rearrange("k (h d) -> k h d", d=dst.shape[3])).then_inc(done, 16)
                sp.wait_ge(done, 16 * len(v_pieces(keys)))

            store_v(v0stage, v0_d, KEYS0, S_V0, v0_stored)
            load_v(0, 0)

            def body(b, do_a, do_b, do_c, more_a):
                if do_a:
                    a_full(sp, b, A_Q2G)
                    if more_a:
                        load_xt(b + 1)
                    wait(sp, mtc_ready, b, 1, 1)
                    sp.dma_start(mtc_d, mtc[:, :].bitcast(f32)).then_inc(mtc_st, 16)
                    wait(sp, mtc_st, b, 16, 16)
                    sp.dma_start(cast[96:97, :].bitcast(f32), mtc_d.rearrange("j c -> (j c)").unsqueeze(0)).then_inc(mtc_placed, 16)
                if do_c:
                    b_drained(sp, b - 2, B_O, B_O + 1)
                    sp.dma_start(t["out"][b - 2], outs[:, :, :]).then_inc(out_stored, 16)
                if do_a:
                    if more_a:
                        wait(sp, v0_ready, b, 1, 1)
                        load_v(0, b + 1)
                    if isinstance(b, int) and b == 0:
                        sp.wait_ge(setup_free, S_V2W + 2)
                        for p in range(PAIRS):
                            sp.dma_start(wk2_d[:, :, p, :].rearrange("b r n -> r b n"), wk2[:, p, :].rearrange("r (b n) -> r b n", b=B))\
                                .then_inc(wk2_stored, 16)
                        sp.dma_start(v2w_d.rearrange("(j b) r n -> (b r) j n", j=2), v2w).then_inc(v2w_stored, 16)
                    a_drained(sp, b, A_CU, A_CU + 1)
                    for odd in range(2):
                        sp.dma_start(denc_d[odd], uc[64 * odd + D0:64 * odd + D0 + 1, :, :]).then_inc(denc_st, 16)
                    wait(sp, denc_st, b, 32, 32)
                    sp.dma_start(denc[:, :], denc_d.rearrange("o p c -> (o p c)").rearrange("(r n) -> r n", r=128)).then_inc(denc_in, 16)
                    if isinstance(b, int) and b == 0:
                        sp.wait_ge(wk2_stored, 16 * PAIRS)
                        load_wk2(0)
                        sp.wait_ge(v2w_stored, 16)
                        load_v2w(0)
                    if more_a:
                        load_xkeys(b + 1)
                    wait(sp, recc_ready, b, 1, 1)
                    sp.dma_start(rc_d.rearrange("o p c -> (o p c)").rearrange("(r n) -> r n", r=128), recc[:, :]).then_inc(recc_st, 16)
                    wait(sp, recc_st, b, 16, 16)
                    for odd in range(2):
                        sp.dma_start(rbc[64 * odd:64 * odd + D0, :, :],
                                     rc_d[odd].unsqueeze(0).to_broadcast([D0, PAIRS, CAD])).then_inc(rbc_in, 16)
                    a_drained(sp, b, A_U + 2)
                    sp.dma_start(den0_d[0:6, :].rearrange("(g h) q -> h g q", g=2), u0[120:123, 0:2, :]).then_inc(den0_st, 16)
                    sp.dma_start(den0_d[6:8, :], u0[G0[2]:G0[2] + HG0[2], 2, :]).then_inc(den0_st, 16)
                    wait(sp, den0_st, b, 32, 32)
                    sp.dma_start(den0[:, :], den0_d.rearrange("h q -> (h q)").rearrange("(r n) -> r n", r=128)).then_inc(den0_in, 16)
                    wait(sp, rec0_ready, b, 1, 1)
                    sp.dma_start(r0_d.rearrange("h q -> (h q)").rearrange("(r n) -> r n", r=128), rec0[:, :]).then_inc(rec0_st, 16)
                    wait(sp, rec0_st, b, 16, 16)
                    for g in range(3):
                        sp.dma_start(rb0[0:G0[g], g, :], r0_d[HO0[g]:HO0[g] + HG0[g], :].unsqueeze(1)
                                     .to_broadcast([HG0[g], D0, SQ])).then_inc(rb0_in, 16)
                    if isinstance(b, int) and b == 0:
                        store_v(v1stage, v1_d, KEYS1, S_V1, v1_stored)
                    wait(sp, v1_ready, b, 1, 0)
                    load_v(1, b)
                if do_b:
                    b_drained(sp, b - 1, B_U + 2)
                    sp.dma_start(den1_d[0:14, :].rearrange("(g h) q -> h g q", g=2), u1[112:119, 0:2, :]).then_inc(den1_st, 16)
                    sp.dma_start(den1_d[14:20, :], u1[96:102, 2, :]).then_inc(den1_st, 16)
                    wait(sp, den1_st, b - 1, 32, 32)
                    sp.dma_start(den1[:, :], den1_d.rearrange("h q -> (h q)").rearrange("(r n) -> r n", r=128)).then_inc(den1_in, 16)
                    wait(sp, rec1_ready, b - 1, 1, 1)
                    sp.dma_start(r1_d.rearrange("h q -> (h q)").rearrange("(r n) -> r n", r=128), rec1[:, :]).then_inc(rec1_st, 16)
                    wait(sp, rec1_st, b - 1, 16, 16)
                    for g in range(3):
                        sp.dma_start(rb1[0:XG[g], g, :], r1_d[HO1[g]:HO1[g] + HG1[g], :].unsqueeze(1)
                                     .to_broadcast([HG1[g], D1, SQ])).then_inc(rb1_in, 16)
                if do_a and more_a:
                    a_drained(sp, b, A_O, A_O + 1, A_O + 2)
                    load_xres(b + 1)
                    load_v2w(b + 1)
                    load_wk2(b + 1)

            schedule(sp, body)
            sp.wait_ge(out_stored, 16 * B)

        @block.tensor
        def _(pe):
            mm, tr = nc.tensor.matmul, nc.tensor.transpose

            def setup_free_bank(job):
                if job >= 4:
                    pe.wait_ge(setup_free, job - 3)
                return setup_bank(job)

            def setup_k(w, keys, rows, offs, job):
                for g, half in HALVES:
                    ps = setup_free_bank(job)
                    for j in range(2):
                        last = mm(ps[0:rows[g], 0:4 * keys], w[:, j, offs[g]:offs[g] + rows[g]],
                                  enc[:, j, 4 * half:4 * half + 4, 0:keys], start=j == 0, stop=j == 1)
                    last.then_inc(setup_full, 1)
                    job += 1

            def setup_v(w, job):
                flat = enc[:, :, :, :].rearrange("p j b k -> p j (b k)")
                for o, n in VT:
                    ps = setup_free_bank(job)
                    for j in range(2):
                        last = mm(ps[0:n, 0:H], flat[:, j, o:o + n], w[:, j, :], start=j == 0, stop=j == 1)
                    last.then_inc(setup_full, 1)
                    job += 1

            def setup_ca():
                pe.wait_ge(kvca_in, 32)
                for job, w in ((S_CA, wkca), (S_CA + 1, wvca)):
                    ps = setup_free_bank(job)
                    for g in range(3):
                        for j in range(2):
                            last = mm(ps[0:G0[g], g * B * T:(g + 1) * B * T], w[:, j, GO0[g]:GO0[g] + G0[g]],
                                      enc[:, j, :, KEYS0:CTX], start=j == 0, stop=j == 1)
                    last.then_inc(setup_full, 1)

            def setup_ca_products():
                pe.wait_ge(kv2_masked, 6)
                pe.wait_ge(wq0t_in, 16)
                for half in range(PAIRS // 2):
                    ps = setup_free_bank(S_WK2 + half)
                    for e in range(2):
                        p = 2 * half + e
                        for g in range(3):
                            last = mm(ps[:, e * B * HT:(e + 1) * B * HT], wq0t[0:G0[g], g, p * 128:(p + 1) * 128],
                                      k2bd[0:G0[g], g, :], start=g == 0, stop=g == 2)
                    last.then_inc(setup_full, 1)
                pe.wait_ge(wo0_in, 16)
                for half in range(2):
                    ps = setup_free_bank(S_V2W + half)
                    for g in range(3):
                        last = mm(ps[:, 0:H], v2bd[0:G0[g], g, 128 * half:128 * (half + 1)], wo0[0:G0[g], g, :],
                                  start=g == 0, stop=g == 2)
                    last.then_inc(setup_full, 1)

            pe.wait_ge(kv0_in, 48)
            setup_k(wk0, KEYS0, G0, GO0, S_K0)
            setup_v(wv0, S_V0)
            pe.wait_ge(wide_in, 16)

            def body(b, do_a, do_b, do_c, more_a):
                if do_a:
                    wait(pe, xt_in, b, 16, 16)
                    a_free(pe, b, A_Q01)
                    for g in range(2):
                        for k in range(3):
                            last = mm(bank_a(A_Q01)[0:G0[g], g * SQ:(g + 1) * SQ], wq0[0:XG[k], k, GO0[g]:GO0[g] + G0[g]],
                                      xt[0:XG[k], k, :], start=k == 0, stop=k == 2)
                    last.then_inc(full_a[A_Q01 % 4], 1)
                    a_free(pe, b, A_Q2G)
                    for k in range(3):
                        mm(bank_a(A_Q2G)[0:G0[2], 0:SQ], wq0[0:XG[k], k, GO0[2]:H], xt[0:XG[k], k, :], start=k == 0, stop=k == 2)
                    for k in range(3):
                        last = mm(bank_a(A_Q2G)[0:3 * HT, SQ:2 * SQ], wca[0:XG[k], k, :], xt[0:XG[k], k, :], start=k == 0, stop=k == 2)
                    last.then_inc(full_a[A_Q2G % 4], 1)
                if do_a:
                    wait(pe, cast_ready, b, 1, 1)
                    a_drained(pe, b, A_Q2G)
                    for i in range(NC // 2):
                        a_free(pe, b, A_CS + i)
                        for e in range(2):
                            c = (2 * i + e) * 128
                            last = mm(bank_a(A_CS + i)[:, e * SQ:(e + 1) * SQ], cast[0:96, c:c + 128], gst[0:96, :], start=True, stop=True)
                        last.then_inc(full_a[(A_CS + i) % 4], 1)
                    wait(pe, q0hi_ready, b, 1, 1)
                    if isinstance(b, int) and b == 0:
                        pe.wait_ge(init_pool, 1)
                        pe.wait_ge(init_dve, 1)
                        pe.wait_ge(small_in, 16)
                        pe.wait_ge(sel_ready, 32)
                    wait(pe, k0_ready, b, 1, 1)
                    for i in range(3):
                        a_free(pe, b, A_SM + i)
                        for q, g in (((i, 0), (i, 1)) if i < 2 else ((0, 2), (1, 2))):
                            cols = (HG0[g] * KEYS0 + 1) // 2 * 2
                            c = (220 * g) if i < 2 else 146 * q
                            last = mm(bank_a(A_SM + i)[:, c:c + cols], q0hi[:, g, q * 128:(q + 1) * 128],
                                      k0hi[:, 256 * g:256 * g + cols], start=True, stop=True)
                        last.then_inc(full_a[(A_SM + i) % 4], 1)
                    a_drained(pe, b, A_SM, A_SM + 1, A_SM + 2)
                    a_drained(pe, b, A_CS + 2, A_CS + 3, A_CS + 4, A_CS + 5)
                    a_free(pe, b, A_M)
                    for q in range(QT):
                        tr(bank_a(A_M)[0:HEADS0, q * 128:(q + 1) * 128], negm0[:, q, :], ident[:, :])
                    tr(bank_a(A_M)[0:NC, SQ:SQ + 128], negmc[:, :], ident[:, :]).then_inc(full_a[A_M % 4], 1)
                if isinstance(b, int) and b == 0:
                    setup_ca()
                if do_c:
                    wait(pe, at1_ready, b - 2, 2, 2)
                    for i, ms in enumerate(((0, 1), (2,))):
                        b_free(pe, b - 2, B_O + i)
                        for e, m in enumerate(ms):
                            for g in range(3):
                                last = mm(bank_b(B_O + i)[0:XG[m], e * SQ:(e + 1) * SQ], wo1[0:XG[g], g, XO[m]:XO[m] + XG[m]],
                                          at1[0:XG[g], g, :], start=g == 0, stop=g == 2)
                        last.then_inc(full_b[(B_O + i) % 4], 1)
                if do_b:
                    a_drained(pe, b - 1, A_O, A_O + 1, A_O + 2)
                    if isinstance(b, int) and b == 1:
                        pe.wait_ge(setup_free, SETUP)
                    for i, ms in enumerate(((0, 1), (2,))):
                        b_free(pe, b - 1, B_Q + i)
                        for e, m in enumerate(ms):
                            for g in range(3):
                                last = mm(bank_b(B_Q + i)[0:XG[m], e * SQ:(e + 1) * SQ], wq1[0:XG[g], g, XO[m]:XO[m] + XG[m]],
                                          x1[0:XG[g], g, :], start=g == 0, stop=g == 2)
                        last.then_inc(full_b[(B_Q + i) % 4], 1)
                if do_a:
                    wait(pe, mtc_placed, b, 16, 16)
                    for c in range(3):
                        for k in range(QT):
                            job = A_CT + 2 * c + k
                            a_free(pe, b, job)
                            mm(bank_a(job)[:, :], gst[:, k * 128:(k + 1) * 128], cast[:, c * 512:(c + 1) * 512], start=True, stop=True)\
                                .then_inc(full_a[job % 4], 1)
                    wait(pe, xkeys_in, b, 16, 16)
                    for i in range(2):
                        a_drained(pe, b, *(range(A_CT, A_CT + 4), range(A_CT + 4, A_CT + 6))[i])
                        a_free(pe, b, A_CU + i)
                        for e in range(2):
                            for k in range(QT):
                                for odd in range(2):
                                    h = 4 * i + 2 * e + odd
                                    last = mm(bank_a(A_CU + i)[64 * odd:64 * odd + 64, e * CAD:(e + 1) * CAD], xkeys[:, k, h, :],
                                              pc[:, k, h * CAD:(h + 1) * CAD], start=k == 0, stop=k == QT - 1)
                        last.then_inc(full_a[(A_CU + i) % 4], 1)
                if isinstance(b, int) and b == 0:
                    setup_ca_products()
                    pe.wait_ge(kv1_in, 32)
                    setup_k(wk1, KEYS1, XG, XO, S_K1)
                if do_b:
                    wait(pe, q1hi_ready, b - 1, 2, 2)
                    wait(pe, k1_ready, b - 1, 1, 1)
                    for q in range(QT):
                        for i, parts in enumerate((((0, 0, 308, 0),), ((0, 308, 232, 0), (1, 308, 232, 232)), ((1, 0, 308, 0),), ((2, 0, 462, 0),))):
                            job = B_SM + 4 * q + i
                            b_free(pe, b - 1, job)
                            for g, k, cols, c in parts:
                                last = mm(bank_b(job)[:, c:c + cols], q1hi[0:XG[g], g, q * 128:(q + 1) * 128],
                                          k1hi[0:XG[g], 128 * TO1[g] + k:128 * TO1[g] + k + cols], start=True, stop=True)
                            last.then_inc(full_b[job % 4], 1)
                if do_a:
                    a_drained(pe, b, A_Q01, A_Q2G)
                    a_drained(pe, b, A_M)
                    for i in range(3):
                        a_free(pe, b, A_ST + i)
                        for e in range(2):
                            tile = 2 * i + e
                            g = TILE_GROUP0[tile][0]
                            ps = bank_a(A_ST + i)[:, e * SQ:(e + 1) * SQ]
                            mm(ps, k0[:, tile * 128:(tile + 1) * 128], q0[:, g, :], start=True, stop=False)
                            last = mm(ps, sel0[:, tile, :], mt0[:, :], start=False, stop=True)
                        last.then_inc(full_a[(A_ST + i) % 4], 1)
                    wait(pe, v0_ready, b, 1, 1)
                    for g in range(3):
                        a_drained(pe, b, A_ST + g)
                        a_free(pe, b, A_U + g)
                        rows = G0[g] + HG0[g]
                        for tile in range(2):
                            last = mm(bank_a(A_U + g)[0:rows, 0:SQ], v0[:, 2 * g + tile, 0:rows], p0[:, 2 * g + tile, :],
                                      start=tile == 0, stop=tile == 1)
                        last.then_inc(full_a[(A_U + g) % 4], 1)
                if isinstance(b, int) and b == 0:
                    setup_v(wv1, S_V1)
                if do_b:
                    b_drained(pe, b - 1, *range(B_SM + 4, B_SM + 8))
                    for q in range(QT):
                        b_free(pe, b - 1, B_M + q)
                        tr(bank_b(B_M + q)[0:HEADS1, 0:128], negm1[:, q, :], ident[:, :]).then_inc(full_b[(B_M + q) % 4], 1)
                    b_drained(pe, b - 1, B_Q, B_Q + 1)
                    b_drained(pe, b - 1, B_M, B_M + 1)
                    for i in range(T1 // 2):
                        b_free(pe, b - 1, B_ST + i)
                        for e in range(2):
                            tile = 2 * i + e
                            g = TILE_GROUP1[tile][0]
                            ps = bank_b(B_ST + i)[:, e * SQ:(e + 1) * SQ]
                            mm(ps, k1[0:XG[g], tile * 128:(tile + 1) * 128], q1[0:XG[g], g, :], start=True, stop=False)
                            last = mm(ps, sel1[:, tile, :], mt1[:, :], start=False, stop=True)
                        last.then_inc(full_b[(B_ST + i) % 4], 1)
                if do_a:
                    wait(pe, hsc_ready, b, 1, 1)
                    wait(pe, wk2b_in, b, 16, 16)
                    a_free(pe, b, A_S2)
                    for p in range(PAIRS):
                        last = mm(bank_a(A_S2)[0:HT, 0:CAD], wk2b[:, p, :], hsc[:, p, :], start=p == 0, stop=p == PAIRS - 1)
                    last.then_inc(full_a[A_S2 % 4], 1)
                    a_drained(pe, b, A_S2)
                    a_free(pe, b, A_TR)
                    for c in range(2):
                        last = mm(bank_a(A_TR)[0:96, c * HT:(c + 1) * HT], s2t[:, c * 96:(c + 1) * 96], ident[0:HT, 0:HT], start=True, stop=True)
                    last.then_inc(full_a[A_TR % 4], 1)
                if do_b:
                    wait(pe, v1_ready, b - 1, 1, 1)
                    for g in range(3):
                        b_drained(pe, b - 1, *range(B_ST + TO1[g] // 2, B_ST + (TO1[g] + TILES1[g] + 1) // 2))
                        b_free(pe, b - 1, B_U + g)
                        rows = HG1[g] * (D1 + 1)
                        for tile in range(TILES1[g]):
                            last = mm(bank_b(B_U + g)[0:rows, 0:SQ], v1[:, TO1[g] + tile, 0:rows], p1[:, TO1[g] + tile, :],
                                      start=tile == 0, stop=tile == TILES1[g] - 1)
                        last.then_inc(full_b[(B_U + g) % 4], 1)
                if do_a:
                    wait(pe, p2_ready, b, 1, 1)
                    if isinstance(b, int) and b == 0:
                        pe.wait_ge(expand_in, 16)
                    a_free(pe, b, A_EX)
                    for c in range(2):
                        last = mm(bank_a(A_EX)[96:128, 0:SQ], p2[:, c * HEADS0:(c + 1) * HEADS0, :].rearrange("p h t -> p (h t)"),
                                  expand[:, c, :], start=c == 0, stop=c == 1)
                    last.then_inc(full_a[A_EX % 4], 1)
                    wait(pe, at0_ready, b, 2, 2)
                    a_drained(pe, b, A_EX)
                    wait(pe, v2w_in, b, 16, 16)
                    for m in range(3):
                        a_free(pe, b, A_O + m)
                        for g in range(3):
                            rows = (120, 120, 128)[g]
                            last = mm(bank_a(A_O + m)[0:XG[m], 0:SQ], wo0[0:rows, g, XO[m]:XO[m] + XG[m]],
                                      at0[0:rows, g, :], start=g == 0, stop=g == 2)
                        last.then_inc(full_a[(A_O + m) % 4], 1)

            schedule(pe, body)

        @block.scalar
        def _(act):
            def copy(out, in_):
                return nc.scalar.activation(out, in_, ACT.Copy)

            def setup_copy(job, *pairs):
                act.wait_ge(setup_full, job + 1)
                for dst, src in pairs:
                    last = copy(dst, src)
                last.then_inc(setup_free, 1)

            def setup_k(kt, keys, rows, job):
                for g, half in HALVES:
                    setup_copy(job, (kt[0:rows[g], g, 4 * half:4 * half + 4, :].rearrange("p b k -> p (b k)"),
                                     setup_bank(job)[0:rows[g], 0:4 * keys]))
                    job += 1

            def setup_v(stage, job):
                for tile, (_, n) in enumerate(VT):
                    setup_copy(job + tile, (stage[0:n, tile, :], setup_bank(job + tile)[0:n, 0:H]))

            setup_k(kt0, KEYS0, G0, S_K0)
            setup_v(v0stage, S_V0)

            def body(b, do_a, do_b, do_c, more_a):
                if do_a:
                    a_full(act, b, A_Q01)
                    copy(q0[:, 0:2, :], bank_a(A_Q01)[0:120, :].rearrange("p (g q) -> p g q", q=SQ))\
                        .then_inc(free_a[A_Q01 % 4], 1)
                if isinstance(b, int) and b == 0:
                    for job, kt in ((S_CA, k2t), (S_CA + 1, v2t)):
                        setup_copy(job, *((kt[0:G0[g], g, :], setup_bank(job)[0:G0[g], g * B * T:(g + 1) * B * T]) for g in range(3)))
                    act.wait_ge(v0_stored, 16 * len(v_pieces(KEYS0)))
                if do_b:
                    for i in range(2):
                        b_full(act, b - 1, B_Q + i)
                        dst, src = ((q1[:, 0:2, :], bank_b(B_Q)[0:112, :].rearrange("p (g q) -> p g q", q=SQ)),
                                    (q1[0:96, 2, :], bank_b(B_Q + 1)[0:96, 0:SQ]))[i]
                        copy(dst, src).then_inc(free_b[(B_Q + i) % 4], 1)
                if do_a:
                    for c in range(3):
                        for k in range(QT):
                            job = A_CT + 2 * c + k
                            a_full(act, b, job)
                            nc.scalar.activation(pc[:, k, c * 512:(c + 1) * 512], bank_a(job)[:, :], ACT.Exp, scale=SCALE0)\
                                .then_inc(free_a[job % 4], 1)
                    wait(act, hsc_ready, b, 1, 0)
                    for i in range(2):
                        a_full(act, b, A_CU + i)
                        copy(uc[:, 2 * i:2 * i + 2, :].rearrange("p e c -> p (e c)"), bank_a(A_CU + i)[:, 0:2 * CAD])\
                            .then_inc(free_a[(A_CU + i) % 4], 1)
                    if isinstance(b, int) and b == 0:
                        act.wait_ge(ca_split, 2)
                        for half in range(2):
                            setup_copy(S_WK2 + half, (wk2[:, 2 * half:2 * half + 2, :].rearrange("p a n -> p (a n)"), setup_bank(S_WK2 + half)[:, :]))
                        for half in range(2):
                            setup_copy(S_V2W + half, (v2w[:, half, :], setup_bank(S_V2W + half)[:, 0:H]))
                        setup_k(kt1, KEYS1, XG, S_K1)
                    for i in range(3):
                        a_full(act, b, A_ST + i)
                        nc.scalar.activation(p0[:, 2 * i:2 * i + 2, :].rearrange("p a q -> p (a q)"), bank_a(A_ST + i)[:, :], ACT.Exp, scale=SCALE0)\
                            .then_inc(free_a[(A_ST + i) % 4], 1)
                    wait(act, at0_ready, b, 2, 0)
                    for g in range(3):
                        a_full(act, b, A_U + g)
                        rows = G0[g] + HG0[g]
                        copy(u0[0:rows, g, :], bank_a(A_U + g)[0:rows, 0:SQ]).then_inc(free_a[(A_U + g) % 4], 1)
                if isinstance(b, int) and b == 0:
                    setup_v(v1stage, S_V1)
                if isinstance(b, int) and b == 1:
                    act.wait_ge(wk2_stored, 16 * PAIRS)
                    act.wait_ge(v2w_stored, 16)
                    act.wait_ge(v1_stored, 16 * len(v_pieces(KEYS1)))
                if do_b:
                    for i in range(T1 // 2):
                        b_full(act, b - 1, B_ST + i)
                        nc.scalar.activation(p1[:, 2 * i:2 * i + 2, :].rearrange("p a q -> p (a q)"), bank_b(B_ST + i)[:, :], ACT.Exp, scale=SCALE1)\
                            .then_inc(free_b[(B_ST + i) % 4], 1)
                if do_a:
                    a_full(act, b, A_S2)
                    copy(s2t[:, :], bank_a(A_S2)[0:HT, 0:CAD]).then_inc(free_a[A_S2 % 4], 1)
                    a_drained(act, b, A_TR)
                    nc.scalar.activation(e2[:, :, :], sh2[:, :, :], ACT.Exp, scale=SCALE0).then_inc(e2_ready, 1)
                if do_b:
                    wait(act, at1_ready, b - 1, 2, 0)
                    for g in range(3):
                        b_full(act, b - 1, B_U + g)
                        rows = HG1[g] * (D1 + 1)
                        copy(u1[0:rows, g, :], bank_b(B_U + g)[0:rows, 0:SQ]).then_inc(free_b[(B_U + g) % 4], 1)

            schedule(act, body)

        @block.vector
        def _(dve):
            tt, cp = nc.vector.tensor_tensor, nc.vector.tensor_copy
            nc.vector.memset(xkeys[:, :, :, :].rearrange("p k h d -> p (k h d)"), 0.0).then_inc(dve_init_step, 1)
            nc.vector.memset(q0[:, 2, :], 0.0)
            nc.vector.memset(q0hi[:, 2, :].bitcast(f32), 0.0)
            nc.vector.memset(mt0[:, :].bitcast(f32), 0.0)
            nc.vector.memset(mt1[:, :].bitcast(f32), 0.0)
            nc.vector.memset(at0[:, 2, :], 0.0)
            nc.vector.memset(outs[96:112, 2, :], 0.0)
            nc.vector.memset(rbc[:, :, :].rearrange("p a c -> p (a c)"), 1.0)
            nc.vector.memset(gst[96:97, :].bitcast(f32), 1.0)
            nc.vector.memset(v0c[:, :, :], 0.0)
            nc.vector.memset(v1c[:, :, :], 0.0)
            dve.wait_ge(dve_init_step, 1)
            nc.vector.memset(xkeys[:, :, :, D0:D0 + 1].rearrange("p k h d -> p (k h) d"), 1.0).then_inc(init_dve, 1)
            dve.wait_ge(ca_in, 16)
            flat = ca[:, :, :].rearrange("p b c -> p (b c)")
            cp(flat, ca_whole).then_inc(ca_split, 1)
            dve.wait_ge(ca_split, 1)
            tt(flat[64:96, :], ca_whole[64:96, :], flat[64:96, :].bitcast(f32), ALU.subtract).then_inc(ca_split, 1)
            dve.wait_ge(small_in, 16)
            dve.wait_ge(wide_in, 16)

            def mask_kv2():
                dve.wait_ge(setup_free, S_CA + 2)
                for src, dst in ((k2t, k2bd), (v2t, v2bd)):
                    for g in range(3):
                        r = G0[g]
                        tt(dst[0:r, g, :].rearrange("p (b h t) -> p b h t", b=B, h=HEADS0),
                           src[0:r, g, :].rearrange("p (b t) -> p b t", t=T).unsqueeze(2).to_broadcast([r, B, HEADS0, T]),
                           head8[0:r, g, :].unsqueeze(1).unsqueeze(3).to_broadcast([r, B, HEADS0, T]), ALU.mult).then_inc(kv2_masked, 1)

            def body(b, do_a, do_b, do_c, more_a):
                if do_a:
                    a_full(dve, b, A_Q2G)
                    ps = bank_a(A_Q2G)
                    cp(q0[0:G0[2], 2, :], ps[0:G0[2], 0:SQ])
                    cp(gst[0:96, :], ps[0:96, SQ:2 * SQ]).then_inc(g_hi, 1)
                    wait(dve, g_hi, b, 1, 1)
                    tt(gst[32:64, :], ps[32:64, SQ:2 * SQ], gst[32:64, :].bitcast(f32), ALU.subtract)\
                        .then_inc(free_a[A_Q2G % 4], 1)
                    a_drained(dve, b, A_Q01)
                    cp(q0hi[:, :, :].rearrange("p g q -> p (g q)"), q0[:, :, :].rearrange("p g q -> p (g q)")).then_inc(q0hi_ready, 1)
                if do_a:
                    for i in range(NC // 2):
                        a_full(dve, b, A_CS + i)
                        nc.vector.tensor_reduce(out=negmc[:, 2 * i:2 * i + 2], in_=bank_a(A_CS + i)[:, :].rearrange("p (e k) -> p e k", e=2),
                                                axis=AX, op=ALU.max, negate=True).then_inc(free_a[(A_CS + i) % 4], 1)
                    for i in range(3):
                        a_full(dve, b, A_SM + i)
                        if i < 2:
                            dst = negm0[:, i, 0:6].rearrange("p (g h) -> p g h", g=2)
                            src = bank_a(A_SM + i)[:, 0:440].rearrange("p (g k) -> p g k", g=2)[:, :, 0:219]\
                                .rearrange("p g (h k) -> p g h k", k=KEYS0)
                        else:
                            dst = negm0[:, :, 6:8]
                            src = bank_a(A_SM + i)[:, 0:292].rearrange("p (q h k) -> p q h k", q=2, k=KEYS0)
                        nc.vector.tensor_reduce(out=dst, in_=src, axis=AX, op=ALU.max, negate=True)\
                            .then_inc(free_a[(A_SM + i) % 4], 1)
                    a_full(dve, b, A_M)
                    cp(mtc[:, :], bank_a(A_M)[0:NC, SQ:SQ + 128]).then_inc(mtc_ready, 1)
                    cp(mt0[0:HEADS0, :], bank_a(A_M)[0:HEADS0, 0:SQ]).then_inc(free_a[A_M % 4], 1)
                if isinstance(b, int) and b == 0:
                    mask_kv2()
                if do_c:
                    wait(dve, rb1_in, b - 2, 48, 48)
                    tt(at1[:, 0:2, :], u1[0:112, 0:2, :], rb1[:, 0:2, :], ALU.mult).then_inc(at1_ready, 1)
                    tt(at1[0:96, 2, :], u1[0:96, 2, :], rb1[0:96, 2, :], ALU.mult).then_inc(at1_ready, 1)
                if do_c:
                    wait(dve, out_stored, b - 2, 16, 0)
                    wait(dve, x1res_ready, b - 2, 1, 1)
                    for i, ms in enumerate(((0, 1), (2,))):
                        b_full(dve, b - 2, B_O + i)
                        for e, m in enumerate(ms):
                            r = XG[m]
                            last = tt(outs[0:r, m, :], bank_b(B_O + i)[0:r, e * SQ:(e + 1) * SQ], x1res[0:r, m, :], ALU.add)
                        last.then_inc(free_b[(B_O + i) % 4], 1)
                if do_b:
                    b_drained(dve, b - 1, B_Q, B_Q + 1)
                    cp(q1hi[:, 0:2, :], q1[:, 0:2, :]).then_inc(q1hi_ready, 1)
                    cp(q1hi[0:96, 2, :], q1[0:96, 2, :]).then_inc(q1hi_ready, 1)
                if do_b:
                    for q in range(QT):
                        for i in range(4):
                            job = B_SM + 4 * q + i
                            b_full(dve, b - 1, job)
                            ps = bank_b(job)
                            if i == 1:
                                dst = negm1[:, q, 0:14].rearrange("p (g h) -> p g h", g=2)[:, :, 4:7]
                                src = ps[:, 0:464].rearrange("p (g k) -> p g k", g=2)[:, :, 0:231].rearrange("p g (h k) -> p g h k", k=KEYS1)
                            else:
                                h, n = ((0, 4), None, (7, 4), (14, 6))[i]
                                dst = negm1[:, q, h:h + n]
                                src = ps[:, 0:n * KEYS1].rearrange("p (h k) -> p h k", k=KEYS1)
                            nc.vector.tensor_reduce(out=dst, in_=src, axis=AX, op=ALU.max, negate=True)\
                                .then_inc(free_b[job % 4], 1)
                if do_a:
                    wait(dve, denc_in, b, 16, 16)
                    nc.vector.reciprocal(recc[:, :], denc[:, :]).then_inc(recc_ready, 1)
                if do_b:
                    for q in range(QT):
                        b_full(dve, b - 1, B_M + q)
                        cp(mt1[0:HEADS1, q * 128:(q + 1) * 128], bank_b(B_M + q)[0:HEADS1, 0:128])\
                            .then_inc(free_b[(B_M + q) % 4], 1)
                if do_a:
                    wait(dve, rbc_in, b, 32, 32)
                    tt(hsc[:, :, :], uc[:, :, :], rbc[:, :, :], ALU.mult).then_inc(hsc_ready, 1)
                    wait(dve, den0_in, b, 16, 16)
                    nc.vector.reciprocal(rec0[:, :], den0[:, :]).then_inc(rec0_ready, 1)
                    a_full(dve, b, A_TR)
                    s2 = bank_a(A_TR)[0:96, 0:2 * HT].rearrange("p (h t) -> p h t", t=T)
                    nc.vector.reduce_max(mx2[:, :], s2, AX).then_inc(soft2, 1)
                    wait(dve, soft2, b, 3, 1)
                    tt(sh2[:, :, :], s2, mx2[:, :].unsqueeze(2).to_broadcast([96, 2 * HEADS0, T]), ALU.subtract)\
                        .then_inc(free_a[A_TR % 4], 1)
                    wait(dve, e2_ready, b, 1, 1)
                    nc.vector.reduce_sum(sum2[:, :], e2[:, :, :], AX).then_inc(soft2, 1)
                    wait(dve, soft2, b, 3, 2)
                    nc.vector.reciprocal(rc2[:, :], sum2[:, :]).then_inc(soft2, 1)
                    wait(dve, soft2, b, 3, 3)
                    tt(p2[:, :, :], e2[:, :, :], rc2[:, :].unsqueeze(2).to_broadcast([96, 2 * HEADS0, T]), ALU.mult).then_inc(p2_ready, 1)
                    wait(dve, rb0_in, b, 48, 48)
                    tt(at0[0:120, 0:2, :], u0[0:120, 0:2, :], rb0[:, 0:2, :], ALU.mult).then_inc(at0_ready, 1)
                    tt(at0[0:80, 2, :], u0[0:80, 2, :], rb0[0:80, 2, :], ALU.mult).then_inc(at0_ready, 1)
                    a_full(dve, b, A_EX)
                    cp(at0[96:128, 2, :], bank_a(A_EX)[96:128, 0:SQ]).then_inc(free_a[A_EX % 4], 1)
                if do_b:
                    wait(dve, den1_in, b - 1, 16, 16)
                    nc.vector.reciprocal(rec1[:, :], den1[:, :]).then_inc(rec1_ready, 1)
                if do_a:
                    wait(dve, xres_in, b, 16, 16)
                    wait(dve, x1res_ready, b, 1, 0)
                    for m in range(3):
                        a_full(dve, b, A_O + m)
                        r = XG[m]
                        nc.vector.scalar_tensor_tensor(
                            out=x1[0:r, m, :], in0=bank_a(A_O + m)[0:r, 0:SQ], scalar=bias0[0:r, m:m + 1],
                            in1=xres[0:r, m, :], op0=ALU.add, op1=ALU.add).then_inc(free_a[(A_O + m) % 4], 1)

            schedule(dve, body)

        @block.gpsimd
        def _(pool):
            for buf in (k0[:, :], k0hi[:, :].bitcast(f32), k1[:, :], k1hi[:, :].bitcast(f32)):
                last = nc.gpsimd.memset(buf, 0.0)
            last.then_inc(init_pool, 1)
            pool.wait_ge(init_pool, 1)
            pool.wait_ge(small_in, 16)
            pool.wait_ge(ca_split, 2)

            def build_cast(b):
                nc.gpsimd.tensor_tensor(cast[0:96, :].rearrange("p (h c) -> p h c", c=CAD),
                                        (ca[:, b, :] if isinstance(b, int) else ca[:, bass.ds(b, 1), :].rearrange("p o c -> p (o c)"))
                                        .bitcast(f32).unsqueeze(1).to_broadcast([96, HEADS0, CAD]),
                                        head96[0:96, :].unsqueeze(2).to_broadcast([96, HEADS0, CAD]), ALU.mult).then_inc(cast_ready, 1)

            def build_v(layer, b):
                vc, mask, v, hg, to, tiles, d, ready, loaded, count = (
                    (v0c, vhead0, v0, HG0, TO0, TILES0, D0, v0_ready, v0c_in, N_V0),
                    (v1c, vhead1, v1, HG1, TO1, TILES1, D1, v1_ready, v1c_in, N_V1))[layer]
                wait(pool, loaded, b, count, count)
                for g in range(3):
                    a, n, h = to[g], tiles[g], hg[g]
                    last = nc.gpsimd.tensor_tensor(
                        v[:, a:a + n, 0:h * d].rearrange("p a (h d) -> p a h d", d=d),
                        vc[:, a:a + n, :].unsqueeze(2).to_broadcast([128, n, h, d]),
                        mask[:, a:a + n, 0:h].unsqueeze(3).to_broadcast([128, n, h, d]), ALU.mult)
                last.then_inc(ready, 1)

            def build_k(layer, b):
                kt, mask, k, khi, hg, rows, to, keys, ready = (
                    (kt0, head0, k0, k0hi, HG0, G0, TO0, KEYS0, k0_ready), (kt1, head1, k1, k1hi, HG1, XG, TO1, KEYS1, k1_ready))[layer]
                for dst in (khi, k):
                    for g in range(3):
                        r, h, o = rows[g], hg[g], 128 * to[g]
                        last = nc.gpsimd.tensor_tensor(
                            dst[0:r, o:o + h * keys].rearrange("p (h k) -> p h k", k=keys),
                            kt[0:r, g, b, :].unsqueeze(1).to_broadcast([r, h, keys]),
                            mask[0:r, 0:h].unsqueeze(2).to_broadcast([r, h, keys]), ALU.mult)
                last.then_inc(ready, 1)

            build_cast(0)
            pool.wait_ge(setup_free, S_K0 + 6)
            build_k(0, 0)
            pool.wait_ge(vones_in, 32)
            build_v(0, 0)

            def body(b, do_a, do_b, do_c, more_a):
                if do_b:
                    if isinstance(b, int) and b == 1:
                        pool.wait_ge(setup_free, S_K1 + 6)
                    else:
                        b_full(pool, b - 2, B_ST + T1 // 2 - 1)
                    build_k(1, b - 1)
                    if not isinstance(b, int) or b > 1:
                        b_full(pool, b - 2, B_U + 2)
                    build_v(1, b - 1)
                    if do_c:
                        b_drained(pool, b - 2, B_O, B_O + 1)
                    a_drained(pool, b - 1, A_O, A_O + 1, A_O + 2)
                    for g in range(3):
                        r = XG[g]
                        last = nc.gpsimd.tensor_tensor(x1res[0:r, g, :], x1[0:r, g, :],
                                                       bias1[0:r, g:g + 1].to_broadcast([r, SQ]), ALU.add)
                    last.then_inc(x1res_ready, 1)
                if do_a and more_a:
                    a_full(pool, b, A_CT + 5)
                    build_cast(b + 1)
                    a_full(pool, b, A_ST + 2)
                    build_k(0, b + 1)
                    a_full(pool, b, A_U + 2)
                    build_v(0, b + 1)

            schedule(pool, body)


_OUT = (B, 112, 3, SQ)


def kernel(**inputs):
    import concourse.bacc as bacc
    from concourse.bass_utils import run_bass_kernel_spmd

    a = {k: np.asarray(v) for k, v in inputs.items()}
    x, ctx = a["x"], a["ctx_768"]
    wca = np.zeros((H, HEADS0, T), np.float32)
    wq0t = np.zeros((H, PAIRS, 2, 64), np.float32)
    for h in range(HEADS0):
        wca[h * D0:(h + 1) * D0, h, :] = a["L0_xattn_Wq_ca"].T[h * D0:(h + 1) * D0]
    wq0t[:, :, :, 0:D0] = a["L0_xattn_Wq"].T.reshape(H, PAIRS, 2, D0)
    wca = wca.reshape(H, HT)

    def groups(w, sizes, rows):
        out = np.zeros((rows, 3, w.shape[1]), np.float32)
        for g, o in enumerate(offsets(sizes)):
            out[0:sizes[g], g] = w[o:o + sizes[g]]
        return out

    wide = np.concatenate([a["L0_xattn_Wq"], wca, wca, wca, a["L1_xattn_Wq"], a["L1_xattn_Wo"],
                           a["L0_xattn_b_out"].reshape(H, 1), a["L1_xattn_bo"].reshape(H, 1)], axis=1)
    xt = np.zeros((B, 3 * 112, SQ), np.float32)
    xt[:, 0:H] = x.transpose(0, 2, 1)
    arrays = {
        "xt": xt.reshape(B, 3, 112, SQ).transpose(0, 2, 1, 3), "x": x.reshape(B, QT, 128, H).transpose(0, 2, 1, 3).reshape(B, 128, QT * H),
        "enc": ctx.transpose(2, 0, 1).reshape(CAD, B * CTX),
        "ca": np.broadcast_to(ctx[:, KEYS0:, :].transpose(1, 0, 2), (3, HEADS0, T, B, CAD)).reshape(3 * HT, B * CAD),
        "wk0": a["L0_xattn_Wk"], "wv0": a["L0_xattn_Wv"], "wkca": a["L0_xattn_Wk_ca"], "wvca": a["L0_xattn_Wv_ca"],
        "wk1": a["L1_xattn_Wk"], "wv1": a["L1_xattn_Wv"],
        "wide": groups(wide, XG, 112), "wo0": groups(a["L0_xattn_Wout"], G0, 128), "wq0t": groups(wq0t.reshape(H, PAIRS * 128), G0, 120),
        **constants(),
    }
    nc = bacc.Bacc("TRN2", target_bir_lowering=False, num_devices=1)
    f32 = mybir.dt.float32
    feed, t = {}, {}
    for name, v in arrays.items():
        feed["in_" + name] = np.ascontiguousarray(v)
        t[name] = nc.dram_tensor("in_" + name, v.shape, f32, kind="ExternalInput").ap()
    t["out"] = nc.dram_tensor("out_t", _OUT, f32, kind="ExternalOutput").ap()
    xattn_kernel(nc, t)
    r = run_bass_kernel_spmd(nc, [feed], core_ids=[0])
    out = np.asarray(r.results[0]["out_t"]).transpose(0, 3, 2, 1).reshape(B, SQ, 3 * 112)
    return np.ascontiguousarray(out[:, :, 0:H])
```

```python
import concourse.bass as bass
from concourse import mybir
from contextlib import ExitStack
import numpy as np

B, SQ, H = 8, 256, 320
CTX, CAD, T = 77, 192, 4
QT = SQ // 128
CK = CAD // 2
XG = [112, 112, 96]
HEADS0, D0, KEYS0 = 8, 40, CTX - T
HG0 = [3, 3, 2]
G0 = [h * D0 for h in HG0]
HEADS1, D1, KEYS1 = 20, 16, CTX
HG1 = [7, 7, 6]
TILES0 = [2, 2, 2]
TILES1 = [5, 5, 4]
T0, T1 = sum(TILES0), sum(TILES1)
V0C, V1C = 3 * D0 + 3, 7 * D1 + 7
CCOL = HEADS0 * CAD
NC = CCOL // 128
PAIRS = HEADS0 // 2
HT = HEADS0 * T
SCALE0, SCALE1 = float(D0) ** -0.5, float(D1) ** -0.5
JOBS_A, JOBS_B = 32, 24
USES_A, USES_B = JOBS_A // 4, JOBS_B // 4
A_Q01, A_Q2G, A_CS, A_SM, A_M, A_ST, A_CT, A_CU, A_U, A_S2, A_TR, A_EX, A_O = (
    0, 1, 2, 8, 11, 12, 15, 21, 23, 26, 27, 28, 29)
B_Q, B_U12, B_SM, B_M, B_ST, B_O, B_U0 = 0, 2, 4, 12, 14, 21, 23
LATE_B = (B_U12, B_U12 + 1, B_O, B_O + 1)


def pieces(heads, keys):
    out = []
    for h in range(heads):
        k = 0
        while k < keys:
            tile, row = divmod(h * keys + k, 128)
            n = min(keys - k, 128 - row)
            out.append((h, k, n, tile, row))
            k += n
    return out


def offsets(sizes):
    return [sum(sizes[:i]) for i in range(len(sizes))]


TO0, TO1, HO0, HO1, GO0, XO = (offsets(s) for s in (TILES0, TILES1, HG0, HG1, G0, XG))
VT = [(o, min(128, B * CTX - o)) for o in range(0, B * CTX, 128)]


def v_pieces(keys):
    out = []
    for tile, (o, n) in enumerate(VT):
        for b in range(B):
            lo, hi = max(o, b * CTX), min(o + n, b * CTX + keys)
            if lo < hi:
                out.append((tile, lo - o, hi - lo, b, lo - b * CTX))
    return out


def v_loads(hg, keys, tiles):
    full = [n * keys // 128 for n in hg]
    rest = [n * keys % 128 for n in hg]
    out = [(128, g, 1, 0, full[g]) for g in range(3) if full[g] > 1] or [(128, 0, 3, 0, 1)]
    return out + [(rest[0], 0, 2, full[0], 1), (rest[2], 2, 1, full[2], 1)]


LOADS0, LOADS1 = v_loads(HG0, KEYS0, TILES0), v_loads(HG1, KEYS1, TILES1)
N_V0, N_V1 = 16 * len(LOADS0), 16 * len(LOADS1)


SMALL = {"ident": 128, "head0": 3, "head1": 7, "head8": 3 * HEADS0, "head96": HEADS0, "vhead0": T0 * 3, "vhead1": T1 * 7}
WIDE = {"wq1": H, "b0": 1, "b1": 1}
CA_ROW = 96
SPLIT = {"wq0": H + CA_ROW - G0[2] + HT, "wo1": H}


def constants():
    c = {}
    c["ident"] = np.eye(128)
    head0 = np.zeros((128, 3))
    head1 = np.zeros((128, 7))
    head8 = np.zeros((128, 3, HEADS0))
    for r in range(120):
        head0[r, r // D0] = 1
    for r in range(112):
        head1[r, r // D1] = 1
    for g in range(3):
        for r in range(G0[g]):
            head8[r, g, HO0[g] + r // D0] = 1
    head96 = np.zeros((128, HEADS0))
    for i in range(3 * HT):
        head96[i, i % HT // T] = 1
    c["head0"], c["head1"], c["head8"], c["head96"] = head0, head1, head8.reshape(128, -1), head96
    for name, hg, to, ho, keys, tiles, cols, d in (("0", HG0, TO0, HO0, KEYS0, T0, V0C, D0), ("1", HG1, TO1, HO1, KEYS1, T1, V1C, D1)):
        sel = np.zeros((HEADS0 if name == "0" else hg[0], tiles, 128))
        v = np.zeros((128, tiles, cols))
        for g in range(3):
            for h, _, n, tile, row in pieces(hg[g], keys):
                sel[h + (ho[g] if name == "0" else 0), to[g] + tile, row:row + n] = 1
                v[row:row + n, to[g] + tile, hg[g] * d + h] = 1
        c["sel" + name], c["vone" + name] = sel.reshape(len(sel), -1), v.reshape(128, -1)
        mask = np.zeros((128, tiles, hg[0]))
        for g in range(3):
            for h, _, n, tile, row in pieces(hg[g], keys):
                mask[row:row + n, to[g] + tile, h] = 1
        c["vhead" + name] = mask.reshape(128, -1)
    expand = np.zeros((96, 2, SQ))
    for q, ch in enumerate(np.linspace(0, CAD - 1, SQ).astype(np.int64)):
        expand[ch % 96, ch // 96, q] = 1
    c["expand"] = expand.reshape(96, -1)
    spread = np.zeros((128, 2, 112))
    for i, heads in enumerate((HG1[0], HG1[2])):
        for r in range(heads * D1):
            spread[heads * D1 + r // D1, i, r] = 1
    c["spread1"] = spread.reshape(128, -1)
    c["small"] = np.concatenate([c.pop(n) for n in SMALL], axis=1)
    return {k: np.ascontiguousarray(v, dtype=np.float32) for k, v in c.items()}


def xattn_kernel(nc, t):
    f32, f32r = mybir.dt.float32, mybir.dt.float32r
    ALU, ACT, AX = mybir.AluOpType, mybir.ActivationFunctionType, mybir.AxisListType.X
    es = ExitStack()
    with es:
        def sb(name, shape, dt=f32):
            return es.enter_context(nc.sbuf_tensor(name, shape, dt))

        def sem(name):
            return es.enter_context(nc.semaphore(name))

        small = sb("small", [128, sum(SMALL.values())])
        o = offsets(list(SMALL.values()))
        ident, head0, head1, head8, head96, vhead0, vhead1 = (small[:, a:a + n] for a, n in zip(o, SMALL.values()))
        head8 = head8.rearrange("p (g h) -> p g h", g=3)
        vhead0, vhead1 = vhead0.rearrange("p (a h) -> p a h", h=3), vhead1.rearrange("p (a h) -> p a h", h=7)
        expand = sb("expand", [96, 2, SQ])
        spread1 = sb("spread1", [128, 2, 112])
        wide = sb("wide", [112, 3, sum(WIDE.values())])
        o = offsets(list(WIDE.values()))
        wq1, bias0, bias1 = (wide[:, :, a:a + n] for a, n in zip(o, WIDE.values()))
        whi = sb("whi", [112, 3, sum(SPLIT.values())], f32r)
        wlo = sb("wlo", [112, 3, sum(SPLIT.values())], f32r)
        o = offsets(list(SPLIT.values()))
        wq0, wo1 = ([w[:, :, a:a + n] for w in (whi, wlo)] for a, n in zip(o, SPLIT.values()))
        bias0, bias1 = (w.rearrange("p g o -> p (g o)") for w in (bias0, bias1))
        wo0 = sb("wo0", [128, 3, H])
        enc = sb("enc", [CK, 2, B, CTX])
        kt0hi = sb("kt0hi", [120, 3, B, KEYS0], f32r)
        kt0lo = sb("kt0lo", [120, 3, B, KEYS0])
        kt1hi = sb("kt1hi", [112, 3, B, KEYS1], f32r)
        kt1lo = sb("kt1lo", [112, 3, B, KEYS1])
        k2t = sb("k2t", [120, 3, B * T])
        v2t = sb("v2t", [120, 3, B * T])
        ca = sb("ca", [3 * HT, B, CAD], f32r)
        xt = sb("xt", [112, 3, SQ])
        xthi = sb("xthi", [112, 3, SQ], f32r)
        xtlo = sb("xtlo", [112, 3, SQ], f32r)
        xres = sb("xres", [112, 3, SQ])
        xkeys = sb("xkeys", [128, QT, HEADS0, 64])
        cast = sb("cast", [97, CCOL], f32r)
        gst = sb("gst", [97, SQ], f32r)
        q0hi = sb("q0hi", [120 + HEADS0, 3, SQ], f32r)
        q0lo = sb("q0lo", [120, 3, SQ], f32r)
        q1hi = sb("q1hi", [119, 3, SQ], f32r)
        q1lo = sb("q1lo", [112, 3, SQ], f32r)
        k0hi = sb("k0hi", [120 + HEADS0, T0 * 128], f32r)
        k0lo = sb("k0lo", [120, T0 * 128], f32r)
        k1hi = sb("k1hi", [119, T1 * 128], f32r)
        k1lo = sb("k1lo", [112, T1 * 128], f32r)
        v0c = sb("v0c", [128, T0, D0])
        v1c = sb("v1c", [128, T1, D1])
        v0 = sb("v0", [128, T0, V0C])
        v1 = sb("v1", [128, T1, V1C])
        negm0 = sb("negm0", [128, QT, HEADS0])
        negm1 = sb("negm1", [128, QT, 21])
        negmc = sb("negmc", [128, NC])
        mt0 = sb("mt0", [HEADS0, SQ], f32r)
        mt1 = sb("mt1", [7, 3, SQ], f32r)
        mtc = sb("mtc", [NC, 128], f32r)
        p0 = sb("p0", [128, T0, SQ])
        p1 = sb("p1", [128, T1, SQ])
        pc = sb("pc", [128, QT, CCOL])
        u0 = sb("u0", [V0C, 3, SQ])
        u1 = sb("u1", [120, 3, SQ])
        uc = sb("uc", [128, PAIRS, CAD])
        den0, rec0 = (sb(n, [128, 3 * HG0[0] * QT]) for n in ("den0", "rec0"))
        den1, rec1 = (sb(n, [128, 3 * HG1[0] * QT]) for n in ("den1", "rec1"))
        denc, recc = sb("denc", [128, CCOL // 128]), sb("recc", [128, CCOL // 128])
        rb = sb("rb", [120, 3, SQ])
        rbc = sb("rbc", [128, PAIRS, CAD])
        at0 = sb("at0", [128, 3, SQ])
        at1hi = sb("at1hi", [112, 3, SQ], f32r)
        at1lo = sb("at1lo", [112, 3, SQ], f32r)
        hsc = sb("hsc", [128, PAIRS, CAD])
        wk2b = sb("wk2b", [128, PAIRS, HT])
        s2t = sb("s2t", [HT, CAD])
        mx2 = sb("mx2", [96, 2 * HEADS0])
        sh2 = sb("sh2", [96, 2 * HEADS0, T])
        e2 = sb("e2", [96, 2 * HEADS0, T])
        sum2 = sb("sum2", [96, 2 * HEADS0])
        rc2 = sb("rc2", [96, 2 * HEADS0])
        p2 = sb("p2", [96, 2 * HEADS0, T])
        x1 = sb("x1", [112, 3, SQ])
        x1res = sb("x1res", [112, 3, SQ])
        def inside(buf, at=0):
            flat = buf if len(buf.shape) == 2 else buf[:, :, :].rearrange("p a n -> p (a n)")
            return flat[0:CK, at:at + 2 * H].rearrange("p (j n) -> p j n", j=2)

        p1flat = p1[:, :, :].rearrange("p a q -> p (a q)")
        kt1flat = kt1lo[:, :, :, :].rearrange("p g b k -> p (g b k)")
        wk0, wv0, wkca, wvca = inside(kt1flat), inside(kt1flat, 2 * H), inside(x1), inside(x1res)
        split_cols = 3 * sum(SPLIT.values())
        w_whole = p1flat[0:112, 0:split_cols]
        wk1, wv1 = inside(p1flat, split_cols), inside(p1flat, split_cols + 2 * H)
        wq0t = v1[0:120, :, :].rearrange("p a c -> p (a c)")[:, 0:3 * PAIRS * 128].rearrange("p (g n) -> p g n", g=3)
        k2bd, v2bd = rb, u1
        ca_whole = p0[0:3 * HT, :, :].rearrange("p a q -> p (a q)")
        vstage = pc[:, :, :].rearrange("p a n -> p (a n)")[:, 0:5 * H].rearrange("p (a n) -> p a n", a=5)
        wk2 = p1[:, 0:4, :]
        v2w = p1flat[:, 4 * SQ:4 * SQ + 2 * H].rearrange("p (a n) -> p a n", a=2)
        bank = [es.enter_context(nc.psum_tensor(f"bank{i}", [128, 512], f32)) for i in range(8)]
        def dram(name, shape, dt=f32):
            return nc.dram_tensor(name, shape, dt, kind="Internal").ap()

        sel_d = [dram("sel0_scratch", (HEADS0, T0 * 128)), dram("sel1_scratch", (7, T1 * 128))]
        v0_d = dram("v0_scratch", (B, HEADS0, KEYS0, D0))
        v1_d = dram("v1_scratch", (B, HEADS1, KEYS1, D1))
        wk2_d = dram("wk2_scratch", (B, 128, PAIRS, HT))
        v2w_d = dram("v2w_scratch", (B, HT, H))
        mtc_d = dram("mtc_scratch", (NC, 128))
        den0_d, r0_d = (dram(n, (HG0[0], 3, SQ)) for n in ("den0_scratch", "rec0_scratch"))
        den1_d, r1_d = (dram(n, (HG1[0], 3, SQ)) for n in ("den1_scratch", "rec1_scratch"))
        denc_d, rc_d = dram("denc_scratch", (2, PAIRS, CAD)), dram("recc_scratch", (2, PAIRS, CAD))

        full_a = [sem(f"bank_a{i}_full") for i in range(4)]
        free_a = [sem(f"bank_a{i}_drained") for i in range(4)]
        full_b = [sem(f"bank_b{i}_full") for i in range(4)]
        free_b = [sem(f"bank_b{i}_drained") for i in range(4)]
        kv0_in, kv1_in, kvca_in, wq0t_in = (sem(n) for n in ("kv0_weights_loaded", "kv1_weights_loaded", "kvca_weights_loaded", "wq0t_loaded"))
        wsplit_in, ca_in, small_in, wide_in, wo0_in, expand_in, vones_in = (
            sem(n) for n in ("split_weights_loaded", "ca_loaded", "small_loaded", "wide_loaded", "wo0_loaded", "expand_loaded", "value_ones_loaded"))
        sel_copied = sem("sel_copied")
        sel_ready = sem("sel_loaded")
        ones_stored = sem("missing_heads_ones_stored")
        setup_full = sem("setup_bank_full")
        setup_copied, setup_k_split, k_hi_step = sem("setup_bank_copied"), sem("setup_k_split"), sem("setup_k_hi")
        init_dve = sem("dve_buffers_initialised")
        init_pool = sem("pool_buffers_initialised")
        ca_split, whi_ready, wlo_ready = sem("ca_split"), sem("weights_high_ready"), sem("weights_low_ready")
        xthi_ready, xtlo_ready = sem("xthi_ready"), sem("xtlo_ready")
        at1_whole, at1hi_ready = sem("at1_whole"), sem("at1hi_ready")
        v0_stored, v1_stored = sem("v0_stored"), sem("v1_stored")
        kv2_masked = sem("k2_v2_masked")
        dve_init_step = sem("dve_init_step")
        v2w_stored, wk2_stored = sem("v2w_stored"), sem("wk2_stored")
        xt_in, xres_in, xkeys_in, v2w_in, v0c_in, v1c_in = (
            sem(n) for n in ("xt_loaded", "xres_loaded", "xkeys_loaded", "v2w_loaded", "v0c_loaded", "v1c_loaded"))
        q0hi_ready, q0hi2_ready, q1hi_ready = sem("q0hi_ready"), sem("q0hi2_ready"), sem("q1hi_ready")
        mt0_placed, mt1_placed = sem("mt0_placed"), sem("mt1_placed")
        g_hi, g_copied = sem("g_hi_written"), sem("g_hi_copied")
        k0_ready, k1_ready = (sem(n) for n in ("k0_ready", "k1_ready"))
        spread1_in = sem("spread1_loaded")
        tail_full = sem("tail_row_sums_spread")
        v0_ready, v1_ready, cast_ready = sem("v0_ready"), sem("v1_ready"), sem("cast_ready")
        mtc_st, mtc_placed = sem("mtc_stored"), sem("mtc_placed")
        den0_st, den1_st, denc_st = sem("den0_stored"), sem("den1_stored"), sem("denc_stored")
        den0_in, den1_in, denc_in = (sem(n) for n in ("den0_gathered", "den1_gathered", "denc_gathered"))
        rec0_ready, rec1_ready, recc_ready = (sem(n) for n in ("rec0_ready", "rec1_ready", "recc_ready"))
        rec0_st, rec1_st, recc_st = (sem(n) for n in ("rec0_stored", "rec1_stored", "recc_stored"))
        rb0_in, rb1_in, rbc_in = (sem(n) for n in ("rb0_spread", "rb1_spread", "rbc_spread"))
        at0_ready, at1_ready, hsc_ready = (sem(n) for n in ("at0_ready", "at1_ready", "hsc_ready"))
        wk2b_in, p2_ready = sem("wk2b_loaded"), sem("p2_ready")
        e2_ready, soft2 = sem("e2_ready"), sem("soft2_step")
        x1res_ready, out_stored = sem("x1res_ready"), sem("out_stored")

        def at(b, n, k):
            return b * n + k

        def wait(eng, s, b, n, k):
            v = at(b, n, k)
            if not isinstance(v, int) or v > 0:
                eng.wait_ge(s, v)

        def a_free(pe, b, j):
            wait(pe, free_a[j % 4], b, USES_A, j // 4)

        def a_full(eng, b, j):
            wait(eng, full_a[j % 4], b, USES_A, j // 4 + 1)

        def a_drained(eng, b, *jobs):
            for j in jobs:
                wait(eng, free_a[j % 4], b, USES_A, j // 4 + 1)

        def uses_b(b, j):
            first, none_left = isinstance(b, int) and b == 0, isinstance(b, int) and b == B
            same_bank = range(j % 4, JOBS_B, 4)
            missing = sum(1 for i in same_bank if i in LATE_B and (i < j or not first))
            if none_left:
                missing += sum(1 for i in same_bank if i not in LATE_B and i < j)
            return b * USES_B + (j // 4 - missing)

        def values_job(b, g):
            return (b, B_U0) if g == 0 else (b + 1, B_U12 + g - 1)

        def b_drained(eng, b, *jobs):
            for j in jobs:
                eng.wait_ge(free_b[j % 4], uses_b(b, j) + 1)

        def b_free(pe, b, j):
            if not isinstance(b, int) or uses_b(b, j) > 0:
                pe.wait_ge(free_b[j % 4], uses_b(b, j))

        def b_full(eng, b, j):
            eng.wait_ge(full_b[j % 4], uses_b(b, j) + 1)

        def bank_a(j):
            return bank[j % 4]

        def bank_b(j):
            return bank[4 + j % 4]

        S_K0, S_V0, S_CA, S_K1, S_WK2, S_V2W, S_V1 = offsets([6, 5, 2, 6, 2, 2, 5])
        SETUP = S_V1 + 5
        HALVES = [(g, half) for g in range(3) for half in range(2)]

        def setup_bank(job):
            return bank[4 + job % 4]

        def setup_drained(eng, job):
            if S_K0 <= job < S_K0 + 6:
                eng.wait_ge(setup_k_split, job - S_K0 + 1)
            elif S_K1 <= job < S_K1 + 6:
                eng.wait_ge(setup_k_split, 6 + job - S_K1 + 1)
            else:
                eng.wait_ge(setup_copied, job + 1 - 6 * (1 if job < S_K1 else 2))

        TILE_GROUP0 = [(g, tile) for g in range(3) for tile in range(TILES0[g])]
        TILE_GROUP1 = [(g, tile) for g in range(3) for tile in range(TILES1[g])]

        def schedule(eng, body):
            body(0, True, False, False, True)
            body(1, True, True, False, True)
            with eng.Fori(2, B - 1) as b:
                body(b, True, True, True, True)
            body(B - 1, True, True, True, False)
            body(B, False, True, True, False)
            body(B + 1, False, False, True, False)

        block = es.enter_context(nc.Block())

        @block.sync
        def _(sp):
            def load_xt(b):
                sp.dma_start(xt[:, :, :], t["xt"][b]).then_inc(xt_in, 16)

            def load_xres(b):
                sp.dma_start(xres[:, :, :], t["xt"][b]).then_inc(xres_in, 16)

            def load_xkeys(b):
                sp.dma_start(xkeys[:, :, :, 0:D0].rearrange("p k h d -> p (k h) d"), t["x"][b].rearrange("p (a d) -> p a d", d=D0))\
                    .then_inc(xkeys_in, 16)

            def load_v2w(b):
                sp.dma_start(wo0[96:128, 2, :], v2w_d[b, :, :]).then_inc(v2w_in, 16)

            def load_wk2(b):
                sp.dma_start(wk2b[:, :, :], wk2_d[b, :, :, :]).then_inc(wk2b_in, 16)

            def spread(src, heads, d, done):
                sp.dma_start(rb[0:heads * d, :, :], src.rearrange("h g q -> h (g q)").unsqueeze(1).to_broadcast([heads, d, 3 * SQ]))\
                    .then_inc(done, 16)

            def load_v(layer, b):
                src, dst, loads, ho, to, keys, done = (
                    (v0_d, v0c, LOADS0, HO0, TO0, KEYS0, v0c_in), (v1_d, v1c, LOADS1, HO1, TO1, KEYS1, v1c_in))[layer]
                rows_of = src[b].rearrange("h k d -> (h k) d")
                for rows, g, groups, tile, tiles in loads:
                    o = ho[g] * keys + tile * 128
                    if groups > 1:
                        step = (ho[g + 1] - ho[g]) * keys
                        part = bass.AP(rows_of.tensor, rows_of.offset + o * rows_of.ap[0][0],
                                       [[rows_of.ap[0][0], rows], [step * rows_of.ap[0][0], groups], rows_of.ap[1]])
                        to_step = to[g + 1] - to[g]
                        a = to[g] + tile
                        sp.dma_start(dst[0:rows, a:a + to_step * (groups - 1) + 1:to_step, :], part).then_inc(done, 16)
                    else:
                        part = rows_of[o:o + rows * tiles, :].rearrange("(a p) d -> p a d", p=rows)
                        sp.dma_start(dst[0:rows, to[g] + tile:to[g] + tile + tiles, :], part).then_inc(done, 16)

            sp.dma_start(enc[:, :, :, :].rearrange("p j b k -> p j (b k)"), t["enc"].rearrange("(j p) n -> p j n", p=CK)).then_inc(kv0_in, 16)
            for w, name, done in ((wk0, "wk0", kv0_in), (wv0, "wv0", kv0_in)):
                sp.dma_start(w, t[name].rearrange("(j p) n -> p j n", p=CK)).then_inc(done, 16)
            sp.dma_start(w_whole, t["wsplit"]).then_inc(wsplit_in, 16)
            load_xt(0)
            sp.dma_start(ca_whole, t["ca"]).then_inc(ca_in, 16)
            sp.dma_start(small[:, :], t["small"]).then_inc(small_in, 16)
            sp.dma_start(wide[:, :, :], t["wide"]).then_inc(wide_in, 16)
            for part, name in zip(sel_d, ("sel0", "sel1")):
                sp.dma_start(part, t[name]).then_inc(sel_copied, 16)
            for w, name, done in ((wkca, "wkca", kvca_in), (wvca, "wvca", kvca_in), (wk1, "wk1", kv1_in), (wv1, "wv1", kv1_in)):
                sp.dma_start(w, t[name].rearrange("(j p) n -> p j n", p=CK)).then_inc(done, 16)
            sp.dma_start(wq0t, t["wq0t"]).then_inc(wq0t_in, 16)
            sp.dma_start(wo0[:, :, :], t["wo0"]).then_inc(wo0_in, 16)
            sp.dma_start(v0[:, :, :].rearrange("p a c -> p (a c)"), t["vone0"]).then_inc(vones_in, 16)
            sp.wait_ge(init_dve, 1)
            for den_d, heads in ((den0_d, HG0), (den1_d, HG1)):
                sp.dma_start(den_d[heads[2]:heads[0], 2, :], rbc[0:1, 0:2, 0:128]).then_inc(ones_stored, 16)
            load_xkeys(0)
            sp.wait_ge(init_pool, 1)
            sp.wait_ge(sel_copied, 32)
            sp.dma_start(k0hi[120:128, :].bitcast(f32), sel_d[0]).then_inc(sel_ready, 16)
            sp.dma_start(k1hi[112:119, :].bitcast(f32), sel_d[1]).then_inc(sel_ready, 16)
            sp.dma_start(expand[:, :, :].rearrange("p a q -> p (a q)"), t["expand"]).then_inc(expand_in, 16)
            sp.dma_start(spread1[:, :, :].rearrange("p i c -> p (i c)"), t["spread1"]).then_inc(spread1_in, 16)
            load_xres(0)

            def store_v(stage, dst, keys, first_job, done):
                for tile, row, n, b, k in v_pieces(keys):
                    setup_drained(sp, first_job + tile)
                    sp.dma_start(dst[b, :, k:k + n, :].rearrange("h k d -> k h d"),
                                 stage[row:row + n, tile, :].rearrange("k (h d) -> k h d", d=dst.shape[3])).then_inc(done, 16)
                sp.wait_ge(done, 16 * len(v_pieces(keys)))

            store_v(vstage, v0_d, KEYS0, S_V0, v0_stored)
            load_v(0, 0)
            sp.wait_ge(ones_stored, 32)

            def body(b, do_a, do_b, do_c, more_a):
                last_step = not do_a and not do_b
                if do_a:
                    if more_a:
                        wait(sp, xtlo_ready, b, 1, 1)
                        load_xt(b + 1)
                    a_drained(sp, b, A_M)
                    sp.dma_start(q0hi[120:128, :, :].bitcast(f32), mt0[:, :].bitcast(f32).unsqueeze(1).to_broadcast([HEADS0, 3, SQ])).then_inc(mt0_placed, 16)
                    sp.dma_start(mtc_d, mtc[:, :].bitcast(f32)).then_inc(mtc_st, 16)
                    wait(sp, mtc_st, b, 16, 16)
                    sp.dma_start(cast[96:97, :].bitcast(f32), mtc_d.rearrange("j c -> (j c)").unsqueeze(0)).then_inc(mtc_placed, 16)
                def place_mt1():
                    b_drained(sp, b - 1, B_M + 1)
                    sp.dma_start(q1hi[112:119, :, :].bitcast(f32), mt1[:, :, :].bitcast(f32)).then_inc(mt1_placed, 16)

                if do_c and not last_step:
                    b_drained(sp, *values_job(b - 2, 2))
                    sp.dma_start(den1_d[:, 0:2, :], u1[112:119, 0:2, :]).then_inc(den1_st, 16)
                    sp.dma_start(den1_d[0:HG1[2], 2, :], u1[96:102, 2, :]).then_inc(den1_st, 16)
                    if not do_a:
                        place_mt1()
                    wait(sp, den1_st, b - 2, 32, 32)
                    sp.dma_start(den1[:, :], den1_d.rearrange("h g q -> (h g q)").rearrange("(r n) -> r n", r=128)).then_inc(den1_in, 16)
                    wait(sp, rec1_ready, b - 2, 1, 1)
                    sp.dma_start(r1_d.rearrange("h g q -> (h g q)").rearrange("(r n) -> r n", r=128), rec1[:, :]).then_inc(rec1_st, 16)
                if do_b and do_a:
                    place_mt1()
                if do_c and not last_step:
                    wait(sp, rec1_st, b - 2, 16, 16)
                    spread(r1_d, HG1[0], D1, rb1_in)
                if do_a:
                    a_drained(sp, b, A_CU, A_CU + 1)
                    for odd in range(2):
                        sp.dma_start(denc_d[odd], uc[64 * odd + D0:64 * odd + D0 + 1, :, :]).then_inc(denc_st, 16)
                    wait(sp, denc_st, b, 32, 32)
                    sp.dma_start(denc[:, :], denc_d.rearrange("o p c -> (o p c)").rearrange("(r n) -> r n", r=128)).then_inc(denc_in, 16)
                    a_drained(sp, b, A_U + 2)
                    sp.dma_start(den0_d[:, 0:2, :], u0[120:123, 0:2, :]).then_inc(den0_st, 16)
                    sp.dma_start(den0_d[0:HG0[2], 2, :], u0[G0[2]:G0[2] + HG0[2], 2, :]).then_inc(den0_st, 16)
                    wait(sp, recc_ready, b, 1, 1)
                    sp.dma_start(rc_d.rearrange("o p c -> (o p c)").rearrange("(r n) -> r n", r=128), recc[:, :]).then_inc(recc_st, 16)
                    wait(sp, den0_st, b, 32, 32)
                    sp.dma_start(den0[:, :], den0_d.rearrange("h g q -> (h g q)").rearrange("(r n) -> r n", r=128)).then_inc(den0_in, 16)
                    wait(sp, recc_st, b, 16, 16)
                    for odd in range(2):
                        sp.dma_start(rbc[64 * odd:64 * odd + D0, :, :],
                                     rc_d[odd].unsqueeze(0).to_broadcast([D0, PAIRS, CAD])).then_inc(rbc_in, 16)
                    wait(sp, rec0_ready, b, 1, 1)
                    sp.dma_start(r0_d.rearrange("h g q -> (h g q)").rearrange("(r n) -> r n", r=128), rec0[:, :]).then_inc(rec0_st, 16)
                    if isinstance(b, int) and b == 0:
                        setup_drained(sp, S_WK2 + 1)
                        for p in range(PAIRS):
                            sp.dma_start(wk2_d[:, :, p, :].rearrange("b r n -> r b n"), wk2[:, p, :].rearrange("r (b n) -> r b n", b=B))\
                                .then_inc(wk2_stored, 16)
                    wait(sp, rec0_st, b, 16, 16)
                    spread(r0_d, HG0[0], D0, rb0_in)
                    if isinstance(b, int) and b == 0:
                        setup_drained(sp, S_V2W + 1)
                        sp.dma_start(v2w_d.rearrange("(j b) r n -> (b r) j n", j=2), v2w).then_inc(v2w_stored, 16)
                        sp.wait_ge(wk2_stored, 16 * PAIRS)
                        load_wk2(0)
                        sp.dma_start(v1[:, :, :].rearrange("p a c -> p (a c)"), t["vone1"]).then_inc(vones_in, 16)
                        sp.wait_ge(v2w_stored, 16)
                        load_v2w(0)
                    if more_a:
                        wait(sp, v0_ready, b, 1, 1)
                        load_v(0, b + 1)
                if do_c:
                    b_drained(sp, b - 1, B_O + 1)
                    sp.dma_start(t["out"][b - 2], x1res[:, :, :]).then_inc(out_stored, 16)
                if do_a:
                    if more_a:
                        load_xkeys(b + 1)
                    if isinstance(b, int) and b == 0:
                        store_v(vstage, v1_d, KEYS1, S_V1, v1_stored)
                    wait(sp, v1_ready, b, 1, 0)
                    load_v(1, b)
                if do_a and more_a:
                    a_drained(sp, b, A_O, A_O + 1, A_O + 2)
                    load_xres(b + 1)
                    load_v2w(b + 1)
                    load_wk2(b + 1)

            schedule(sp, body)
            sp.wait_ge(out_stored, 16 * B)

        SM1_PARTS = (((0, 0, 308, 0),), ((0, 308, 232, 0), (1, 308, 232, 232)), ((1, 0, 308, 0),), ((2, 0, 462, 0),))

        @block.tensor
        def _(pe):
            mm, tr = nc.tensor.matmul, nc.tensor.transpose

            def setup_free_bank(job):
                if job >= 4:
                    setup_drained(pe, job - 4)
                return setup_bank(job)

            def setup_k(w, keys, rows, offs, job):
                for g, half in HALVES:
                    ps = setup_free_bank(job)
                    for j in range(2):
                        last = mm(ps[0:rows[g], 0:4 * keys], w[:, j, offs[g]:offs[g] + rows[g]],
                                  enc[:, j, 4 * half:4 * half + 4, 0:keys], start=j == 0, stop=j == 1)
                    last.then_inc(setup_full, 1)
                    job += 1

            def setup_v(w, job):
                flat = enc[:, :, :, :].rearrange("p j b k -> p j (b k)")
                for o, n in VT:
                    ps = setup_free_bank(job)
                    for j in range(2):
                        last = mm(ps[0:n, 0:H], flat[:, j, o:o + n], w[:, j, :], start=j == 0, stop=j == 1)
                    last.then_inc(setup_full, 1)
                    job += 1

            def setup_ca(job, w):
                pe.wait_ge(kvca_in, 32)
                ps = setup_free_bank(job)
                for g in range(3):
                    for j in range(2):
                        last = mm(ps[0:G0[g], g * B * T:(g + 1) * B * T], w[:, j, GO0[g]:GO0[g] + G0[g]],
                                  enc[:, j, :, KEYS0:CTX], start=j == 0, stop=j == 1)
                last.then_inc(setup_full, 1)

            def setup_ca_products():
                pe.wait_ge(kv2_masked, 6)
                pe.wait_ge(wq0t_in, 16)
                for half in range(PAIRS // 2):
                    ps = setup_free_bank(S_WK2 + half)
                    for e in range(2):
                        p = 2 * half + e
                        for g in range(3):
                            last = mm(ps[:, e * B * HT:(e + 1) * B * HT], wq0t[0:G0[g], g, p * 128:(p + 1) * 128],
                                      k2bd[0:G0[g], g, :], start=g == 0, stop=g == 2)
                    last.then_inc(setup_full, 1)
                pe.wait_ge(wo0_in, 16)
                for half in range(2):
                    ps = setup_free_bank(S_V2W + half)
                    for g in range(3):
                        last = mm(ps[:, 0:H], v2bd[0:G0[g], g, 128 * half:128 * (half + 1)], wo0[0:G0[g], g, :],
                                  start=g == 0, stop=g == 2)
                    last.then_inc(setup_full, 1)

            pe.wait_ge(kv0_in, 48)
            setup_k(wk0, KEYS0, G0, GO0, S_K0)
            setup_v(wv0, S_V0)
            pe.wait_ge(whi_ready, 1)
            pe.wait_ge(wlo_ready, 1)

            def body(b, do_a, do_b, do_c, more_a):
                last_step = not do_a and not do_b

                def q1_projection(i):
                    if i == 0:
                        if isinstance(b, int) and b == 1:
                            pe.wait_ge(wide_in, 16)
                        a_drained(pe, b - 1, A_O, A_O + 1, A_O + 2)
                        if isinstance(b, int) and b == 1:
                            for job in range(SETUP - 4, SETUP):
                                setup_drained(pe, job)
                    b_free(pe, b - 1, B_Q + i)
                    for e, m in enumerate(((0, 1), (2,))[i]):
                        for g in range(3):
                            last = mm(bank_b(B_Q + i)[0:XG[m], e * SQ:(e + 1) * SQ], wq1[0:XG[g], g, XO[m]:XO[m] + XG[m]],
                                      x1[0:XG[g], g, :], start=g == 0, stop=g == 2)
                    last.then_inc(full_b[(B_Q + i) % 4], 1)

                def products(out, w, cols, hi, lo):
                    last = None
                    for k in range(3):
                        r = XG[k]
                        for n, (wpart, part) in enumerate(((w[0], hi), (w[0], lo), (w[1], hi))):
                            last = mm(out, wpart[0:r, k, cols], part[0:r, k, :], start=k == n == 0, stop=k == n == 2)
                    return last

                def spread_row_sums(g):
                    if g == 0:
                        pe.wait_ge(spread1_in, 16)
                        a_drained(pe, B - 1, A_O, A_O + 1, A_O + 2)
                    b_drained(pe, *values_job(b - 2, g))
                    rows = HG1[g] * (D1 + 1)
                    mm(bank[g + 1][0:XG[g], 0:SQ], spread1[0:rows, g // 2, 0:XG[g]], u1[0:rows, g, :], start=True, stop=True)\
                        .then_inc(tail_full, 1)

                def output_projection(i):
                    if i == 0:
                        wait(pe, at1_ready, b - 2, 2, 2)
                    b_free(pe, b - 1, B_O + i)
                    for e, m in enumerate(((0, 1), (2,))[i]):
                        last = products(bank_b(B_O + i)[0:XG[m], e * SQ:(e + 1) * SQ], wo1, slice(XO[m], XO[m] + XG[m]), at1hi, at1lo)
                    last.then_inc(full_b[(B_O + i) % 4], 1)

                def layer1_values(b1, g):
                    at_b, job = values_job(b1, g)
                    b_drained(pe, b1, *(j for j in range(B_ST + TO1[g] // 2, B_ST + (TO1[g] + TILES1[g] + 1) // 2) if j % 4 != job % 4))
                    b_free(pe, at_b, job)
                    rows = HG1[g] * (D1 + 1)
                    for tile in range(TILES1[g]):
                        last = mm(bank_b(job)[0:rows, 0:SQ], v1[:, TO1[g] + tile, 0:rows], p1[:, TO1[g] + tile, :],
                                  start=tile == 0, stop=tile == TILES1[g] - 1)
                    last.then_inc(full_b[job % 4], 1)

                def layer1_maxima(q, first, last_):
                    if q == first == 0:
                        wait(pe, q1hi_ready, b - 1, 2, 2)
                        wait(pe, k1_ready, b - 1, 1, 1)
                    for i in range(first, last_):
                        job, parts = B_SM + 4 * q + i, SM1_PARTS[i]
                        b_free(pe, b - 1, job)
                        for g, k, cols, c in parts:
                            last = mm(bank_b(job)[:, c:c + cols], q1hi[0:XG[g], g, q * 128:(q + 1) * 128],
                                      k1hi[0:XG[g], 128 * TO1[g] + k:128 * TO1[g] + k + cols], start=True, stop=True)
                        last.then_inc(full_b[job % 4], 1)

                def ca_maxima(first, last_):
                    if first == 0:
                        wait(pe, cast_ready, b, 1, 1)
                        a_drained(pe, b, A_Q2G)
                        wait(pe, g_copied, b, 1, 1)
                    for i in range(first, last_):
                        a_free(pe, b, A_CS + i)
                        for e in range(2):
                            c = (2 * i + e) * 128
                            last = mm(bank_a(A_CS + i)[:, e * SQ:(e + 1) * SQ], cast[0:96, c:c + 128], gst[0:96, :], start=True, stop=True)
                        last.then_inc(full_a[(A_CS + i) % 4], 1)

                if do_a:
                    wait(pe, xthi_ready, b, 1, 1)
                    wait(pe, xtlo_ready, b, 1, 1)
                    a_free(pe, b, A_Q01)
                    for g in range(2):
                        last = products(bank_a(A_Q01)[0:G0[g], g * SQ:(g + 1) * SQ], wq0, slice(GO0[g], GO0[g] + G0[g]), xthi, xtlo)
                    last.then_inc(full_a[A_Q01 % 4], 1)
                    a_free(pe, b, A_Q2G)
                    products(bank_a(A_Q2G)[:, 0:SQ], wq0, slice(GO0[2], GO0[2] + 128), xthi, xtlo)\
                        .then_inc(full_a[A_Q2G % 4], 1)
                if isinstance(b, int) and b == 0:
                    setup_ca(S_CA, wkca)
                if do_b:
                    q1_projection(0)
                if do_a:
                    ca_maxima(0, 4)
                if do_b:
                    q1_projection(1)
                if do_a:
                    ca_maxima(4, NC // 2)
                    wait(pe, q0hi_ready, b, 1, 1)
                    wait(pe, q0hi2_ready, b, 1, 1)
                    if isinstance(b, int) and b == 0:
                        pe.wait_ge(init_pool, 1)
                        pe.wait_ge(init_dve, 1)
                        pe.wait_ge(small_in, 16)
                    wait(pe, k0_ready, b, 1, 1)
                    for i in range(3):
                        a_free(pe, b, A_SM + i)
                        for q, g in (((i, 0), (i, 1)) if i < 2 else ((0, 2), (1, 2))):
                            cols = (HG0[g] * KEYS0 + 1) // 2 * 2
                            c = (220 * g) if i < 2 else 146 * q
                            last = mm(bank_a(A_SM + i)[:, c:c + cols], q0hi[0:120, g, q * 128:(q + 1) * 128],
                                      k0hi[0:120, 256 * g:256 * g + cols], start=True, stop=True)
                        last.then_inc(full_a[(A_SM + i) % 4], 1)
                if do_c:
                    layer1_values(b - 2, 1)
                if isinstance(b, int) and b == 0:
                    setup_ca(S_CA + 1, wvca)
                if last_step:
                    spread_row_sums(0)
                if do_a:
                    a_drained(pe, b, A_SM, A_SM + 1, A_SM + 2)
                    a_drained(pe, b, A_CS + 2, A_CS + 3, A_CS + 4, A_CS + 5)
                    a_free(pe, b, A_M)
                    for q in range(QT):
                        tr(bank_a(A_M)[0:HEADS0, q * 128:(q + 1) * 128], negm0[:, q, :], ident[:, :])
                    tr(bank_a(A_M)[0:NC, SQ:SQ + 128], negmc[:, :], ident[:, :]).then_inc(full_a[A_M % 4], 1)
                if do_c:
                    layer1_values(b - 2, 2)
                if isinstance(b, int) and b == 0:
                    pe.wait_ge(kv1_in, 32)
                    setup_k(wk1, KEYS1, XG, XO, S_K1)
                def layer0_scores(i):
                    if i == 0:
                        a_drained(pe, b, A_Q01, A_Q2G)
                        wait(pe, mt0_placed, b, 16, 16)
                        if isinstance(b, int) and b == 0:
                            pe.wait_ge(sel_ready, 32)
                    a_free(pe, b, A_ST + i)
                    for e in range(2):
                        tile = 2 * i + e
                        g = TILE_GROUP0[tile][0]
                        ps = bank_a(A_ST + i)[:, e * SQ:(e + 1) * SQ]
                        keys = slice(tile * 128, (tile + 1) * 128)
                        mm(ps, k0hi[:, keys], q0hi[:, g, :], start=True, stop=False)
                        mm(ps, k0hi[0:120, keys], q0lo[:, g, :], start=False, stop=False)
                        last = mm(ps, k0lo[:, keys], q0hi[0:120, g, :], start=False, stop=True)
                    last.then_inc(full_a[(A_ST + i) % 4], 1)

                if do_b:
                    layer1_maxima(0, 0, 4)
                    layer1_maxima(1, 0, 1)
                if do_a:
                    layer0_scores(0)
                if do_b:
                    layer1_maxima(1, 1, 2)
                if do_a:
                    layer0_scores(1)
                if do_b:
                    layer1_maxima(1, 2, 3)
                if do_a:
                    layer0_scores(2)
                if do_b:
                    layer1_maxima(1, 3, 4)
                if do_a:
                    wait(pe, mtc_placed, b, 16, 16)
                    for c in range(3):
                        for k in range(QT):
                            job = A_CT + 2 * c + k
                            a_free(pe, b, job)
                            mm(bank_a(job)[:, :], gst[:, k * 128:(k + 1) * 128], cast[:, c * 512:(c + 1) * 512], start=True, stop=True)\
                                .then_inc(full_a[job % 4], 1)
                if do_b:
                    b_drained(pe, b - 1, *range(B_SM + 4, B_SM + 8))
                    for q in range(QT):
                        b_free(pe, b - 1, B_M + q)
                        for g in range(3):
                            last = tr(bank_b(B_M + q)[0:7, g * 128:(g + 1) * 128], negm1[:, q, 7 * g:7 * g + 7], ident[:, :])
                        last.then_inc(full_b[(B_M + q) % 4], 1)
                if last_step:
                    spread_row_sums(1)
                    spread_row_sums(2)
                if do_a:
                    wait(pe, xkeys_in, b, 16, 16)
                    for i in range(2):
                        a_drained(pe, b, *(range(A_CT, A_CT + 4), range(A_CT + 4, A_CT + 6))[i])
                        a_free(pe, b, A_CU + i)
                        for e in range(2):
                            for k in range(QT):
                                for odd in range(2):
                                    h = 4 * i + 2 * e + odd
                                    last = mm(bank_a(A_CU + i)[64 * odd:64 * odd + 64, e * CAD:(e + 1) * CAD], xkeys[:, k, h, :],
                                              pc[:, k, h * CAD:(h + 1) * CAD], start=k == 0, stop=k == QT - 1)
                        last.then_inc(full_a[(A_CU + i) % 4], 1)
                    wait(pe, v0_ready, b, 1, 1)
                    for g in range(3):
                        a_drained(pe, b, A_ST + g)
                        a_free(pe, b, A_U + g)
                        rows = G0[g] + HG0[g]
                        for tile in range(2):
                            last = mm(bank_a(A_U + g)[0:rows, 0:SQ], v0[:, 2 * g + tile, 0:rows], p0[:, 2 * g + tile, :],
                                      start=tile == 0, stop=tile == 1)
                        last.then_inc(full_a[(A_U + g) % 4], 1)
                if isinstance(b, int) and b == 0:
                    setup_ca_products()
                    setup_v(wv1, S_V1)
                if do_b:
                    b_drained(pe, b - 1, B_Q, B_Q + 1)
                    wait(pe, mt1_placed, b - 1, 16, 16)
                    for i in range(T1 // 2):
                        b_free(pe, b - 1, B_ST + i)
                        for e in range(2):
                            tile = 2 * i + e
                            g = TILE_GROUP1[tile][0]
                            ps = bank_b(B_ST + i)[:, e * SQ:(e + 1) * SQ]
                            keys, r = slice(tile * 128, (tile + 1) * 128), XG[g]
                            mm(ps, k1hi[:, keys], q1hi[:, g, :], start=True, stop=False)
                            mm(ps, k1hi[0:r, keys], q1lo[0:r, g, :], start=False, stop=False)
                            last = mm(ps, k1lo[0:r, keys], q1hi[0:r, g, :], start=False, stop=True)
                        last.then_inc(full_b[(B_ST + i) % 4], 1)
                if do_c and do_a:
                    output_projection(0)
                    output_projection(1)
                if do_b:
                    wait(pe, v1_ready, b - 1, 1, 1)
                    layer1_values(b - 1, 0)
                if do_c and not do_a:
                    output_projection(0)
                    output_projection(1)
                if do_a:
                    wait(pe, hsc_ready, b, 1, 1)
                    wait(pe, wk2b_in, b, 16, 16)
                    a_free(pe, b, A_S2)
                    for p in range(PAIRS):
                        last = mm(bank_a(A_S2)[0:HT, 0:CAD], wk2b[:, p, :], hsc[:, p, :], start=p == 0, stop=p == PAIRS - 1)
                    last.then_inc(full_a[A_S2 % 4], 1)
                    a_drained(pe, b, A_S2)
                    a_free(pe, b, A_TR)
                    for c in range(2):
                        last = mm(bank_a(A_TR)[0:96, c * HT:(c + 1) * HT], s2t[:, c * 96:(c + 1) * 96], ident[0:HT, 0:HT], start=True, stop=True)
                    last.then_inc(full_a[A_TR % 4], 1)
                    wait(pe, at0_ready, b, 2, 2)
                    wait(pe, v2w_in, b, 16, 16)
                    def layer0_output(m):
                        a_free(pe, b, A_O + m)
                        for g in range(2):
                            mm(bank_a(A_O + m)[0:XG[m], 0:SQ], wo0[0:120, g, XO[m]:XO[m] + XG[m]], at0[0:120, g, :], start=g == 0, stop=False)

                    layer0_output(0)
                    layer0_output(1)
                    wait(pe, p2_ready, b, 1, 1)
                    if isinstance(b, int) and b == 0:
                        pe.wait_ge(expand_in, 16)
                    a_free(pe, b, A_EX)
                    for c in range(2):
                        last = mm(bank_a(A_EX)[96:128, 0:SQ], p2[:, c * HEADS0:(c + 1) * HEADS0, :].rearrange("p h t -> p (h t)"),
                                  expand[:, c, :], start=c == 0, stop=c == 1)
                    last.then_inc(full_a[A_EX % 4], 1)
                    layer0_output(2)
                    a_drained(pe, b, A_EX)
                    for m in range(3):
                        mm(bank_a(A_O + m)[0:XG[m], 0:SQ], wo0[:, 2, XO[m]:XO[m] + XG[m]], at0[:, 2, :], start=False, stop=True)\
                            .then_inc(full_a[(A_O + m) % 4], 1)

            schedule(pe, body)

        @block.scalar
        def _(act):
            def copy(out, in_):
                return nc.scalar.activation(out, in_, ACT.Copy)

            def setup_copy(job, *pairs):
                act.wait_ge(setup_full, job + 1)
                for dst, src in pairs:
                    last = copy(dst, src)
                last.then_inc(setup_copied, 1)

            def setup_v(stage, job):
                for tile, (_, n) in enumerate(VT):
                    setup_copy(job + tile, (stage[0:n, tile, :], setup_bank(job + tile)[0:n, 0:H]))

            act.wait_ge(wsplit_in, 16)
            copy(whi[:, :, :].rearrange("p g n -> p (g n)"), w_whole).then_inc(whi_ready, 1)

            def split_x(b):
                wait(act, xt_in, b, 16, 16)
                copy(xthi[:, :, :], xt[:, :, :]).then_inc(xthi_ready, 1)

            def copy_u1(b1, *groups):
                wait(act, at1_ready, b1, 2, 0)
                for g in groups:
                    at_b, job = values_job(b1, g)
                    b_full(act, at_b, job)
                    rows = HG1[g] * (D1 + 1)
                    copy(u1[0:rows, g, :], bank_b(job)[0:rows, 0:SQ]).then_inc(free_b[job % 4], 1)

            split_x(0)
            setup_v(vstage, S_V0)

            def body(b, do_a, do_b, do_c, more_a):
                if do_a:
                    a_full(act, b, A_Q01)
                    copy(q0hi[0:120, 0:2, :], bank_a(A_Q01)[0:120, :].rearrange("p (g q) -> p g q", q=SQ)).then_inc(q0hi_ready, 1)
                    wait(act, g_hi, b, 1, 1)
                    copy(gst[2 * HT:3 * HT, :], gst[0:HT, :].bitcast(f32)).then_inc(g_copied, 1)
                if isinstance(b, int) and b == 0:
                    for job, kt in ((S_CA, k2t), (S_CA + 1, v2t)):
                        setup_copy(job, *((kt[0:G0[g], g, :], setup_bank(job)[0:G0[g], g * B * T:(g + 1) * B * T]) for g in range(3)))
                    act.wait_ge(v0_stored, 16 * len(v_pieces(KEYS0)))
                if isinstance(b, int) and b == 1:
                    act.wait_ge(wk2_stored, 16 * PAIRS)
                    act.wait_ge(v2w_stored, 16)
                    act.wait_ge(v1_stored, 16 * len(v_pieces(KEYS1)))
                if do_b:
                    for i in range(2):
                        b_full(act, b - 1, B_Q + i)
                        dst, src = ((q1hi[0:112, 0:2, :], bank_b(B_Q)[0:112, :].rearrange("p (g q) -> p g q", q=SQ)),
                                    (q1hi[0:96, 2, :], bank_b(B_Q + 1)[0:96, 0:SQ]))[i]
                        copy(dst, src).then_inc(q1hi_ready, 1)
                if do_c:
                    copy_u1(b - 2, 1, 2)
                if do_a:
                    for i in range(3):
                        a_full(act, b, A_ST + i)
                        nc.scalar.activation(p0[:, 2 * i:2 * i + 2, :].rearrange("p a q -> p (a q)"), bank_a(A_ST + i)[:, :], ACT.Exp, scale=SCALE0)\
                            .then_inc(free_a[(A_ST + i) % 4], 1)
                    for c in range(3):
                        for k in range(QT):
                            job = A_CT + 2 * c + k
                            a_full(act, b, job)
                            nc.scalar.activation(pc[:, k, c * 512:(c + 1) * 512], bank_a(job)[:, :], ACT.Exp, scale=SCALE0)\
                                .then_inc(free_a[job % 4], 1)
                    wait(act, hsc_ready, b, 1, 0)
                    for i in range(2):
                        a_full(act, b, A_CU + i)
                        copy(uc[:, 2 * i:2 * i + 2, :].rearrange("p e c -> p (e c)"), bank_a(A_CU + i)[:, 0:2 * CAD])\
                            .then_inc(free_a[(A_CU + i) % 4], 1)
                    wait(act, at0_ready, b, 2, 0)
                    for g in range(3):
                        a_full(act, b, A_U + g)
                        rows = G0[g] + HG0[g]
                        copy(u0[0:rows, g, :], bank_a(A_U + g)[0:rows, 0:SQ]).then_inc(free_a[(A_U + g) % 4], 1)
                if do_a and more_a:
                    a_full(act, b, A_U + 2)
                    split_x(b + 1)
                def split_at1():
                    wait(act, at1_whole, b - 2, 2, 2)
                    copy(at1hi[:, 0:2, :], u1[0:112, 0:2, :])
                    copy(at1hi[0:96, 2, :], u1[0:96, 2, :]).then_inc(at1hi_ready, 1)

                if do_c and do_a:
                    split_at1()
                if isinstance(b, int) and b == 0:
                    act.wait_ge(wlo_ready, 1)
                    for half in range(2):
                        setup_copy(S_WK2 + half, (wk2[:, 2 * half:2 * half + 2, :].rearrange("p a n -> p (a n)"), setup_bank(S_WK2 + half)[:, :]))
                    for half in range(2):
                        setup_copy(S_V2W + half, (v2w[:, half, :], setup_bank(S_V2W + half)[:, 0:H]))
                    setup_v(vstage, S_V1)
                if do_b:
                    for i in range(T1 // 2):
                        b_full(act, b - 1, B_ST + i)
                        nc.scalar.activation(p1[:, 2 * i:2 * i + 2, :].rearrange("p a q -> p (a q)"), bank_b(B_ST + i)[:, :], ACT.Exp, scale=SCALE1)\
                            .then_inc(free_b[(B_ST + i) % 4], 1)
                    if do_c and not do_a:
                        split_at1()
                    copy_u1(b - 1, 0)
                elif do_c:
                    split_at1()
                if do_a:
                    a_full(act, b, A_S2)
                    copy(s2t[:, :], bank_a(A_S2)[0:HT, 0:CAD]).then_inc(free_a[A_S2 % 4], 1)
                    a_drained(act, b, A_TR)
                    nc.scalar.activation(e2[:, :, :], sh2[:, :, :], ACT.Exp, scale=SCALE0).then_inc(e2_ready, 1)

            schedule(act, body)

        @block.vector
        def _(dve):
            tt, cp = nc.vector.tensor_tensor, nc.vector.tensor_copy
            nc.vector.memset(xkeys[:, :, :, :].rearrange("p k h d -> p (k h d)"), 0.0).then_inc(dve_init_step, 1)
            nc.vector.memset(q0lo[:, 2, :].bitcast(f32), 0.0)
            nc.vector.memset(q1hi[96:119, 2, :].bitcast(f32), 0.0)
            nc.vector.memset(negm1[:, :, 20:21], 0.0)
            nc.vector.memset(q0hi[:, 2, :].bitcast(f32), 0.0)
            nc.vector.memset(at0[:, 2, :], 0.0)
            nc.vector.memset(x1res[96:112, 2, :], 0.0)
            nc.vector.memset(rbc[:, :, :].rearrange("p a c -> p (a c)"), 1.0)
            nc.vector.memset(gst[96:97, :].bitcast(f32), 1.0)
            nc.vector.memset(v0c[:, :, :], 0.0)
            nc.vector.memset(v1c[:, :, :], 0.0)
            dve.wait_ge(dve_init_step, 1)
            nc.vector.memset(xkeys[:, :, :, D0:D0 + 1].rearrange("p k h d -> p (k h) d"), 1.0).then_inc(init_dve, 1)
            def split_k(hi, lo, keys, rows, first, done):
                for i, (g, half) in enumerate(HALVES):
                    dve.wait_ge(setup_full, first + i + 1)
                    part = hi[0:rows[g], g, 4 * half:4 * half + 4, :].rearrange("p b k -> p (b k)")
                    rest = lo[0:rows[g], g, 4 * half:4 * half + 4, :].rearrange("p b k -> p (b k)")
                    ps = setup_bank(first + i)[0:rows[g], 0:4 * keys]
                    cp(part, ps).then_inc(k_hi_step, 1)
                    dve.wait_ge(k_hi_step, done + i + 1)
                    tt(rest, ps, part.bitcast(f32), ALU.subtract).then_inc(setup_k_split, 1)

            split_k(kt0hi, kt0lo, KEYS0, G0, S_K0, 0)
            dve.wait_ge(whi_ready, 1)
            tt(wlo[:, :, :].rearrange("p g n -> p (g n)"), w_whole, whi[:, :, :].rearrange("p g n -> p (g n)").bitcast(f32), ALU.subtract)\
                .then_inc(wlo_ready, 1)
            dve.wait_ge(ca_in, 16)
            flat = ca[:, :, :].rearrange("p b c -> p (b c)")
            cp(flat, ca_whole).then_inc(ca_split, 1)
            dve.wait_ge(ca_split, 1)
            tt(flat[64:96, :], ca_whole[64:96, :], flat[64:96, :].bitcast(f32), ALU.subtract).then_inc(ca_split, 1)
            dve.wait_ge(small_in, 16)
            dve.wait_ge(wide_in, 16)

            def mask_kv2():
                setup_drained(dve, S_CA + 1)
                for src, dst in ((k2t, k2bd), (v2t, v2bd)):
                    for g in range(3):
                        r = G0[g]
                        tt(dst[0:r, g, :].rearrange("p (b h t) -> p b h t", b=B, h=HEADS0),
                           src[0:r, g, :].rearrange("p (b t) -> p b t", t=T).unsqueeze(2).to_broadcast([r, B, HEADS0, T]),
                           head8[0:r, g, :].unsqueeze(1).unsqueeze(3).to_broadcast([r, B, HEADS0, T]), ALU.mult).then_inc(kv2_masked, 1)

            def body(b, do_a, do_b, do_c, more_a):
                last_step = not do_a and not do_b

                def layer1_maxima(q):
                    for i in range(4):
                        job = B_SM + 4 * q + i
                        b_full(dve, b - 1, job)
                        ps = bank_b(job)
                        if i == 1:
                            dst = negm1[:, q, 0:14].rearrange("p (g h) -> p g h", g=2)[:, :, 4:7]
                            src = ps[:, 0:464].rearrange("p (g k) -> p g k", g=2)[:, :, 0:231].rearrange("p g (h k) -> p g h k", k=KEYS1)
                        else:
                            h, n = ((0, 4), None, (7, 4), (14, 6))[i]
                            dst = negm1[:, q, h:h + n]
                            src = ps[:, 0:n * KEYS1].rearrange("p (h k) -> p h k", k=KEYS1)
                        nc.vector.tensor_reduce(out=dst, in_=src, axis=AX, op=ALU.max, negate=True)\
                            .then_inc(free_b[job % 4], 1)

                if do_a:
                    a_full(dve, b, A_Q2G)
                    ps = bank_a(A_Q2G)
                    cp(gst[0:HT, :], ps[CA_ROW:CA_ROW + HT, 0:SQ]).then_inc(g_hi, 1)
                    cp(q0hi[0:G0[2], 2, :], ps[0:G0[2], 0:SQ]).then_inc(q0hi2_ready, 1)
                    wait(dve, q0hi2_ready, b, 1, 1)
                    tt(q0lo[0:G0[2], 2, :], ps[0:G0[2], 0:SQ], q0hi[0:G0[2], 2, :].bitcast(f32), ALU.subtract)
                    wait(dve, g_hi, b, 1, 1)
                    tt(gst[HT:2 * HT, :], ps[CA_ROW:CA_ROW + HT, 0:SQ], gst[0:HT, :].bitcast(f32), ALU.subtract)\
                        .then_inc(free_a[A_Q2G % 4], 1)
                    wait(dve, q0hi_ready, b, 1, 1)
                    tt(q0lo[:, 0:2, :], bank_a(A_Q01)[0:120, :].rearrange("p (g q) -> p g q", q=SQ), q0hi[0:120, 0:2, :].bitcast(f32),
                       ALU.subtract).then_inc(free_a[A_Q01 % 4], 1)
                    for i in range(NC // 2):
                        a_full(dve, b, A_CS + i)
                        nc.vector.tensor_reduce(out=negmc[:, 2 * i:2 * i + 2], in_=bank_a(A_CS + i)[:, :].rearrange("p (e k) -> p e k", e=2),
                                                axis=AX, op=ALU.max, negate=True).then_inc(free_a[(A_CS + i) % 4], 1)
                    for i in range(3):
                        a_full(dve, b, A_SM + i)
                        if i < 2:
                            dst = negm0[:, i, 0:6].rearrange("p (g h) -> p g h", g=2)
                            src = bank_a(A_SM + i)[:, 0:440].rearrange("p (g k) -> p g k", g=2)[:, :, 0:219]\
                                .rearrange("p g (h k) -> p g h k", k=KEYS0)
                        else:
                            dst = negm0[:, :, 6:8]
                            src = bank_a(A_SM + i)[:, 0:292].rearrange("p (q h k) -> p q h k", q=2, k=KEYS0)
                        nc.vector.tensor_reduce(out=dst, in_=src, axis=AX, op=ALU.max, negate=True)\
                            .then_inc(free_a[(A_SM + i) % 4], 1)
                if do_b:
                    for i, (r, gs) in enumerate(((112, slice(0, 2)), (96, slice(2, 3)))):
                        wait(dve, q1hi_ready, b - 1, 2, i + 1)
                        n = (gs.stop - gs.start) * SQ
                        tt(q1lo[0:r, gs, :], bank_b(B_Q + i)[0:r, 0:n].rearrange("p (g q) -> p g q", q=SQ),
                           q1hi[0:r, gs, :].bitcast(f32), ALU.subtract).then_inc(free_b[(B_Q + i) % 4], 1)
                if do_a:
                    a_full(dve, b, A_M)
                    cp(mtc[:, :], bank_a(A_M)[0:NC, SQ:SQ + 128])
                    cp(mt0[0:HEADS0, :], bank_a(A_M)[0:HEADS0, 0:SQ]).then_inc(free_a[A_M % 4], 1)
                if isinstance(b, int) and b == 0:
                    mask_kv2()
                    split_k(kt1hi, kt1lo, KEYS1, XG, S_K1, 6)
                if do_b:
                    layer1_maxima(0)
                    layer1_maxima(1)
                def layer1_reciprocals():
                    wait(dve, den1_in, b - 2, 16, 16)
                    nc.vector.reciprocal(rec1[:, :], den1[:, :]).then_inc(rec1_ready, 1)

                if do_c and do_a:
                    layer1_reciprocals()
                if do_b:
                    for q in range(QT):
                        b_full(dve, b - 1, B_M + q)
                        cp(mt1[:, :, q * 128:(q + 1) * 128], bank_b(B_M + q)[0:7, 0:384].rearrange("p (g q) -> p g q", g=3))\
                            .then_inc(free_b[(B_M + q) % 4], 1)
                if do_c and do_b and not do_a:
                    layer1_reciprocals()
                if do_c:
                    if not last_step:
                        wait(dve, rb1_in, b - 2, 16, 16)
                        tt(u1[0:112, 0:2, :], u1[0:112, 0:2, :], rb[0:112, 0:2, :], ALU.mult).then_inc(at1_whole, 1)
                        tt(u1[0:96, 2, :], u1[0:96, 2, :], rb[0:96, 2, :], ALU.mult).then_inc(at1_whole, 1)
                    else:
                        for g in range(3):
                            dve.wait_ge(tail_full, g + 1)
                            nc.vector.reciprocal(rb[0:XG[g], g, :], bank[g + 1][0:XG[g], 0:SQ]).then_inc(rec1_ready, 1)
                            dve.wait_ge(rec1_ready, B - 1 + g + 1)
                            last = tt(u1[0:XG[g], g, :], u1[0:XG[g], g, :], rb[0:XG[g], g, :], ALU.mult)
                            if g > 0:
                                last.then_inc(at1_whole, 1)
                    wait(dve, at1hi_ready, b - 2, 1, 1)
                    tt(at1lo[:, 0:2, :], u1[0:112, 0:2, :], at1hi[:, 0:2, :].bitcast(f32), ALU.subtract).then_inc(at1_ready, 1)
                    tt(at1lo[0:96, 2, :], u1[0:96, 2, :], at1hi[0:96, 2, :].bitcast(f32), ALU.subtract).then_inc(at1_ready, 1)
                if do_a:
                    wait(dve, denc_in, b, 16, 16)
                    nc.vector.reciprocal(recc[:, :], denc[:, :]).then_inc(recc_ready, 1)
                    wait(dve, den0_in, b, 16, 16)
                    nc.vector.reciprocal(rec0[:, :], den0[:, :]).then_inc(rec0_ready, 1)
                    wait(dve, rbc_in, b, 32, 32)
                    tt(hsc[:, :, :], uc[:, :, :], rbc[:, :, :], ALU.mult).then_inc(hsc_ready, 1)
                if do_c:
                    wait(dve, x1res_ready, b - 2, 1, 1)
                    for i, ms in enumerate(((0, 1), (2,))):
                        b_full(dve, b - 1, B_O + i)
                        for e, m in enumerate(ms):
                            r = XG[m]
                            last = tt(x1res[0:r, m, :], bank_b(B_O + i)[0:r, e * SQ:(e + 1) * SQ], x1res[0:r, m, :], ALU.add)
                        last.then_inc(free_b[(B_O + i) % 4], 1)
                if do_a:
                    wait(dve, rb0_in, b, 16, 16)
                    tt(at0[0:120, 0:2, :], u0[0:120, 0:2, :], rb[:, 0:2, :], ALU.mult).then_inc(at0_ready, 1)
                    tt(at0[0:80, 2, :], u0[0:80, 2, :], rb[0:80, 2, :], ALU.mult).then_inc(at0_ready, 1)
                    a_full(dve, b, A_TR)
                    s2 = bank_a(A_TR)[0:96, 0:2 * HT].rearrange("p (h t) -> p h t", t=T)
                    nc.vector.reduce_max(mx2[:, :], s2, AX).then_inc(soft2, 1)
                    wait(dve, soft2, b, 3, 1)
                    tt(sh2[:, :, :], s2, mx2[:, :].unsqueeze(2).to_broadcast([96, 2 * HEADS0, T]), ALU.subtract)\
                        .then_inc(free_a[A_TR % 4], 1)
                    wait(dve, e2_ready, b, 1, 1)
                    nc.vector.reduce_sum(sum2[:, :], e2[:, :, :], AX).then_inc(soft2, 1)
                    wait(dve, soft2, b, 3, 2)
                    nc.vector.reciprocal(rc2[:, :], sum2[:, :]).then_inc(soft2, 1)
                    wait(dve, soft2, b, 3, 3)
                    tt(p2[:, :, :], e2[:, :, :], rc2[:, :].unsqueeze(2).to_broadcast([96, 2 * HEADS0, T]), ALU.mult).then_inc(p2_ready, 1)
                    a_full(dve, b, A_EX)
                    cp(at0[96:128, 2, :], bank_a(A_EX)[96:128, 0:SQ]).then_inc(free_a[A_EX % 4], 1)
                    wait(dve, xres_in, b, 16, 16)
                    wait(dve, x1res_ready, b, 1, 0)
                    for m in range(3):
                        a_full(dve, b, A_O + m)
                        r = XG[m]
                        nc.vector.scalar_tensor_tensor(
                            out=x1[0:r, m, :], in0=bank_a(A_O + m)[0:r, 0:SQ], scalar=bias0[0:r, m:m + 1],
                            in1=xres[0:r, m, :], op0=ALU.add, op1=ALU.add).then_inc(free_a[(A_O + m) % 4], 1)

            schedule(dve, body)

        @block.gpsimd
        def _(pool):
            for buf in (k0lo, k0hi, k1lo, k1hi):
                last = nc.gpsimd.memset(buf[:, :].bitcast(f32), 0.0)
            last.then_inc(init_pool, 1)
            pool.wait_ge(init_pool, 1)
            pool.wait_ge(small_in, 16)

            def build_cast(b):
                nc.gpsimd.tensor_tensor(cast[0:96, :].rearrange("p (h c) -> p h c", c=CAD),
                                        (ca[:, b, :] if isinstance(b, int) else ca[:, bass.ds(b, 1), :].rearrange("p o c -> p (o c)"))
                                        .bitcast(f32).unsqueeze(1).to_broadcast([96, HEADS0, CAD]),
                                        head96[0:96, :].unsqueeze(2).to_broadcast([96, HEADS0, CAD]), ALU.mult).then_inc(cast_ready, 1)

            def build_v(layer, b):
                vc, mask, v, hg, to, tiles, d, ready, loaded, count = (
                    (v0c, vhead0, v0, HG0, TO0, TILES0, D0, v0_ready, v0c_in, N_V0),
                    (v1c, vhead1, v1, HG1, TO1, TILES1, D1, v1_ready, v1c_in, N_V1))[layer]
                wait(pool, loaded, b, count, count)
                for g in range(3):
                    a, n, h = to[g], tiles[g], hg[g]
                    last = nc.gpsimd.tensor_tensor(
                        v[:, a:a + n, 0:h * d].rearrange("p a (h d) -> p a h d", d=d),
                        vc[:, a:a + n, :].unsqueeze(2).to_broadcast([128, n, h, d]),
                        mask[:, a:a + n, 0:h].unsqueeze(3).to_broadcast([128, n, h, d]), ALU.mult)
                last.then_inc(ready, 1)

            def build_k(layer, b):
                hi, lo, mask, khi, klo, hg, rows, to, keys, ready = (
                    (kt0hi, kt0lo, head0, k0hi, k0lo, HG0, G0, TO0, KEYS0, k0_ready),
                    (kt1hi, kt1lo, head1, k1hi, k1lo, HG1, XG, TO1, KEYS1, k1_ready))[layer]
                for kt, dst in ((hi, khi), (lo, klo)):
                    for g in range(3):
                        r, h, o = rows[g], hg[g], 128 * to[g]
                        last = nc.gpsimd.tensor_tensor(
                            dst[0:r, o:o + h * keys].rearrange("p (h k) -> p h k", k=keys),
                            kt[0:r, g, b, :].bitcast(f32).unsqueeze(1).to_broadcast([r, h, keys]),
                            mask[0:r, 0:h].unsqueeze(2).to_broadcast([r, h, keys]), ALU.mult)
                last.then_inc(ready, 1)

            def split_x(b):
                wait(pool, xthi_ready, b, 1, 1)
                nc.gpsimd.tensor_tensor(xtlo[:, :, :], xt[:, :, :], xthi[:, :, :].bitcast(f32), ALU.subtract).then_inc(xtlo_ready, 1)

            split_x(0)
            pool.wait_ge(ca_split, 2)
            build_cast(0)
            setup_drained(pool, S_K0 + 5)
            build_k(0, 0)
            pool.wait_ge(vones_in, 16)
            build_v(0, 0)

            def body(b, do_a, do_b, do_c, more_a):
                if do_b:
                    if isinstance(b, int) and b == 1:
                        pool.wait_ge(vones_in, 32)
                        setup_drained(pool, S_K1 + 5)
                    else:
                        b_full(pool, b - 2, B_ST + T1 // 2 - 1)
                    build_k(1, b - 1)
                    if not isinstance(b, int) or b > 1:
                        b_full(pool, *values_job(b - 2, 2))
                    build_v(1, b - 1)
                if do_a and more_a:
                    a_full(pool, b, A_CT + 5)
                    build_cast(b + 1)
                    a_full(pool, b, A_ST + 2)
                    build_k(0, b + 1)
                    a_full(pool, b, A_U + 2)
                    build_v(0, b + 1)
                    split_x(b + 1)
                if do_b:
                    if do_c:
                        b_drained(pool, b - 1, B_O, B_O + 1)
                        wait(pool, out_stored, b - 2, 16, 16)
                    a_drained(pool, b - 1, A_O, A_O + 1, A_O + 2)
                    for g in range(3):
                        r = XG[g]
                        last = nc.gpsimd.tensor_tensor(x1res[0:r, g, :], x1[0:r, g, :],
                                                       bias1[0:r, g:g + 1].to_broadcast([r, SQ]), ALU.add)
                    last.then_inc(x1res_ready, 1)

            schedule(pool, body)


_OUT = (B, 112, 3, SQ)


def kernel(**inputs):
    import concourse.bacc as bacc
    from concourse.bass_utils import run_bass_kernel_spmd

    a = {k: np.asarray(v) for k, v in inputs.items()}
    x, ctx = a["x"], a["ctx_768"]
    wca = np.zeros((H, HEADS0, T), np.float32)
    wq0t = np.zeros((H, PAIRS, 2, 64), np.float32)
    for h in range(HEADS0):
        wca[h * D0:(h + 1) * D0, h, :] = a["L0_xattn_Wq_ca"].T[h * D0:(h + 1) * D0]
    wq0t[:, :, :, 0:D0] = a["L0_xattn_Wq"].T.reshape(H, PAIRS, 2, D0)
    wca = wca.reshape(H, HT)

    def groups(w, sizes, rows):
        out = np.zeros((rows, 3, w.shape[1]), np.float32)
        for g, o in enumerate(offsets(sizes)):
            out[0:sizes[g], g] = w[o:o + sizes[g]]
        return out

    wide = np.concatenate([a["L1_xattn_Wq"], a["L0_xattn_b_out"].reshape(H, 1), a["L1_xattn_bo"].reshape(H, 1)], axis=1)
    wsplit = np.concatenate([a["L0_xattn_Wq"], np.zeros((H, CA_ROW - G0[2]), np.float32), wca, a["L1_xattn_Wo"]], axis=1)
    xt = np.zeros((B, 3 * 112, SQ), np.float32)
    xt[:, 0:H] = x.transpose(0, 2, 1)
    arrays = {
        "xt": xt.reshape(B, 3, 112, SQ).transpose(0, 2, 1, 3), "x": x.reshape(B, QT, 128, H).transpose(0, 2, 1, 3).reshape(B, 128, QT * H),
        "enc": ctx.transpose(2, 0, 1).reshape(CAD, B * CTX),
        "ca": np.broadcast_to(ctx[:, KEYS0:, :].transpose(1, 0, 2), (3, HEADS0, T, B, CAD)).reshape(3 * HT, B * CAD),
        "wk0": a["L0_xattn_Wk"], "wv0": a["L0_xattn_Wv"], "wkca": a["L0_xattn_Wk_ca"], "wvca": a["L0_xattn_Wv_ca"],
        "wk1": a["L1_xattn_Wk"], "wv1": a["L1_xattn_Wv"],
        "wide": groups(wide, XG, 112), "wsplit": groups(wsplit, XG, 112).reshape(112, -1), "wo0": groups(a["L0_xattn_Wout"], G0, 128), "wq0t": groups(wq0t.reshape(H, PAIRS * 128), G0, 120),
        **constants(),
    }
    nc = bacc.Bacc("TRN2", target_bir_lowering=False, num_devices=1)
    f32 = mybir.dt.float32
    feed, t = {}, {}
    for name, v in arrays.items():
        feed["in_" + name] = np.ascontiguousarray(v)
        t[name] = nc.dram_tensor("in_" + name, v.shape, f32, kind="ExternalInput").ap()
    t["out"] = nc.dram_tensor("out_t", _OUT, f32, kind="ExternalOutput").ap()
    xattn_kernel(nc, t)
    r = run_bass_kernel_spmd(nc, [feed], core_ids=[0])
    out = np.asarray(r.results[0]["out_t"]).transpose(0, 3, 2, 1).reshape(B, SQ, 3 * 112)
    return np.ascontiguousarray(out[:, :, 0:H])
```
